# Optimizing a Trainium2 kernel written in Bass

```python
import numpy as np
import jax
import jax.numpy as jnp

def _softmax(x, axis=-1):
    return jax.nn.softmax(x, axis=axis)

def _gelu(x):
    return jax.nn.gelu(x, approximate=True)

def _silu(x):
    return jax.nn.silu(x)

def _sigmoid(x):
    return jax.nn.sigmoid(x)

def _layernorm(x, axis=-1, eps=1e-05):
    m = jnp.mean(x, axis=axis, keepdims=True)
    v = jnp.var(x, axis=axis, keepdims=True)
    return (x - m) / jnp.sqrt(v + eps)

def _scatter_add(tgt, idx, src, axis=0):
    return tgt.at[idx].add(src)

def _segment_sum(src, seg, n):
    return jax.ops.segment_sum(src, seg, n)
kernel_name = 'mk_gnn_resnorm_d2_gnn_r8_248d2e'

def setup_inputs(seed: int=0):
    np.random.seed(seed)
    _w = jnp.asarray

    def _rec_inputs():
        import jax
        import jax.numpy as jnp
        _gk = jax.random.key(seed)
        x = -0.0003713 + 1 * jax.random.normal(jax.random.fold_in(_gk, 1), (6250, 256), jnp.float32)
        src = jax.random.randint(jax.random.fold_in(_gk, 2), (200000,), 0, 6250, jnp.int32)
        dst = jax.random.randint(jax.random.fold_in(_gk, 3), (200000,), 0, 6250, jnp.int32)
        _o = jnp.argsort(dst, stable=True)
        src = src[_o]
        dst = dst[_o]
        edge_type_6 = jax.random.randint(jax.random.fold_in(_gk, 12), (200000,), 0, 6, jnp.int32)
        edge_type_64 = jax.random.randint(jax.random.fold_in(_gk, 13), (200000,), 0, 64, jnp.int32)
        return (x, src, dst, edge_type_6, edge_type_64)
    x, src, dst, edge_type_6, edge_type_64 = _rec_inputs()

    def _L0_gnn_setup():
        import jax, jax.numpy as jnp
        import numpy as np
        N_NODES = 6250
        N_EDGES = 62500
        IN_DIM = 256
        HID = 64
        HEADS = 4
        N_REL = 64
        key = jax.random.key(seed)
        ks = jax.random.split(key, 16)
        s = 0.02
        return {'node_features': jax.random.normal(ks[0], (N_NODES, IN_DIM), jnp.float32), 'edge_index': jax.random.randint(ks[1], (2, N_EDGES), 0, N_NODES, jnp.int32), 'edge_relations': jax.random.randint(ks[2], (N_EDGES,), 0, N_REL, jnp.int32), 'query_emb': jax.random.normal(ks[3], (IN_DIM,), jnp.float32), 'Wq': jax.random.normal(ks[4], (IN_DIM, HID * HEADS), jnp.float32) * s, 'bq': jnp.zeros((HID * HEADS,), jnp.float32), 'Wk': jax.random.normal(ks[5], (IN_DIM, HID * HEADS), jnp.float32) * s, 'bk': jnp.zeros((HID * HEADS,), jnp.float32), 'Wv': jax.random.normal(ks[6], (IN_DIM, HID * HEADS), jnp.float32) * s, 'bv': jnp.zeros((HID * HEADS,), jnp.float32), 'rel_w': jax.random.normal(ks[7], (N_REL, HID), jnp.float32) * s, 'Wo': jax.random.normal(ks[8], (HID * HEADS, IN_DIM), jnp.float32) * s, 'bo': jnp.zeros((IN_DIM,), jnp.float32), 'gamma': jnp.ones((IN_DIM,), jnp.float32), 'beta': jnp.zeros((IN_DIM,), jnp.float32)}
    _L0_gnn_all = _L0_gnn_setup()
    _L0_gnn_in = {k: v for k, v in _L0_gnn_all.items() if k in ('query_emb', 'Wq', 'bq', 'Wk', 'bk', 'Wv', 'bv', 'rel_w', 'Wo', 'bo', 'gamma', 'beta')}
    del _L0_gnn_all

    def _L1_gnn_setup():
        import jax, jax.numpy as jnp
        import numpy as np
        N_NODES = 6250
        N_EDGES = 50000
        D_IN = 256
        D_OUT = 256
        N_REL = 6
        N_HEADS = 4
        key = jax.random.key(seed)
        ks = jax.random.split(key, 12)
        s_in = 1.0 / np.sqrt(D_IN)
        s_out = 1.0 / np.sqrt(D_OUT)
        return {'x': jax.random.normal(ks[0], (N_NODES, D_IN), dtype=jnp.float32), 'edge_index': jax.random.randint(ks[1], (2, N_EDGES), 0, N_NODES, dtype=jnp.int64), 'edge_types': jax.random.randint(ks[2], (N_EDGES,), 0, N_REL, dtype=jnp.int64), 'W': jax.random.uniform(ks[3], (N_REL, D_IN, D_OUT), jnp.float32, -s_in, s_in), 'b': jax.random.uniform(ks[4], (N_REL, D_OUT), jnp.float32, -s_in, s_in), 'in_proj_w': jax.random.uniform(ks[5], (3 * D_OUT, D_OUT), jnp.float32, -s_out, s_out), 'in_proj_b': jnp.zeros((3 * D_OUT,), jnp.float32), 'attn_out_w': jax.random.uniform(ks[6], (D_OUT, D_OUT), jnp.float32, -s_out, s_out), 'attn_out_b': jnp.zeros((D_OUT,), jnp.float32), 'proj_w': jax.random.uniform(ks[7], (D_OUT, D_OUT), jnp.float32, -s_out, s_out), 'proj_b': jax.random.uniform(ks[8], (D_OUT,), jnp.float32, -s_out, s_out)}
    _L1_gnn_all = _L1_gnn_setup()
    _L1_gnn_in = {k: v for k, v in _L1_gnn_all.items() if k in ('W', 'b', 'in_proj_w', 'in_proj_b', 'attn_out_w', 'attn_out_b', 'proj_w', 'proj_b')}
    del _L1_gnn_all
    return {'x': x, 'src': src, 'dst': dst, 'edge_type_6': edge_type_6, 'edge_type_64': edge_type_64, 'L0_gnn_query_emb': _L0_gnn_in['query_emb'], 'L0_gnn_Wq': _L0_gnn_in['Wq'], 'L0_gnn_bq': _L0_gnn_in['bq'], 'L0_gnn_Wk': _L0_gnn_in['Wk'], 'L0_gnn_bk': _L0_gnn_in['bk'], 'L0_gnn_Wv': _L0_gnn_in['Wv'], 'L0_gnn_bv': _L0_gnn_in['bv'], 'L0_gnn_rel_w': _L0_gnn_in['rel_w'], 'L0_gnn_Wo': _L0_gnn_in['Wo'], 'L0_gnn_bo': _L0_gnn_in['bo'], 'L0_gnn_gamma': _L0_gnn_in['gamma'], 'L0_gnn_beta': _L0_gnn_in['beta'], 'L1_gnn_W': _L1_gnn_in['W'], 'L1_gnn_b': _L1_gnn_in['b'], 'L1_gnn_in_proj_w': _L1_gnn_in['in_proj_w'], 'L1_gnn_in_proj_b': _L1_gnn_in['in_proj_b'], 'L1_gnn_attn_out_w': _L1_gnn_in['attn_out_w'], 'L1_gnn_attn_out_b': _L1_gnn_in['attn_out_b'], 'L1_gnn_proj_w': _L1_gnn_in['proj_w'], 'L1_gnn_proj_b': _L1_gnn_in['proj_b']}

def reference(x, src, dst, edge_type_6, edge_type_64, L0_gnn_query_emb, L0_gnn_Wq, L0_gnn_bq, L0_gnn_Wk, L0_gnn_bk, L0_gnn_Wv, L0_gnn_bv, L0_gnn_rel_w, L0_gnn_Wo, L0_gnn_bo, L0_gnn_gamma, L0_gnn_beta, L1_gnn_W, L1_gnn_b, L1_gnn_in_proj_w, L1_gnn_in_proj_b, L1_gnn_attn_out_w, L1_gnn_attn_out_b, L1_gnn_proj_w, L1_gnn_proj_b):
    import jax
    import jax.numpy as jnp

    def _L0_gnn_ref(node_features, edge_index, edge_relations, query_emb, Wq, bq, Wk, bk, Wv, bv, rel_w, Wo, bo, gamma, beta):
        import jax, jax.numpy as jnp
        import numpy as np
        N_NODES = 6250
        N_EDGES = 62500
        IN_DIM = 256
        HID = 64
        HEADS = 4
        N_REL = 64
        N = node_features.shape[0]
        D = rel_w.shape[1]
        H = Wq.shape[1] // D
        enh = node_features + 0.1 * query_emb[None, :]
        Q = (enh @ Wq + bq).reshape(N, H, D)
        K = (enh @ Wk + bk).reshape(N, H, D)
        V = (enh @ Wv + bv).reshape(N, H, D)
        src, dst = (edge_index[0], edge_index[1])
        rel = rel_w[edge_relations]
        mod_k = K[src] + 0.2 * rel[:, None, :]
        scores = jnp.einsum('ehd,ehd->eh', Q[dst], mod_k) / D ** 0.5
        seg_max = jax.ops.segment_max(scores, dst, num_segments=N)
        ex = jnp.exp(scores - seg_max[dst])
        denom = jax.ops.segment_sum(ex, dst, num_segments=N)
        w = ex / denom[dst]
        agg = jax.ops.segment_sum(w[:, :, None] * V[src], dst, num_segments=N)
        deg = jax.ops.segment_sum(jnp.ones((src.shape[0],), jnp.float32), dst, num_segments=N)
        msgs = jnp.where(deg[:, None, None] > 0, agg, V)
        out = msgs.reshape(N, H * D) @ Wo + bo
        x = out + node_features
        mu = jnp.mean(x, axis=-1, keepdims=True)
        var = jnp.var(x, axis=-1, keepdims=True)
        return (x - mu) / jnp.sqrt(var + 1e-05) * gamma + beta

    def _L1_gnn_ref(x, edge_index, edge_types, W, b, in_proj_w, in_proj_b, attn_out_w, attn_out_b, proj_w, proj_b):
        import jax, jax.numpy as jnp
        import numpy as np
        N_NODES = 6250
        N_EDGES = 50000
        D_IN = 256
        D_OUT = 256
        N_REL = 6
        N_HEADS = 4
        num_nodes = x.shape[0]
        hd = D_OUT // N_HEADS
        transformed = jnp.einsum('ni,rio->rno', x, W) + b[:, None, :]
        src, dst = (edge_index[0], edge_index[1])
        msgs = transformed[edge_types, src]
        agg = jnp.zeros((N_REL, num_nodes, D_OUT), x.dtype).at[edge_types, dst].add(msgs)
        s = jnp.transpose(agg, (1, 0, 2))
        qkv = s @ in_proj_w.T + in_proj_b
        q, k, v = jnp.split(qkv, 3, axis=-1)
        q = q.reshape(num_nodes, N_REL, N_HEADS, hd)
        k = k.reshape(num_nodes, N_REL, N_HEADS, hd)
        v = v.reshape(num_nodes, N_REL, N_HEADS, hd)
        scores = jnp.einsum('nrhd,nshd->nhrs', q, k) / np.sqrt(hd)
        probs = jax.nn.softmax(scores, axis=-1)
        attn = jnp.einsum('nhrs,nshd->nrhd', probs, v).reshape(num_nodes, N_REL, D_OUT)
        attended = attn @ attn_out_w.T + attn_out_b
        aggregated_output = attended.mean(axis=1)
        out = (aggregated_output + x[:, :D_OUT]) @ proj_w.T + proj_b
        return out
    edge_index = jnp.stack([src, dst])
    x = _layernorm(x + _L0_gnn_ref(x, edge_index, edge_type_64, L0_gnn_query_emb, L0_gnn_Wq, L0_gnn_bq, L0_gnn_Wk, L0_gnn_bk, L0_gnn_Wv, L0_gnn_bv, L0_gnn_rel_w, L0_gnn_Wo, L0_gnn_bo, L0_gnn_gamma, L0_gnn_beta), axis=-1)
    x = _layernorm(x + _L1_gnn_ref(x, edge_index, edge_type_6, L1_gnn_W, L1_gnn_b, L1_gnn_in_proj_w, L1_gnn_in_proj_b, L1_gnn_attn_out_w, L1_gnn_attn_out_b, L1_gnn_proj_w, L1_gnn_proj_b), axis=-1)
    return x

_drawn_inputs = setup_inputs


def setup_inputs(seed=0):
    import zlib

    import numpy as np

    out = dict(_drawn_inputs(seed))
    spreads = {'L0_gnn_bq': (0.0, 0.8),
     'L0_gnn_bk': (0.0, 2.0),
     'L0_gnn_bv': (0.0, 0.487),
     'L0_gnn_bo': (0.0, 0.279),
     'L0_gnn_gamma': (1.0, 0.2),
     'L0_gnn_beta': (0.0, 0.1),
     'L1_gnn_in_proj_b': (0.0, 0.283),
     'L1_gnn_attn_out_b': (0.0, 0.1)}
    factors = {'L0_gnn_query_emb': 8.0,
     'L0_gnn_Wq': 8.0,
     'L0_gnn_Wk': 8.0,
     'L0_gnn_Wv': 5.354,
     'L0_gnn_rel_w': 37.832,
     'L0_gnn_Wo': 2.891,
     'L1_gnn_b': 3.132}
    for name, (base, spread) in spreads.items():
        noise = np.random.default_rng([zlib.crc32(name.encode()), seed]).standard_normal(out[name].shape)
        drawn = base * np.exp(spread * noise) if base else spread * noise
        out[name] = jnp.asarray(drawn.astype(out[name].dtype))
    for name, factor in factors.items():
        out[name] = (out[name] * factor).astype(out[name].dtype)
    return out
```

```python
from contextlib import ExitStack

import concourse.bass as bass
from concourse import mybir

ALU = mybir.AluOpType
ACT = mybir.ActivationFunctionType
AXX = mybir.AxisListType.X
F32 = mybir.dt.float32
BF16 = mybir.dt.bfloat16
I32 = mybir.dt.int32

P = 128
N = 6250
E = 200000
D = 256
H = 4
HD = D // H
R6 = 6
R64 = 64
EPAD = 392 * 512
HEADS = -(-E // 512)
FAR = 1 << 20
BIG = float(2 ** 100)
EPS = 1e-5

NB = -(-N // P)
C0 = 512
SUP = 4
K0 = -(-(E // C0 + NB + 1) // SUP) * SUP
NSUP = K0 // SUP
WN = 21
WR = WN * R6
SBW = 12
NSB = -(-N // (WN * SBW))
NW = NSB * SBW
C1 = 128
K1 = -(-(E // C1 + NW + 1) // 24) * 24
G0, G1 = -(-K0 // P), -(-(K1 + 8) // P)
GB0, GB1 = 1, -(-(NW + 1) // P)


class Scope:

    def __init__(self, nc, ctx, tag):
        self.nc, self.ctx, self.tag = nc, ctx, tag

    def sb(self, name, shape, dt=F32):
        return self.ctx.enter_context(self.nc.sbuf_tensor(f"{self.tag}_{name}", shape, dt))

    def ps(self, name, shape, dt=F32):
        return self.ctx.enter_context(self.nc.psum_tensor(f"{self.tag}_{name}", shape, dt))

    def sem(self, name):
        return self.ctx.enter_context(self.nc.semaphore(f"{self.tag}_{name}"))


class Count:

    def __init__(self, sem):
        self.sem, self.n = sem, 0

    def up(self, ins):
        self.n += 1
        ins.then_inc(self.sem, 1)
        return self.n


def past(i, n):
    return not isinstance(i, int) or i >= n


def tables_phase(nc, a, t):
    with ExitStack() as ctx:
        s = Scope(nc, ctx, "tab")
        src1 = s.sb("src1", [P, G1 * P], I32)
        row1 = s.sb("row1", [P, G1 * P])
        keep = s.sb("keep", [P, G1 * P])
        win = s.sb("win", [P, G1 * P], I32)
        last = s.sb("last", [P, G1 * P], I32)
        tables_out = s.sem("tables_out")
        pad_i = s.sb("pad_i", [2, EPAD - E], I32)
        heads_i = s.sb("heads_i", [1, HEADS], I32)
        heads_r = s.sb("heads_r", [1, HEADS])
        heads = s.sb("heads", [P, HEADS])
        junk = s.sb("junk", [P, 512])
        pcol_i = s.sb("pcol_i", [P, 1], I32)
        bounds = s.sb("bounds", [P, GB1])
        cnt = s.sb("cnt", [P, GB1])
        cnt2 = s.sb("cnt2", [P, GB1])
        crow_i = s.sb("crow_i", [P, GB1], I32)
        crow = s.sb("crow", [P, GB1])
        found_i = s.sb("found_i", [P, 512], I32)
        found = s.sb("found", [P, 512])
        start = s.sb("start", [P, GB1])
        diag = s.sb("diag", [P, P])
        srow = s.sb("srow", [P, GB1 * P])
        num_i = s.sb("num_i", [P, GB1 * P], I32)
        shr_i = s.sb("shr_i", [P, GB1 * P], I32)
        tiles = s.sb("tiles", [P, GB1 * P])
        zero = s.sb("zero", [P, GB1 * P])
        tend = s.sb("tend", [P, GB1 * P])
        tbeg = s.sb("tbeg", [P, GB1 * P])
        off = s.sb("off", [P, GB1 * P])
        doff = s.sb("doff", [P, GB1 * P])
        step = s.sb("step", [P, G1])
        rng = s.sb("rng", [P, G1])
        e0f = s.sb("e0f", [P, G1])
        e0i = s.sb("e0i", [P, G1], I32)
        rngneg = s.sb("rngneg", [P, G1])
        rows_i = s.sb("rows_i", [P, 2, 3, 512], I32)
        rows_f = s.sb("rows_f", [P, 3, 512])
        lastb = s.sb("lastb", [P, 514])
        rngrow = s.sb("rngrow", [P, G1 * P + 1])
        lastf = s.sb("lastf", [P, G1 * P])
        pb = s.ps("pb", [P, 512])
        pt = [s.ps(f"pt{i}", [P, 512]) for i in range(3)]

        pads_set = s.sem("pads_set")
        arrays_padded = s.sem("arrays_padded")
        heads_in = s.sem("heads_in")
        iota_done = s.sem("iota_done")
        dve = Count(s.sem("dve_done"))
        pe = Count(s.sem("pe_done"))
        gathered = s.sem("gathered")
        rows_in = [s.sem("rows_in0"), s.sem("rows_in1")]
        lastb_out = s.sem("lastb_out")

        names = ("src", "dst", "edge_type_6", "edge_type_64")
        plan = {}

        def layer_plan():
            for L in (0, 1):
                gk = (G0, G1)[L]
                yield L, (P, WN)[L], (GB0, GB1)[L], (NB, NW)[L], (C0, C1)[L], gk

        def plan_rows(L, g):
            before = -(-G0 // 2) if g % 2 == 0 else G0 // 2
            return g // 2 + 1 + (before if L else 0)

        with nc.Block() as block:
            @block.vector
            def _(eng):
                v = nc.vector

                def link(ins):
                    eng.wait_ge(dve.sem, dve.up(ins))
                    return dve.n

                link(v.memset(pad_i[:, :], 0))
                plan["pad0"] = link(v.memset(pad_i[0:1, :], FAR))
                eng.wait_ge(iota_done, 4)
                link(v.tensor_copy(t.col[:, :], pcol_i[:, :]))
                link(v.tensor_copy(t.iota[:, :], t.iota_i[:, :]))
                link(v.tensor_copy(t.iota_b[:, :], t.iota_i[:, 0:R64]))
                link(v.tensor_scalar(t.ident[:, :], t.iota[:, :], t.col[:, 0:1], None, ALU.is_equal))
                link(v.tensor_copy(t.ident_b[:, :], t.ident[:, :]))
                link(v.memset(t.ones[:, :], 1.0))
                link(v.memset(zero[:, :], 0.0))
                link(v.memset(rngrow[:, :], -1.0))
                eng.wait_ge(heads_in, 16)
                plan["heads_r"] = link(v.tensor_copy(heads_r[:, :], heads_i[:, :]))
                eng.wait_ge(pe.sem, 1)
                link(v.tensor_copy(heads[:, :], pb[:, 0:HEADS]))
                pe_n = 1
                ptn = 0
                gath = 0
                for L, stride, gb, nr, cs, gk in layer_plan():
                    for g in range(gb):
                        link(v.tensor_scalar(bounds[:, g:g + 1], t.col[:, 0:1], float(P * g), float(stride),
                                             ALU.add, ALU.mult))
                        link(v.tensor_scalar(junk[:, 0:HEADS], heads[:, :], bounds[:, g:g + 1], 0.0,
                                             ALU.is_lt, ALU.add, accum_out=cnt[:, g:g + 1]))
                        link(v.tensor_scalar(crow[:, g:g + 1], cnt[:, g:g + 1], -1.0, 0.0, ALU.add, ALU.max))
                        plan["crow", L, g] = link(v.tensor_copy(crow_i[:, g:g + 1], crow[:, g:g + 1]))
                        gath += 1
                        eng.wait_ge(gathered, 16 * gath)
                        link(v.tensor_copy(found[:, :], found_i[:, :]))
                        link(v.tensor_scalar(junk[:, :], found[:, :], bounds[:, g:g + 1], 0.0,
                                             ALU.is_lt, ALU.add, accum_out=cnt2[:, g:g + 1]))
                        link(v.scalar_tensor_tensor(start[:, g:g + 1], crow[:, g:g + 1], 512.0,
                                                    cnt2[:, g:g + 1], ALU.mult, ALU.add))
                        plan["diag", L, g] = link(v.tensor_scalar(diag[:, :], t.ident[:, :], start[:, g:g + 1],
                                                                  None, ALU.mult))
                        pe_n += 1
                        eng.wait_ge(pe.sem, pe_n)
                        link(v.tensor_copy(srow[:, P * g:P * g + P], pb[:, 0:P]))
                    link(v.tensor_tensor(tiles[:, 0:nr], srow[:, 1:nr + 1], srow[:, 0:nr], ALU.subtract))
                    link(v.tensor_scalar(num_i[:, 0:nr], tiles[:, 0:nr], float(cs - 1), None, ALU.add))
                    link(v.tensor_scalar(shr_i[:, 0:nr], num_i[:, 0:nr], cs.bit_length() - 1, None,
                                         ALU.logical_shift_right))
                    link(v.tensor_scalar(tiles[:, 0:nr], shr_i[:, 0:nr], 1.0, None, ALU.max))
                    link(v.tensor_tensor_scan(tend[:, 0:nr], tiles[:, 0:nr], zero[:, 0:nr], 0.0, ALU.add, ALU.max))
                    link(v.tensor_tensor(tbeg[:, 0:nr], tend[:, 0:nr], tiles[:, 0:nr], ALU.subtract))
                    link(v.scalar_tensor_tensor(off[:, 0:nr], tbeg[:, 0:nr], float(-cs), srow[:, 0:nr],
                                                ALU.mult, ALU.add))
                    link(v.tensor_tensor(doff[:, 0:nr - 1], off[:, 1:nr], off[:, 0:nr - 1], ALU.subtract))
                    for g in range(gk):
                        link(v.tensor_scalar(step[:, g:g + 1], t.col[:, 0:1], float(P * g), None, ALU.add))
                        link(v.tensor_scalar(junk[:, 0:nr - 1], tend[:, 0:nr - 1], step[:, g:g + 1], 0.0,
                                             ALU.is_le, ALU.add, accum_out=rng[:, g:g + 1]))
                        link(v.scalar_tensor_tensor(junk[:, 0:nr - 1], tend[:, 0:nr - 1], step[:, g:g + 1],
                                                    doff[:, 0:nr - 1], ALU.is_le, ALU.mult,
                                                    accum_out=e0f[:, g:g + 1]))
                    link(v.scalar_tensor_tensor(e0f[:, 0:gk], step[:, 0:gk], float(cs), e0f[:, 0:gk],
                                                ALU.mult, ALU.add))
                    link(v.tensor_scalar(e0f[:, 0:gk], e0f[:, 0:gk], float(E), None, ALU.min))
                    plan["e0", L] = link(v.tensor_copy(e0i[:, 0:gk], e0f[:, 0:gk]))
                    link(v.tensor_scalar(rngneg[:, 0:gk], rng[:, 0:gk], float(-stride), None, ALU.mult))
                    for g in range(gk):
                        plan["rdiag", L, g] = link(v.tensor_scalar(diag[:, :], t.ident[:, :], rng[:, g:g + 1],
                                                                   None, ALU.mult))
                        pe_n += 1
                        eng.wait_ge(pe.sem, pe_n)
                        link(v.tensor_copy(rngrow[:, P * g:P * g + P], pb[:, 0:P]))
                    if L == 0:
                        link(v.tensor_copy(t.blk[:, :], rngrow[:, 0:G0 * P]))
                    else:
                        link(v.tensor_copy(win[:, :], rngrow[:, 0:G1 * P]))
                        link(v.memset(keep[:, 0:1], 0.0))
                        link(v.tensor_tensor(keep[:, 1:G1 * P], rngrow[:, 1:G1 * P], rngrow[:, 0:G1 * P - 1],
                                             ALU.is_equal))
                        link(v.memset(rngrow[:, K1:K1 + 1], -1.0))
                        link(v.tensor_tensor(lastf[:, :], rngrow[:, 1:G1 * P + 1], rngrow[:, 0:G1 * P],
                                             ALU.not_equal))
                        link(v.tensor_copy(last[:, :], lastf[:, :]))
                    for g in range(gk):
                        ri = rows_i[:, g % 2, :, :]
                        eng.wait_ge(rows_in[g % 2], 48 * plan_rows(L, g))
                        link(v.tensor_copy(rows_f[:, :, 0:cs], ri[:, :, 0:cs]))
                        if L == 0:
                            if g:
                                eng.wait_ge(lastb_out, 64 * g)
                            link(v.memset(lastb[:, :], -BIG))
                            link(v.tensor_tensor(junk[:, 0:511], rows_f[:, 1, 0:511], rows_f[:, 1, 1:512],
                                                 ALU.not_equal))
                            plan["lastb", g] = link(v.tensor_scalar(lastb[:, 1:512], junk[:, 0:511], -BIG, None,
                                                                    ALU.mult))
                        link(v.tensor_scalar(rows_f[:, 1, 0:cs], rows_f[:, 1, 0:cs], rngneg[:, g:g + 1], None,
                                             ALU.add))
                        if L == 1:
                            link(v.scalar_tensor_tensor(rows_f[:, 1, 0:cs], rows_f[:, 1, 0:cs], float(R6),
                                                        rows_f[:, 2, 0:cs], ALU.mult, ALU.add))
                        plan["rows", L, g] = dve.n
                        pe_n += 1
                        eng.wait_ge(pe.sem, pe_n)
                        nj = cs // P
                        for dst, k in (((t.src0, 0), (t.node0, 1), (t.type0, 2)) if L == 0 else
                                       ((src1, 0), (row1, 1))):
                            o = dst[:, P * g * nj:P * (g + 1) * nj].rearrange("p (s j) -> p j s", j=nj)
                            link(v.tensor_copy(o, pt[k][:, 0:cs].rearrange("p (j s) -> p j s", j=nj)))
                        plan["copied", L, g] = dve.n

            @block.gpsimd
            def _(eng):
                eng.iota(pcol_i[:, :], [[0, 1]], base=0, channel_multiplier=1).then_inc(iota_done, 2)
                eng.iota(t.iota_i[:, :], [[1, P]], base=0, channel_multiplier=0).then_inc(iota_done, 2)
                eng.wait_ge(arrays_padded, 16 * 8)
                n = 0
                for L, stride, gb, nr, cs, gk in layer_plan():
                    for g in range(gb):
                        eng.wait_ge(dve.sem, plan["crow", L, g])
                        eng.indirect_dma_start(
                            out=found_i[:, :], out_offset=None,
                            in_=t.pads["dst"].rearrange("(r c) -> r c", c=512),
                            in_offset=bass.IndirectOffsetOnAxis(ap=crow_i[:, g:g + 1], axis=0),
                        ).then_inc(gathered, 16)
                    eng.wait_ge(dve.sem, plan["e0", L])
                    for g in range(gk):
                        if g >= 2:
                            eng.wait_ge(dve.sem, plan["copied", L, g - 2])
                        elif L:
                            eng.wait_ge(dve.sem, plan["copied", 0, G0 - 1])
                        for k, name in enumerate(("src", "dst", ("edge_type_64", "edge_type_6")[L])):
                            eng.indirect_dma_start(
                                out=rows_i[:, g % 2, k, 0:cs], out_offset=None,
                                in_=t.pads[name].rearrange("(r c) -> r c", c=1),
                                in_offset=bass.IndirectOffsetOnAxis(ap=e0i[:, g:g + 1], axis=0),
                            ).then_inc(rows_in[g % 2], 16)

            @block.tensor
            def _(eng):
                eng.wait_ge(dve.sem, plan["heads_r"])
                pe.up(eng.matmul(pb[:, 0:HEADS], t.ones[0:1, :], heads_r[:, :], start=True, stop=True))
                for L, stride, gb, nr, cs, gk in layer_plan():
                    for g in range(gb):
                        eng.wait_ge(dve.sem, plan["diag", L, g])
                        pe.up(eng.matmul(pb[:, 0:P], t.ones[:, :], diag[:, :], start=True, stop=True))
                    for g in range(gk):
                        eng.wait_ge(dve.sem, plan["rdiag", L, g])
                        pe.up(eng.matmul(pb[:, 0:P], t.ones[:, :], diag[:, :], start=True, stop=True))
                    for g in range(gk):
                        eng.wait_ge(dve.sem, plan["rows", L, g])
                        for k in range(3 if L == 0 else 2):
                            for j in range(cs // P):
                                mm = eng.transpose(pt[k][:, P * j:P * j + P], rows_f[:, k, P * j:P * j + P],
                                                     t.ident[:, :])
                        pe.up(mm)

            @block.sync
            def _(eng):
                for name in names:
                    eng.dma_start(t.pads[name][0:E].rearrange("(p f) -> p f", p=160),
                                  a[name].rearrange("(p f) -> p f", p=160)).then_inc(arrays_padded, 16)
                eng.dma_start(heads_i[:, :], a["dst"].rearrange("(o e) -> o e", o=1)[:, 0:E:512],
                              allow_slow_non_contiguous=True).then_inc(heads_in, 16)
                eng.wait_ge(dve.sem, plan["pad0"])
                for name in names:
                    k = 0 if name == "dst" else 1
                    eng.dma_start(t.pads[name][E:EPAD].rearrange("(o e) -> o e", o=1),
                                  pad_i[k:k + 1, :]).then_inc(arrays_padded, 16)
                for g in range(G0):
                    eng.wait_ge(dve.sem, plan["lastb", g])
                    for h in range(H):
                        eng.dma_start(t.lastb[P * g:P * g + P, h, :], lastb[:, :]).then_inc(lastb_out, 16)
                eng.wait_ge(lastb_out, 64 * G0)
                eng.wait_ge(dve.sem, plan["copied", 1, G1 - 1])
                for k, of in enumerate((src1, row1, keep, win, last)):
                    rows = P if k < 3 else 1
                    eng.dma_start(t.tables1[k][0:rows, :], of[0:rows, :]).then_inc(tables_out, 16)
                eng.wait_ge(tables_out, 16 * 5)


def project_phase(nc, a, t):
    with ExitStack() as ctx:
        s = Scope(nc, ctx, "pr")
        w = s.sb("w", [P, 2, 3 * D])
        brow = s.sb("brow", [P, 3 * D])
        bq8 = s.sb("bq8", [P, D])
        qcol = s.sb("qcol", [P, 2])
        qcol01 = s.sb("qcol01", [P, 2])
        relw = s.sb("relw", [R64, HD])
        rel = s.sb("rel", [R64, HD])
        rrest = s.sb("rrest", [R64, 2, HD])
        x = [s.sb(f"x{i}", [P, D]) for i in range(2)]
        enh = [s.sb(f"enh{i}", [P, 2, P]) for i in range(2)]
        kv = [s.sb(f"kv{i}", [P, 2 * D]) for i in range(2)]
        q = [s.sb(f"q{i}", [P, D]) for i in range(2)]
        rest = [s.sb(f"rest{i}", [P, 2, D]) for i in range(2)]
        q3 = [s.sb(f"q3{i}", [P, 3, D], BF16) for i in range(2)]
        p_t = [s.ps(f"pt{i}", [P, 512]) for i in range(2)]
        p_kv = [s.ps(f"pkv{i}", [P, 512]) for i in range(2)]
        p_q = [s.ps(f"pq{i}", [P, 512]) for i in range(2)]

        w_in = s.sem("w_in")
        x_zero = s.sem("x_zero")
        x_in = [s.sem(f"x_in{i}") for i in range(2)]
        x_turned = s.sem("x_turned")
        enh_done = s.sem("enh_done")
        kv_ps = s.sem("kv_ps")
        q_ps = s.sem("q_ps")
        kv_done = s.sem("kv_done")
        q_done = s.sem("q_done")
        part = s.sem("part")
        rest_done = s.sem("rest_done")
        out_kv = [s.sem(f"out_kv{i}") for i in range(2)]
        out_q3 = [s.sem(f"out_q3{i}") for i in range(2)]
        setup = s.sem("setup")

        def each(eng, body):
            body(0, 0, True, P)
            body(1, 1, True, P)
            with eng.Fori(1, NB // 2) as k:
                body(k * 2, 0, False, P)
                body(k * 2 + 1, 1, False, P)
            body(NB - 1, 0, False, N - (NB - 1) * P)

        assert NB % 2 == 1
        with nc.Block() as block:
            @block.sync
            def _(eng):
                for k in range(2):
                    for j, name in enumerate(("L0_gnn_Wk", "L0_gnn_Wv", "L0_gnn_Wq")):
                        eng.dma_start(w[:, k, D * j:D * j + D], a[name][P * k:P * k + P, :]).then_inc(w_in, 16)
                for j, name in enumerate(("L0_gnn_bk", "L0_gnn_bv", "L0_gnn_bq")):
                    eng.dma_start(brow[:, D * j:D * j + D], a[name].partition_broadcast(P)).then_inc(w_in, 16)
                eng.dma_start(qcol[:, :], a["L0_gnn_query_emb"].rearrange("(k p) -> p k", p=P),
                              allow_slow_non_contiguous=True).then_inc(w_in, 16)
                eng.dma_start(relw[:, :], a["L0_gnn_rel_w"]).then_inc(w_in, 16)

                def load(i, par, first, rows):
                    if rows < P:
                        eng.wait_ge(x_zero, 1)
                    elif not first:
                        eng.wait_ge(x_turned, i - 1)
                    eng.dma_start(x[par][0:rows, :], a["x"][bass.ds(i * P, rows), :]).then_inc(x_in[par], 16)
                each(eng, load)

            @block.tensor
            def _(eng):
                eng.wait_ge(w_in, 16 * 11)

                def tile(i, par, first, rows):
                    eng.wait_ge(x_in[par], (i - par) * 8 + 16)
                    if not first:
                        eng.wait_ge(enh_done, (i - 1) * 2)
                    for k in range(2):
                        mm = eng.transpose(p_t[par][:, P * k:P * k + P], x[par][:, P * k:P * k + P], t.ident[:, :])
                    mm.then_inc(x_turned, 1)
                    eng.wait_ge(enh_done, i * 2 + 2)
                    if not first:
                        eng.wait_ge(kv_done, i - 1)
                        eng.wait_ge(q_done, i - 1)
                    for k in range(2):
                        mm = eng.matmul(p_kv[par][:, :], enh[par][:, k, :], w[:, k, 0:2 * D],
                                        start=(k == 0), stop=(k == 1))
                    mm.then_inc(kv_ps, 1)
                    for k in range(2):
                        mm = eng.matmul(p_q[par][:, 0:D], enh[par][:, k, :], w[:, k, 2 * D:3 * D],
                                        start=(k == 0), stop=(k == 1))
                    mm.then_inc(q_ps, 1)
                each(eng, tile)

            @block.vector
            def _(eng):
                v = nc.vector
                eng.wait_ge(w_in, 16 * 11)
                v.tensor_scalar(qcol01[:, :], qcol[:, :], 0.1, None, ALU.mult).then_inc(setup, 1)
                v.tensor_scalar(bq8[:, :], brow[:, 2 * D:3 * D], 0.125, None, ALU.mult).then_inc(setup, 1)
                v.tensor_scalar(rel[:, :], relw[:, :], 0.2, None, ALU.mult).then_inc(setup, 1)
                eng.wait_ge(setup, 3)
                rest_of, n = rel[:, :], 3
                for j in range(3):
                    for h in range(H):
                        v.tensor_copy(t.rel3[:, j, HD * h:HD * h + HD], rest_of).then_inc(setup, 1)
                        n += 1
                    eng.wait_ge(setup, n)
                    if j < 2:
                        v.tensor_tensor(rrest[:, j, :], rest_of, t.rel3[:, j, 0:HD], ALU.subtract).then_inc(setup, 1)
                        n += 1
                        eng.wait_ge(setup, n)
                        rest_of = rrest[:, j, :]

                def tile(i, par, first, rows):
                    if rows < P:
                        eng.wait_ge(x_turned, i - 1)
                        v.memset(x[par][:, :], 0.0).then_inc(x_zero, 1)
                    eng.wait_ge(x_turned, i + 1)
                    if not first:
                        eng.wait_ge(q_ps, i - 1)
                    for k in range(2):
                        v.tensor_scalar(enh[par][:, k, :], p_t[par][:, P * k:P * k + P], qcol01[:, k:k + 1], None,
                                        ALU.add).then_inc(enh_done, 1)
                    eng.wait_ge(kv_ps, i + 1)
                    if not first:
                        eng.wait_ge(out_kv[par], (i - par) * 8)
                    v.tensor_tensor(kv[par][:, :], p_kv[par][:, :], brow[:, 0:2 * D], ALU.add).then_inc(kv_done, 1)
                    eng.wait_ge(q_ps, i + 1)
                    if not first:
                        eng.wait_ge(part, (i - 1) * 3)
                        eng.wait_ge(rest_done, (i - 1) * 2)
                    v.scalar_tensor_tensor(q[par][:, :], p_q[par][:, 0:D], 0.125, bq8[:, :], ALU.mult,
                                           ALU.add).then_inc(q_done, 1)
                each(eng, tile)

            @block.scalar
            def _(eng):

                def tile(i, par, first, rows):
                    for j in range(3):
                        if j == 0:
                            eng.wait_ge(q_done, i + 1)
                            if not first:
                                eng.wait_ge(out_q3[par], (i - par) * 8)
                            of = q[par][:, :]
                        else:
                            eng.wait_ge(rest_done, i * 2 + j)
                            of = rest[par][:, j - 1, :]
                        nc.scalar.activation(q3[par][:, j, :], of, ACT.Copy).then_inc(part, 1)
                    eng.wait_ge(part, i * 3 + 3)
                    eng.dma_start(t.q3[bass.ds(i * P, P), :], q3[par][:, :, :].rearrange("p a b -> p (a b)")
                                  ).then_inc(out_q3[par], 16)
                    eng.wait_ge(kv_done, i + 1)
                    eng.dma_start(t.kv[bass.ds(i * P, P), :], kv[par][:, :]).then_inc(out_kv[par], 16)
                each(eng, tile)
                for par in range(2):
                    eng.wait_ge(out_q3[par], 16 * ((NB + 1 - par) // 2))
                    eng.wait_ge(out_kv[par], 16 * ((NB + 1 - par) // 2))

            @block.gpsimd
            def _(eng):

                def tile(i, par, first, rows):
                    for j in range(2):
                        of = q[par][:, :] if j == 0 else rest[par][:, 0, :]
                        eng.wait_ge(part, i * 3 + j + 1)
                        nc.gpsimd.tensor_tensor(rest[par][:, j, :], of, q3[par][:, j, :],
                                                ALU.subtract).then_inc(rest_done, 1)
                each(eng, tile)


def attend_phase(nc, a, t):
    with ExitStack() as ctx:
        s = Scope(nc, ctx, "at")
        T = 4 * SUP
        M = SUP * H
        VW = H * (HD + 1)
        kv = [s.sb(f"kv{i}", [P, T, 2 * D]) for i in range(2)]
        idx = [s.sb(f"idx{i}", [P, T], I32) for i in range(2)]
        eh = [s.sb(f"eh{i}", [P, T, P]) for i in range(2)]
        et = [s.sb(f"et{i}", [P, T, R64], BF16) for i in range(2)]
        eh_t = [s.sb(f"eh_t{i}", [P, 512], BF16) for i in range(2)]
        et_t = [s.sb(f"et_t{i}", [R64, 512], BF16) for i in range(2)]
        q3 = [s.sb(f"q3{i}", [P, 3, D], BF16) for i in range(SUP)]
        kr = s.sb("kr", [P, 4, D])
        sc = [s.sb(f"sc{i}", [P, 4, SUP, H]) for i in range(2)]
        lastb = [s.sb(f"lastb{i}", [M, 514]) for i in range(2)]
        fmax = s.sb("fmax", [M, 512])
        smax = s.sb("smax", [M, 512])
        ex = s.sb("ex", [M, 512])
        lmax = s.sb("lmax", [M, 512])
        wgt = s.sb("wgt", [P, 2, 4, SUP, H])
        vs = [s.sb(f"vs{i}", [P, 4, VW + H]) for i in range(2)]
        absent = s.sb("absent", [P, H])
        cmax = s.sb("cmax", [P, H])
        nmax = s.sb("nmax", [P, H])
        dmax = [s.sb(f"dmax{i}", [P, 2, H]) for i in range(2)]
        fac = [s.sb(f"fac{i}", [P, 2, H]) for i in range(2)]
        add = [s.sb(f"add{i}", [P, VW]) for i in range(2)]
        p_eh = s.ps("p_eh", [P, 512])
        p_et = s.ps("p_et", [R64, 1024], BF16)
        p_q = [s.ps(f"p_q{i}", [P, 512]) for i in range(2)]
        p_r = [s.ps(f"p_r{i}", [P, 512]) for i in range(2)]
        p_x = s.ps("p_x", [P, 512])
        p_s = s.ps("p_s", [P, 512])

        kv_in = [[s.sem(f"kv_in{i}{c}") for c in range(SUP)] for i in range(2)]
        idx_set = s.sem("idx_set")
        pool_on = s.sem("pool_on")
        pe_on = s.sem("pe_on")
        dve_on = s.sem("dve_on")
        q3_in = [s.sem(f"q3_in{c}") for c in range(SUP)]
        lastb_in = [s.sem(f"lastb_in{i}") for i in range(2)]
        cleared = s.sem("cleared")
        hot = s.sem("hot")
        turned = s.sem("turned")
        hot_t = s.sem("hot_t")
        r_ps = s.sem("r_ps")
        q_ps = s.sem("q_ps")
        kr_sum = s.sem("kr_sum")
        kr_prod = s.sem("kr_prod")
        scored = s.sem("scored")
        sc_turned = s.sem("sc_turned")
        fwd = s.sem("fwd")
        bwd = s.sem("bwd")
        over = s.sem("over")
        lmax_done = s.sem("lmax_done")
        ex_done = s.sem("ex_done")
        w_turned = s.sem("w_turned")
        wgt_done = s.sem("wgt_done")
        vs_w = s.sem("vs_w")
        vs_v = s.sem("vs_v")
        summed = s.sem("summed")
        marked = s.sem("marked")
        cmax_done = s.sem("cmax_done")
        nmax_done = s.sem("nmax_done")
        dmax_done = s.sem("dmax_done")
        max_kept = s.sem("max_kept")
        fac_done = s.sem("fac_done")
        add_done = s.sem("add_done")
        merged = s.sem("merged")

        def run(eng, iteration):
            iteration(0, 0, True, False, True, True)
            iteration(1, 1, True, True, False, True)
            with eng.Fori(1, NSUP // 2) as k:
                iteration(k * 2, 0, True, True, False, False)
                iteration(k * 2 + 1, 1, True, True, False, False)
            iteration(NSUP, 0, False, True, False, False)

        assert NSUP % 2 == 0

        with nc.Block() as block:
            @block.gpsimd
            def _(eng):
                def gather(n, par, first):
                    if not first:
                        eng.wait_ge(kv_in[par][SUP - 1], (n - par) * 32)
                    nc.gpsimd.tensor_copy(idx[par][:, :], t.src0[:, bass.ds(n * T, T)]).then_inc(idx_set, 1)
                    eng.wait_ge(idx_set, n + 1)
                    eng.sem_inc(pool_on, 1)
                    for c in range(SUP):
                        if not first:
                            eng.wait_ge(vs_v, (n - 2) * SUP + c + 1)
                            eng.sem_inc(pool_on, 1)
                        for j in range(4):
                            eng.indirect_dma_start(
                                out=kv[par][:, 4 * c + j, :], out_offset=None, in_=t.kv,
                                in_offset=bass.IndirectOffsetOnAxis(ap=idx[par][:, 4 * c + j:4 * c + j + 1], axis=0),
                            ).then_inc(kv_in[par][c], 16)

                gather(0, 0, True)
                gather(1, 1, True)
                with eng.Fori(1, NSUP // 2) as k:
                    gather(k * 2, 0, False)
                    gather(k * 2 + 1, 1, False)

            @block.sync
            def _(eng):
                def load(n, par, first, head=False):
                    if not first:
                        eng.wait_ge(lmax_done, n - 1)
                    eng.dma_start(lastb[par][:, :], t.lastb[bass.ds(n * SUP, SUP), :, :].rearrange("c h e -> (c h) e")
                                  ).then_inc(lastb_in[par], 16)
                    for c in range(SUP):
                        if not head:
                            eng.wait_ge(q_ps, (n * SUP - SUP + c + 1) * 2)
                        b = eng.value_load(t.blk[0:1, bass.ds(n * SUP + c, 1)], min_val=0, max_val=NB - 1)
                        eng.dma_start(q3[c][:, :, :].rearrange("p a b -> p (a b)"), t.q3[bass.ds(b * P, P), :]
                                      ).then_inc(q3_in[c], 16)

                load(0, 0, True, head=True)
                load(1, 1, True)
                with eng.Fori(1, NSUP // 2) as k:
                    load(k * 2, 0, False)
                    load(k * 2 + 1, 1, False)

            @block.tensor
            def _(eng):
                def turn(n, par, c, first):
                    if c == 0:
                        eng.wait_ge(hot, n * 2 + 2)
                    if not (first and c == 0):
                        eng.wait_ge(hot_t, (n * SUP + c) * 2)
                    for j in range(4):
                        eng.transpose(p_eh[:, P * j:P * j + P], eh[par][:, 4 * c + j, :], t.ident[:, :])
                    for j in range(4):
                        mm = eng.transpose(p_et[:, P * j:P * j + P], et[par][:, 4 * c + j, :], t.ident_b[:, :])
                    mm.then_inc(turned, 1)

                def expand(n, par, c, first):
                    eng.wait_ge(hot_t, (n * SUP + c) * 2 + 2)
                    for half in range(2):
                        if not (first and c == 0):
                            eng.wait_ge(kr_sum, (n * SUP + c) * 2 + half - 1)
                        for j in range(2):
                            for m in range(3):
                                k = 2 * half + j
                                mm = eng.matmul(p_r[half][:, D * j:D * j + D], et_t[c % 2][:, P * k:P * k + P],
                                                t.rel3[:, m, :], start=(m == 0), stop=(m == 2))
                        mm.then_inc(r_ps, 1)
                        if half == 0:
                            eng.wait_ge(q3_in[c], n * 16 + 16)
                        if not (first and c == 0):
                            eng.wait_ge(kr_prod, (n * SUP + c) * 2 + half - 1)
                        for j in range(2):
                            for m in range(3):
                                k = 2 * half + j
                                mm = eng.matmul(p_q[half][:, D * j:D * j + D], eh_t[c % 2][:, P * k:P * k + P],
                                                q3[c][:, m, :], start=(m == 0), stop=(m == 2))
                        mm.then_inc(q_ps, 1)

                def turn_scores(u, par, first):
                    eng.wait_ge(scored, u * SUP + SUP)
                    if not first:
                        eng.wait_ge(wgt_done, u)
                    for j in range(4):
                        mm = eng.transpose(p_x[0:M, P * j:P * j + P],
                                           sc[par][:, j, :, :].rearrange("p c h -> p (c h)"), t.ident[:, :])
                    mm.then_inc(sc_turned, 1)

                def turn_weights(u):
                    eng.wait_ge(ex_done, u + 1)
                    eng.wait_ge(lmax_done, u + 1)
                    eng.sem_inc(pe_on, 1)
                    for k, of in enumerate((ex, lmax)):
                        for j in range(4):
                            o = (4 * k + j) * M
                            mm = eng.transpose(p_x[:, o:o + M], of[:, P * j:P * j + P], t.ident[0:M, 0:M])
                    mm.then_inc(w_turned, 1)

                def sum_up(u, par, c, first):
                    eng.wait_ge(vs_v, u * SUP + c + 1)
                    eng.wait_ge(vs_w, (u * SUP + c) * 2 + 2)
                    if not (first and c == 0):
                        eng.wait_ge(add_done, u * SUP + c)
                        eng.wait_ge(cmax_done, u * SUP + c)
                    for j in range(4):
                        mm = eng.matmul(p_s[:, 0:VW + H], eh[par][:, 4 * c + j, :], vs[c % 2][:, j, :],
                                        start=(j == 0), stop=(j == 3))
                    mm.then_inc(summed, 1)

                def iteration(n, par, scores, sums, first, first_sum):
                    u = n - 1
                    if scores:
                        turn(n, par, 0, first)
                    if sums:
                        turn_scores(u, 1 - par, first_sum)
                    if scores:
                        expand(n, par, 0, first)
                        turn(n, par, 1, first)
                    if sums:
                        turn_weights(u)
                    for c in range(SUP):
                        if scores and c + 1 < SUP:
                            expand(n, par, c + 1, first)
                            if c + 2 < SUP:
                                turn(n, par, c + 2, first)
                        if sums:
                            sum_up(u, 1 - par, c, first_sum)

                run(eng, iteration)

            @block.scalar
            def _(eng):
                act = nc.scalar.activation

                def copy_hot(n, c, first):
                    eng.wait_ge(turned, n * SUP + c + 1)
                    if not (first and c < 2):
                        eng.wait_ge(q_ps, (n * SUP + c - 1) * 2)
                    act(eh_t[c % 2][:, :], p_eh[:, :], ACT.Copy).then_inc(hot_t, 1)
                    act(et_t[c % 2][:, :], p_et[:, 0:512], ACT.Copy).then_inc(hot_t, 1)

                def expo(u):
                    eng.wait_ge(over, u + 1)
                    act(ex[:, :], ex[:, :], ACT.Exp).then_inc(ex_done, 1)

                def scale_v(u, par, c, first):
                    if c == 0:
                        eng.wait_ge(wgt_done, u + 1)
                    if not (first and c < 2):
                        eng.wait_ge(summed, u * SUP + c - 1)
                    for j in range(4):
                        for h in range(H):
                            i = act(vs[c % 2][:, j, 65 * h:65 * h + HD], kv[par][:, 4 * c + j, D + HD * h:D + HD * h + HD],
                                    ACT.Copy, scale=wgt[:, 0, j, c, h:h + 1])
                    i.then_inc(vs_v, 1)

                def rescale(u, c, first):
                    b = c % 2
                    eng.wait_ge(dmax_done, (u * SUP + c) * 2 + 2)
                    if not (first and c < 2):
                        eng.wait_ge(merged, (u * SUP + c - 1) * H)
                    act(fac[b][:, :, :], dmax[b][:, :, :], ACT.Exp).then_inc(fac_done, 1)
                    eng.wait_ge(fac_done, u * SUP + c + 1)
                    for h in range(H):
                        i = act(add[b][:, 65 * h:65 * h + 65], p_s[:, 65 * h:65 * h + 65], ACT.Copy,
                                scale=fac[b][:, 1, h:h + 1])
                    i.then_inc(add_done, 1)

                def iteration(n, par, scores, sums, first, first_sum):
                    u = n - 1
                    if scores:
                        copy_hot(n, 0, first)
                        copy_hot(n, 1, first)
                    if sums:
                        expo(u)
                        scale_v(u, 1 - par, 0, first_sum)
                    for c in range(SUP):
                        if scores and c + 2 < SUP:
                            copy_hot(n, c + 2, first)
                        if sums:
                            if c + 1 < SUP:
                                scale_v(u, 1 - par, c + 1, first_sum)
                            rescale(u, c, first_sum)

                run(eng, iteration)

            @block.vector
            def _(eng):
                v = nc.vector

                def one_hots(n, par, first):
                    if not first:
                        eng.wait_ge(summed, (n - 1) * SUP)
                    v.tensor_tensor(eh[par][:, :, :], t.iota[:, :].unsqueeze(1).to_broadcast([P, T, P]),
                                    t.node0[:, bass.ds(n * T, T)].unsqueeze(2).to_broadcast([P, T, P]),
                                    ALU.is_equal).then_inc(hot, 1)
                    v.tensor_tensor(et[par][:, :, :], t.iota_b[:, :].unsqueeze(1).to_broadcast([P, T, R64]),
                                    t.type0[:, bass.ds(n * T, T)].unsqueeze(2).to_broadcast([P, T, R64]),
                                    ALU.is_equal).then_inc(hot, 1)

                def score(n, par, c, half, first):
                    if half == 0:
                        eng.wait_ge(kv_in[par][c], (n - par) * 32 + 64)
                        if not (first and c == 0):
                            eng.wait_ge(scored, n * SUP + c)
                    i = (n * SUP + c) * 2 + half
                    o = kr[:, 2 * half:2 * half + 2, :]
                    eng.wait_ge(r_ps, i + 1)
                    v.tensor_tensor(o, kv[par][:, 4 * c + 2 * half:4 * c + 2 * half + 2, 0:D],
                                    p_r[half][:, :].rearrange("p (j d) -> p j d", j=2), ALU.add).then_inc(kr_sum, 1)
                    eng.wait_ge(kr_sum, i + 1)
                    eng.wait_ge(q_ps, i + 1)
                    v.tensor_tensor(o, o, p_q[half][:, :].rearrange("p (j d) -> p j d", j=2),
                                    ALU.mult).then_inc(kr_prod, 1)
                    if half == 1:
                        eng.wait_ge(kr_prod, i + 1)
                        if not first:
                            eng.wait_ge(sc_turned, n - 1)
                        v.tensor_reduce(sc[par][:, :, c, :], kr[:, :, :].rearrange("p j (h d) -> p j h d", h=H),
                                        AXX, ALU.add).then_inc(scored, 1)

                def maxima(u, par, first):
                    eng.wait_ge(lastb_in[par], (u - par) * 8 + 16)
                    eng.wait_ge(sc_turned, u + 1)
                    v.tensor_tensor_scan(fmax[:, :], lastb[par][:, 0:512], p_x[0:M, :], -BIG, ALU.add,
                                         ALU.max).then_inc(fwd, 1)
                    eng.wait_ge(fwd, u + 1)
                    if not first:
                        eng.wait_ge(w_turned, u)
                    v.tensor_tensor_scan(smax[:, ::-1], lastb[par][:, 1:513][:, ::-1], fmax[:, ::-1], -BIG,
                                         ALU.add, ALU.max).then_inc(bwd, 1)
                    eng.wait_ge(bwd, u + 1)
                    v.tensor_tensor(ex[:, :], p_x[0:M, :], smax[:, :], ALU.subtract).then_inc(over, 1)
                    v.scalar_tensor_tensor(lmax[:, :], lastb[par][:, 1:513], -1.0 / BIG, smax[:, :], ALU.mult,
                                           ALU.mult).then_inc(lmax_done, 1)

                def weights(u, first):
                    eng.wait_ge(w_turned, u + 1)
                    if not first:
                        eng.wait_ge(vs_v, u * SUP)
                    v.tensor_copy(wgt[:, :, :, :, :].rearrange("p k j c h -> p (k j c h)"),
                                  p_x[:, 0:8 * M]).then_inc(wgt_done, 1)

                def place(u, c, first):
                    if c == 0:
                        eng.wait_ge(wgt_done, u + 1)
                    if not (first and c < 2):
                        eng.wait_ge(summed, u * SUP + c - 1)
                    o = vs[c % 2]
                    v.tensor_copy(o[:, :, 0:VW].rearrange("p j (h e) -> p j h e", h=H)[:, :, :, HD],
                                  wgt[:, 0, :, c, :]).then_inc(vs_w, 1)
                    v.tensor_copy(o[:, :, VW:VW + H], wgt[:, 1, :, c, :]).then_inc(vs_w, 1)

                def new_max(u, c, first):
                    i = u * SUP + c
                    eng.wait_ge(summed, i + 1)
                    den = p_s[:, 0:VW].rearrange("p (h e) -> p h e", h=H)[:, :, HD]
                    v.tensor_scalar(absent[:, :], den, 0.5, -BIG, ALU.is_lt, ALU.mult).then_inc(marked, 1)
                    eng.wait_ge(marked, i + 1)
                    v.tensor_tensor(cmax[:, :], absent[:, :], p_s[:, VW:VW + H], ALU.add).then_inc(cmax_done, 1)
                    b = eng.value_load(t.blk[0:1, bass.ds(i, 1)], min_val=0, max_val=NB - 1)
                    old = t.max0[:, bass.ds(b * H, H)]
                    eng.wait_ge(cmax_done, i + 1)
                    if not (first and c == 0):
                        eng.wait_ge(max_kept, i)
                    v.tensor_tensor(nmax[:, :], old, cmax[:, :], ALU.max).then_inc(nmax_done, 1)
                    eng.wait_ge(nmax_done, i + 1)
                    if not (first and c < 2):
                        eng.wait_ge(fac_done, i - 1)
                    v.tensor_tensor(dmax[c % 2][:, 0, :], old, nmax[:, :], ALU.subtract).then_inc(dmax_done, 1)
                    v.tensor_tensor(dmax[c % 2][:, 1, :], cmax[:, :], nmax[:, :], ALU.subtract).then_inc(dmax_done, 1)
                    eng.wait_ge(dmax_done, i * 2 + 1)
                    eng.sem_inc(dve_on, 1)
                    v.tensor_copy(old, nmax[:, :]).then_inc(max_kept, 1)
                    return b

                def merge(u, c, b, first):
                    i = u * SUP + c
                    if not (first and c == 0):
                        eng.wait_ge(merged, i * H)
                    eng.wait_ge(add_done, i + 1)
                    eng.wait_ge(max_kept, i + 1)
                    for h in range(H):
                        o = t.sum0[:, bass.ds(b * VW + 65 * h, 65)]
                        v.scalar_tensor_tensor(o, o, fac[c % 2][:, 0, h:h + 1], add[c % 2][:, 65 * h:65 * h + 65],
                                               ALU.mult, ALU.add).then_inc(merged, 1)

                def iteration(n, par, scores, sums, first, first_sum):
                    u = n - 1
                    if scores:
                        one_hots(n, par, first)
                    if sums:
                        maxima(u, 1 - par, first_sum)
                    if scores:
                        score(n, par, 0, 0, first)
                    if sums:
                        weights(u, first_sum)
                        place(u, 0, first_sum)
                        place(u, 1, first_sum)
                    if scores:
                        score(n, par, 0, 1, first)
                    b = {}
                    for c in range(1, SUP + 1):
                        if scores and c < SUP:
                            score(n, par, c, 0, first)
                        if sums:
                            b[c - 1] = new_max(u, c - 1, first_sum)
                            if c + 1 < SUP:
                                place(u, c + 1, first_sum)
                        if scores and c < SUP:
                            score(n, par, c, 1, first)
                        if sums:
                            merge(u, c - 1, b[c - 1], first_sum)

                v.memset(t.sum0[:, :], 0.0).then_inc(cleared, 1)
                v.memset(t.max0[:, :], -BIG).then_inc(cleared, 1)
                eng.wait_ge(cleared, 2)
                run(eng, iteration)


def update_phase(nc, a, t):
    with ExitStack() as ctx:
        s = Scope(nc, ctx, "up")
        wo = s.sb("wo", [P, 2, D])
        gamma, beta, bo = (s.sb(n, [P, D]) for n in ("gamma", "beta", "bo"))
        eps = s.sb("eps", [P, 1])
        zero = s.sb("zero", [P, D])
        x = [s.sb(f"x{i}", [P, D]) for i in range(2)]
        vown = [s.sb(f"vown{i}", [P, D]) for i in range(2)]
        xb = [s.sb(f"xb{i}", [P, D]) for i in range(2)]
        none = s.sb("none", [P, H])
        den = s.sb("den", [P, H])
        rden = s.sb("rden", [P, H])
        own = s.sb("own", [P, D])
        mean = s.sb("mean", [P, D])
        msg = s.sb("msg", [P, D])
        msg_t = [s.sb(f"msg_t{i}", [P, 2, P]) for i in range(2)]
        z = s.sb("z", [P, D])
        stats = s.sb("stats", [P, 2, 6])
        mv = s.sb("mv", [P, 2, 2])
        dev = s.sb("dev", [P, 2])
        rdev = s.sb("rdev", [P, 2])
        y = s.sb("y", [P, D])
        yg = s.sb("yg", [P, D])
        yb = s.sb("yb", [P, D])
        z2 = s.sb("z2", [P, D])
        x1 = [s.sb(f"x1{i}", [P, D]) for i in range(2)]
        p_t = [s.ps(f"pt{i}", [P, 512]) for i in range(2)]
        p_o = [s.ps(f"po{i}", [P, 512]) for i in range(2)]

        w_in = s.sem("w_in")
        x_zero = s.sem("x_zero")
        x_in = [s.sem(f"x_in{i}") for i in range(2)]
        xb_done = s.sem("xb_done")
        step = s.sem("step")
        turned = s.sem("turned")
        msg_t_done = s.sem("msg_t_done")
        out_ps = s.sem("out_ps")
        dev_done = s.sem("dev_done")
        dve_on = s.sem("dve_on")
        x1_out = [s.sem(f"x1_out{i}") for i in range(2)]
        pad_out = s.sem("pad_out")
        STEPS = 21
        MSG, Z, VAR1, VAR2, X1 = 7, 8, 10, 18, 20

        def each(eng, body):
            body(0, 0, True, P)
            body(1, 1, True, P)
            with eng.Fori(1, NB // 2) as k:
                body(k * 2, 0, False, P)
                body(k * 2 + 1, 1, False, P)
            body(NB - 1, 0, False, N - (NB - 1) * P)

        with nc.Block() as block:
            @block.sync
            def _(eng):
                eng.dma_start(wo[:, :, :], a["L0_gnn_Wo"].rearrange("(k p) n -> p k n", p=P)).then_inc(w_in, 16)
                for dst, name in ((gamma, "gamma"), (beta, "beta"), (bo, "bo")):
                    eng.dma_start(dst[:, :], a[f"L0_gnn_{name}"].partition_broadcast(P)).then_inc(w_in, 16)

                def load(i, par, first, rows):
                    if rows < P:
                        eng.wait_ge(x_zero, 3)
                    elif not first:
                        eng.wait_ge(step, (i - 1) * STEPS)
                        eng.wait_ge(xb_done, i - 1)
                    eng.dma_start(x[par][0:rows, :], a["x"][bass.ds(i * P, rows), :]).then_inc(x_in[par], 16)
                    eng.dma_start(vown[par][:, :], t.kv[bass.ds(i * P, P), D:2 * D]).then_inc(x_in[par], 16)
                each(eng, load)

            @block.gpsimd
            def _(eng):
                eng.wait_ge(w_in, 64)

                def tile(i, par, first, rows):
                    eng.wait_ge(x_in[par], (i - par) * 16 + 32)
                    if not first:
                        eng.wait_ge(step, (i - 2) * STEPS + Z)
                    nc.gpsimd.tensor_tensor(xb[par][:, :], x[par][:, :], bo[:, :], ALU.add).then_inc(xb_done, 1)
                each(eng, tile)

            @block.tensor
            def _(eng):
                def tile(i, par, first, rows):
                    eng.wait_ge(step, i * STEPS + MSG)
                    if not first:
                        eng.wait_ge(msg_t_done, (i - 1) * 2)
                    for k in range(2):
                        mm = eng.transpose(p_t[par][:, P * k:P * k + P], msg[:, P * k:P * k + P], t.ident[:, :])
                    mm.then_inc(turned, 1)
                    eng.wait_ge(msg_t_done, i * 2 + 2)
                    if not first:
                        eng.wait_ge(step, (i - 2) * STEPS + Z)
                    for k in range(2):
                        mm = eng.matmul(p_o[par][:, 0:D], msg_t[par][:, k, :], wo[:, k, :],
                                        start=(k == 0), stop=(k == 1))
                    mm.then_inc(out_ps, 1)
                eng.wait_ge(w_in, 64)
                each(eng, tile)

            @block.scalar
            def _(eng):
                act = nc.scalar.activation

                def tile(i, par, first, rows):
                    eng.wait_ge(turned, i + 1)
                    if not first:
                        eng.wait_ge(out_ps, i - 1)
                    for k in range(2):
                        act(msg_t[par][:, k, :], p_t[par][:, P * k:P * k + P], ACT.Copy).then_inc(msg_t_done, 1)
                    for m, var in enumerate((VAR1, VAR2)):
                        eng.wait_ge(step, i * STEPS + var)
                        act(dev[:, m:m + 1], mv[:, m, 1:2], ACT.Sqrt, bias=eps[:, 0:1]).then_inc(dev_done, 1)
                    eng.wait_ge(step, i * STEPS + X1 + 1)
                    eng.dma_start(t.x1[bass.ds(i * P, P), :], x1[par][:, :]).then_inc(x1_out[par], 16)
                eng.wait_ge(x_zero, 2)
                each(eng, tile)
                eng.dma_start(t.x1[NB * P:NW * WN, :], zero[0:NW * WN - NB * P, :]).then_inc(pad_out, 16)
                for par in range(2):
                    eng.wait_ge(x1_out[par], 16 * ((NB + 1 - par) // 2))
                eng.wait_ge(pad_out, 16)

            @block.vector
            def _(eng):
                v = nc.vector

                def tile(i, par, first, rows):
                    n = [0]

                    def link(ins):
                        n[0] += 1
                        ins.then_inc(step, 1)
                        eng.wait_ge(step, i * STEPS + n[0])

                    if rows < P:
                        eng.wait_ge(xb_done, i - 1)
                        v.memset(x[par][:, :], 0.0).then_inc(x_zero, 1)
                    eng.wait_ge(x_in[par], (i - par) * 16 + 32)
                    if not first:
                        eng.wait_ge(turned, i)
                    sums = t.sum0[:, bass.ds(i * (H * (HD + 1)), H * (HD + 1))].rearrange("p (h e) -> p h e", h=H)
                    link(v.tensor_scalar(none[:, :], sums[:, :, HD], 0.5, None, ALU.is_lt))
                    link(v.tensor_tensor(den[:, :], sums[:, :, HD], none[:, :], ALU.add))
                    link(v.reciprocal(rden[:, :], den[:, :]))
                    link(v.tensor_tensor(mean[:, :].rearrange("p (h d) -> p h d", h=H), sums[:, :, 0:HD],
                                         rden[:, :].unsqueeze(2).to_broadcast([P, H, HD]), ALU.mult))
                    link(v.tensor_scalar(own[:, :], vown[par][:, :], none[:, 0:1], None, ALU.mult))
                    link(v.tensor_copy(rdev[:, 0:1], none[:, 0:1]))
                    link(v.tensor_tensor(msg[:, :], mean[:, :], own[:, :], ALU.add))
                    assert n[0] == MSG
                    eng.wait_ge(out_ps, i + 1)
                    eng.wait_ge(xb_done, i + 1)
                    link(v.tensor_tensor(z[:, :], p_o[par][:, 0:D], xb[par][:, :], ALU.add))
                    link(v.bn_stats(stats[:, 0, :], z[:, :]))
                    eng.sem_inc(dve_on, 1)
                    link(v.bn_aggr(mv[:, 0, :], stats[:, 0, :]))
                    assert n[0] == VAR1
                    eng.wait_ge(dev_done, i * 2 + 1)
                    link(v.reciprocal(rdev[:, 0:1], dev[:, 0:1]))
                    link(v.tensor_scalar(y[:, :], z[:, :], mv[:, 0, 0:1], rdev[:, 0:1], ALU.subtract, ALU.mult))
                    link(v.tensor_tensor(yg[:, :], y[:, :], gamma[:, :], ALU.mult))
                    link(v.tensor_tensor(yb[:, :], yg[:, :], beta[:, :], ALU.add))
                    link(v.tensor_tensor(z2[:, :], yb[:, :], x[par][:, :], ALU.add))
                    link(v.bn_stats(stats[:, 1, :], z2[:, :]))
                    link(v.tensor_copy(rdev[:, 1:2], rdev[:, 0:1]))
                    eng.sem_inc(dve_on, 1)
                    link(v.bn_aggr(mv[:, 1, :], stats[:, 1, :]))
                    assert n[0] == VAR2
                    eng.wait_ge(dev_done, i * 2 + 2)
                    link(v.reciprocal(rdev[:, 1:2], dev[:, 1:2]))
                    if not first:
                        eng.wait_ge(x1_out[par], (i - par) * 8)
                    link(v.tensor_scalar(x1[par][:, :], z2[:, :], mv[:, 1, 0:1], rdev[:, 1:2], ALU.subtract,
                                         ALU.mult))
                    assert n[0] == X1
                    link(v.tensor_copy(rdev[:, 0:1], rdev[:, 1:2]))
                    assert n[0] == STEPS

                v.memset(eps[:, :], EPS).then_inc(x_zero, 1)
                v.memset(zero[:, :], 0.0).then_inc(x_zero, 1)
                eng.wait_ge(w_in, 64)
                each(eng, tile)


def relate_phase(nc, a, t):
    with ExitStack() as ctx:
        s = Scope(nc, ctx, "re")
        GS = 8
        R = 3
        WA = 2 * WR + WR
        src = s.sb("src", [P, G1 * P], I32)
        row = s.sb("row", [P, G1 * P])
        keep = s.sb("keep", [P, G1 * P])
        win = s.sb("win", [1, G1 * P], I32)
        last = s.sb("last", [1, G1 * P], I32)
        idx = [s.sb(f"idx{i}", [P, GS], I32) for i in range(R)]
        kp = [s.sb(f"kp{i}", [P, GS]) for i in range(R)]
        xg = [s.sb(f"xg{i}", [P, GS, D]) for i in range(R)]
        oh = [s.sb(f"oh{i}", [P, GS, WR]) for i in range(R)]
        acc = [s.sb(f"acc{i}", [P, WA]) for i in range(GS)]
        p_a = [s.ps(f"pa{i}", [P, 512]) for i in range(4)]

        tables_in = s.sem("tables_in")
        idx_set = s.sem("idx_set")
        pool_on = s.sem("pool_on")
        x_in = [[s.sem(f"x_in{i}{g}") for g in range(2)] for i in range(R)]
        hot = s.sem("hot")
        kept = s.sem("kept")
        summed = s.sem("summed")
        acc_done = s.sem("acc_done")
        stored = [s.sem(f"stored{i}") for i in range(GS)]
        acc_zero = s.sem("acc_zero")

        def each(eng, body):
            for j in range(R):
                body(j, j, 0, True)
            with eng.Fori(1, K1 // GS // R) as k:
                for j in range(R):
                    body(k * R + j, j, k, False)
        assert K1 % (GS * R) == 0

        def store(eng, n, odd):
            for g in range(odd, GS, 2):
                w = eng.value_load(win[0:1, bass.ds(n * GS + g, 1)], min_val=0, max_val=NW - 1)
                z = eng.value_load(last[0:1, bass.ds(n * GS + g, 1)], min_val=0, max_val=1)
                eng.wait_ge(acc_done, n * GS + g + 1)
                eng.dma_start(t.agg[bass.ds(w * P, P), :], acc[g][:, :], cond=z).then_inc(stored[g], 16)

        with nc.Block() as block:
            @block.gpsimd
            def _(eng):
                def gather(n, par, k, first):
                    if not first:
                        eng.wait_ge(x_in[par][1], k * 64)
                    nc.gpsimd.tensor_copy(idx[par][:, :], src[:, bass.ds(n * GS, GS)]).then_inc(idx_set, 1)
                    eng.wait_ge(idx_set, n + 1)
                    eng.sem_inc(pool_on, 1)
                    for g in range(GS):
                        if g % 4 == 0 and not first:
                            eng.wait_ge(summed, (n - R) * GS + g + 4)
                            eng.sem_inc(pool_on, 1)
                        eng.indirect_dma_start(
                            out=xg[par][:, g, :], out_offset=None, in_=t.x1,
                            in_offset=bass.IndirectOffsetOnAxis(ap=idx[par][:, g:g + 1], axis=0),
                        ).then_inc(x_in[par][g // 4], 16)
                eng.wait_ge(tables_in, 16 * 5)
                each(eng, gather)

            @block.tensor
            def _(eng):
                def sums(n, par, k, first):
                    eng.wait_ge(hot, n + 1)
                    for g in range(GS):
                        i = n * GS + g
                        if g % 4 == 0:
                            eng.wait_ge(x_in[par][g // 4], k * 64 + 64)
                        if not (first and par == 0 and g < 4):
                            eng.wait_ge(acc_done, i - 3)
                        o = p_a[g % 4]
                        for half in range(2):
                            eng.matmul(o[:, WR * half:WR * half + WR], xg[par][:, g, P * half:P * half + P], oh[par][:, g, :],
                                       start=True, stop=True)
                        eng.matmul(o[:, 2 * WR:WA], t.ones[:, :], oh[par][:, g, :],
                                   start=True, stop=True).then_inc(summed, 1)
                each(eng, sums)

            @block.vector
            def _(eng):
                v = nc.vector

                def one_hots(n, par, first):
                    if not first:
                        eng.wait_ge(summed, (n - R + 1) * GS)
                    v.tensor_tensor(oh[par][:, :, :], t.iota[:, 0:WR].unsqueeze(1).to_broadcast([P, GS, WR]),
                                    row[:, bass.ds(n * GS, GS)].unsqueeze(2).to_broadcast([P, GS, WR]),
                                    ALU.is_equal).then_inc(hot, 1)

                def group(n, par, k, first):
                    if par == 0 and first:
                        one_hots(0, 0, True)
                    one_hots(n + 1, (par + 1) % R, first and par < R - 1)
                    if not first:
                        eng.wait_ge(acc_done, (n - R + 1) * GS)
                    v.tensor_copy(kp[par][:, :], keep[:, bass.ds(n * GS, GS)]).then_inc(kept, 1)
                    eng.wait_ge(kept, n + 1)
                    for g in range(GS):
                        i = n * GS + g
                        eng.wait_ge(summed, i + 1)
                        if not (first and par == 0):
                            eng.wait_ge(stored[g], n * 16)
                        if not (first and par == 0 and g == 0):
                            eng.wait_ge(acc_done, i)
                        v.scalar_tensor_tensor(acc[g][:, :], acc[(g - 1) % GS][:, :], kp[par][:, g:g + 1],
                                               p_a[g % 4][:, 0:WA], ALU.mult, ALU.add).then_inc(acc_done, 1)
                eng.wait_ge(tables_in, 16 * 5)
                v.memset(acc[GS - 1][:, :], 0.0).then_inc(acc_zero, 1)
                eng.wait_ge(acc_zero, 1)
                each(eng, group)

            @block.sync
            def _(eng):
                for j, of in enumerate((src, row, keep, win, last)):
                    eng.dma_start(of[:, :], t.tables1[j][:, :]).then_inc(tables_in, 16)
                eng.wait_ge(tables_in, 16 * 5)

                each(eng, lambda n, par, k, first: store(eng, n, 0))
                for g in range(0, GS, 2):
                    eng.wait_ge(stored[g], K1 // GS * 16)

            @block.scalar
            def _(eng):
                eng.wait_ge(tables_in, 16 * 5)
                each(eng, lambda n, par, k, first: store(eng, n, 1))
                for g in range(1, GS, 2):
                    eng.wait_ge(stored[g], K1 // GS * 16)


def mix_phase(nc, a, out, t):
    with ExitStack() as ctx:
        s = Scope(nc, ctx, "mx")
        SN = SBW * WN
        SR = SBW * WR
        QP = 4 * WR
        HH = SN // 2
        w = s.sb("w", [P, R6, 2, D])
        wrow = s.sb("wrow", [P, 10, D])
        wt = s.sb("wt", [P, 2, 10, P])
        b_in = s.sb("b_in", [P, R6, 2])
        qkv_b = s.sb("qkv_b", [P, 6])
        out_b = s.sb("out_b", [P, 2])
        proj_b = s.sb("proj_b", [P, D])
        eps = s.sb("eps", [P, 1])
        one = s.sb("one", [WR, WN])
        member0 = s.sb("member0", [WR, WN])
        member = s.sb("member", [WR, WN])
        member6 = s.sb("member6", [WR, WN])
        member_t = s.sb("member_t", [WN, WR])
        same = s.sb("same", [WR, WR])
        mask = s.sb("mask", [WR, 2 * WR], BF16)
        agg = [s.sb(f"agg{i}", [P, SBW, 3 * WR]) for i in range(2)]
        x1 = [s.sb(f"x1{i}", [HH, 2, D]) for i in range(2)]
        xb = [s.sb(f"xb{i}", [HH, 2, D]) for i in range(2)]
        st = s.sb("st", [P, 2, SR])
        qk = s.sb("qk", [P, 4, SR])
        top = [s.sb(f"top{i}", [WR, H]) for i in range(2)]
        ntop = [s.sb(f"ntop{i}", [WR, H]) for i in range(2)]
        pr = [s.sb(f"pr{i}", [WR, H, WR]) for i in range(3)]
        den = [s.sb(f"den{i}", [WR, H]) for i in range(3)]
        rden = [s.sb(f"rden{i}", [WR, H]) for i in range(3)]
        gd = [s.sb(f"gd{i}", [WR, H, WN]) for i in range(3)]
        gt = [s.sb(f"gt{i}", [WR, H * WN]) for i in range(2)]
        srow = [s.sb(f"srow{i}", [WR, D]) for i in range(4)]
        ut = s.sb("ut", [P, 2, H, SN])
        att = s.sb("att", [P, 2, SN])
        hid = s.sb("hid", [P, 2, SN])
        z = s.sb("z", [HH, 2, D])
        stats = s.sb("stats", [HH, 2, 6])
        mv = s.sb("mv", [HH, 2, 2])
        dev = s.sb("dev", [HH, 2])
        rdev = s.sb("rdev", [HH, 2])
        y = [s.sb(f"y{i}", [HH, 2, D]) for i in range(2)]
        p_g = [s.ps(f"pg{i}", [P, 512]) for i in range(2)]
        p_qk = [s.ps(f"pqk{i}", [P, 512]) for i in range(2)]
        p_sc = [[s.ps(f"psc{i}", [P, 512]) for i in range(2)], p_qk]
        p_gt = s.ps("pgt", [P, 512])
        p_u = s.ps("pu", [P, 512])

        w_in = s.sem("w_in")
        made = s.sem("made")
        mask_step = s.sem("mask_step")
        mask_ps = s.sem("mask_ps")
        wt_ps = s.sem("wt_ps")
        wt_done = s.sem("wt_done")
        agg_in = [s.sem(f"agg_in{i}") for i in range(2)]
        xb_done = s.sem("xb_done")
        g_ps = s.sem("g_ps")
        g_done = s.sem("g_done")
        qk_ps = s.sem("qk_ps")
        qk_done = s.sem("qk_done")
        sc_ps = s.sem("sc_ps")
        top_done = s.sem("top_done")
        ntop_done = s.sem("ntop_done")
        pr_done = s.sem("pr_done")
        rden_done = s.sem("rden_done")
        gd_done = s.sem("gd_done")
        row_ps = s.sem("row_ps")
        row_done = s.sem("row_done")
        gt_ps = s.sem("gt_ps")
        gt_done = s.sem("gt_done")
        u_ps = s.sem("u_ps")
        u_done = s.sem("u_done")
        stat = s.sem("stat")
        aggr = s.sem("aggr")
        dve_on = s.sem("dve_on")
        dev_done = s.sem("dev_done")
        rdev_done = s.sem("rdev_done")
        y_done = s.sem("y_done")
        y_out = [s.sem(f"y_out{i}") for i in range(2)]

        NG = 2 * R6
        NT = NG + 6
        W_LOADS = 7
        plan = ([("sum", k) for k in range(4)] + [("att", 0), ("att", 1)] + [("sum", k) for k in range(4, 8)] +
                [("hid", 0), ("hid", 1)] + [("sum", k) for k in range(8, NG)] + [("y", 0), ("y", 1)])

        def products(i, first):
            if first:
                return [(k, "sum", k) for k in range(NG)]
            return [(i * NT - 6 + k, kind, j) for k, (kind, j) in enumerate(plan)]

        def nodes_last():
            rest = [p for p in plan if p[0] != "sum"]
            return [(NSB * NT - 6 + k, kind, j) for k, (kind, j) in enumerate(rest)]

        def each(eng, body):
            body(0, 0, True)
            body(1, 1, False)
            with eng.Fori(1, NSB // 2) as k:
                body(k * 2, 0, False)
                body(k * 2 + 1, 1, False)
            body(NSB - 1, 0, False)
        assert NSB % 2 == 1

        with nc.Block() as block:
            @block.sync
            def _(eng):
                eng.dma_start(w[:, :, :, :].rearrange("p r k n -> p (r k) n"),
                              a["L1_gnn_W"].rearrange("r (k p) n -> p (r k) n", p=P)).then_inc(w_in, 16)
                for o, n, name in ((0, 6, "in_proj_w"), (6, 2, "attn_out_w"), (8, 2, "proj_w")):
                    eng.dma_start(wrow[:, o:o + n, :], a[f"L1_gnn_{name}"].rearrange("(k p) n -> p k n", p=P)
                                  ).then_inc(w_in, 16)
                eng.dma_start(qkv_b[:, :], a["L1_gnn_in_proj_b"].rearrange("(k p) -> p k", p=P),
                              allow_slow_non_contiguous=True).then_inc(w_in, 16)
                eng.dma_start(out_b[:, :], a["L1_gnn_attn_out_b"].rearrange("(k p) -> p k", p=P),
                              allow_slow_non_contiguous=True).then_inc(w_in, 16)
                eng.dma_start(proj_b[:, :], a["L1_gnn_proj_b"].partition_broadcast(P)).then_inc(w_in, 16)
                for r in range(R6):
                    eng.dma_start(b_in[:, r, :], a["L1_gnn_b"][r, :].rearrange("(k p) -> p k", p=P),
                                  allow_slow_non_contiguous=True).then_inc(w_in, 16)

                def store(i, par):
                    eng.wait_ge(y_done, i * 2 + 2)
                    full = not (past(i, NSB - 1) and isinstance(i, int))
                    for half in range(2):
                        rows = HH if full else min(HH, N - i * SN - half * HH)
                        eng.dma_start(out[bass.ds(i * SN + half * HH, rows), :],
                                      y[par][0:rows, half, :]).then_inc(y_out[par], 16)

                def load(i, par, first):
                    if past(i, 2):
                        eng.wait_ge(g_ps, i * NT - NG)
                        eng.wait_ge(xb_done, i * 2 - 2)
                    eng.dma_start(agg[par][:, :, :], t.agg[bass.ds(i * (SBW * P), SBW * P), :].rearrange(
                        "(w p) c -> p w c", p=P)).then_inc(agg_in[par], 16)
                    eng.dma_start(x1[par][:, :, :], t.x1[bass.ds(i * SN, SN), :].rearrange("(h p) c -> p h c", p=HH)
                                  ).then_inc(agg_in[par], 16)
                    if past(i, 2):
                        store(i - 2, par)
                each(eng, load)
                store(NSB - 2, 1)
                store(NSB - 1, 0)
                for par in range(2):
                    eng.wait_ge(y_out[par], 32 * ((NSB + 1 - par) // 2))

            @block.gpsimd
            def _(eng):
                eng.memset(one[:, :], 1.0).then_inc(made, 1)
                eng.wait_ge(made, 1)
                eng.affine_select(member0[:, :], one[:, :], [[-R6, WN]], ALU.is_ge, 0.0, base=0,
                                  channel_multiplier=1).then_inc(made, 1)
                eng.wait_ge(made, 2)
                eng.affine_select(member[:, :], member0[:, :], [[R6, WN]], ALU.is_ge, 0.0, base=R6 - 1,
                                  channel_multiplier=-1).then_inc(made, 1)
                eng.wait_ge(w_in, 16 * (W_LOADS + R6))

                def add_bias(i, par, first):
                    eng.wait_ge(agg_in[par], (i - par) * 16 + 32)
                    if past(i, 2):
                        eng.wait_ge(g_done, (i - 1) * NT - 6 + NT)
                    for half in range(2):
                        nc.gpsimd.tensor_tensor(xb[par][:, half, :], x1[par][:, half, :], proj_b[0:HH, :],
                                                ALU.add).then_inc(xb_done, 1)
                each(eng, add_bias)

            @block.tensor
            def _(eng):
                eng.wait_ge(w_in, 16 * (W_LOADS + R6))
                for o in range(10):
                    if o >= 2:
                        eng.wait_ge(wt_done, o - 1)
                    for k in range(2):
                        mm = eng.transpose(p_g[o % 2][:, P * k:P * k + P], wrow[:, o, P * k:P * k + P], t.ident[:, :])
                    mm.then_inc(wt_ps, 1)
                eng.wait_ge(made, 3)
                eng.transpose(p_sc[0][0][0:WN, 0:WR], member[:, :], t.ident[0:WR, 0:WR]).then_inc(mask_ps, 1)
                eng.wait_ge(mask_step, 1)
                eng.matmul(p_sc[0][1][0:WR, 0:WR], member_t[:, :], member_t[:, :], start=True,
                           stop=True).then_inc(mask_ps, 1)
                eng.wait_ge(mask_step, 4)
                eng.wait_ge(wt_done, 10)

                def product(i, par, n, kind, j, first, between=4):
                    o = p_g[j % 2]
                    if kind == "sum" and j < 2:
                        if not first:
                            eng.wait_ge(row_done, i * SBW - 1 + j)
                    else:
                        eng.wait_ge(g_done, n - 1)
                    if kind == "sum":
                        r, half = j // 2, j % 2
                        for k in range(2):
                            mm = eng.matmul(o[:, 0:SN], w[:, r, k, P * half:P * half + P],
                                            agg[par][:, :, k * WR + r:(k + 1) * WR:R6], start=(k == 0), stop=(k == 1))
                    elif kind == "att":
                        for e in range(2):
                            for k in range(2):
                                mm = eng.matmul(o[HD * e:HD * e + HD, 0:SN], wt[:, k, 4 + j, HD * e:HD * e + HD],
                                                ut[:, k, 2 * j + e, :], start=(k == 0), stop=(k == 1))
                    elif kind == "hid":
                        if j == 0:
                            eng.wait_ge(g_done, n - between)
                        for k in range(2):
                            eng.matmul(o[:, 0:SN], wt[:, k, 6 + j, :], att[:, k, :], start=(k == 0), stop=False)
                        for half in range(2):
                            mm = eng.matmul(o[:, HH * half:HH * half + HH], x1[1 - par][:, half, P * j:P * j + P],
                                            t.ident[0:HH, 0:HH], start=False, stop=(half == 1))
                    else:
                        if j == 0:
                            eng.wait_ge(g_done, n - between)
                        for k in range(2):
                            mm = eng.matmul(o[0:HH, 0:D], hid[:, k, HH * j:HH * j + HH],
                                            wt[:, k, 8:10, :].rearrange("p o c -> p (o c)"),
                                            start=(k == 0), stop=(k == 1))
                    mm.then_inc(g_ps, 1)

                def scores(v, x):
                    if past(v, 2):
                        eng.wait_ge(pr_done, v - 1)
                    for e in range(2):
                        o = p_sc[e][x % 2]
                        eng.matmul(o[0:WR, 0:2 * WR], t.ident_b[0:WR, 0:WR], mask[:, :], start=True, stop=False)
                    for b in range(2):
                        for e in range(2):
                            rows = slice(HD * e, HD * e + HD)
                            eng.matmul(p_sc[e][x % 2][0:WR, WR * b:WR * b + WR], qk[rows, b, WR * x:WR * x + WR],
                                       qk[rows, 2 + b, WR * x:WR * x + WR], start=False, stop=(b == 1)
                                       ).then_inc(sc_ps, 1)
                    if past(v, 2):
                        eng.wait_ge(row_done, v - 1)
                    for k in range(2):
                        mm = eng.transpose(p_g[x % 2][0:WR, P * k:P * k + P], st[:, k, WR * x:WR * x + WR], t.ident[:, :])
                    mm.then_inc(row_ps, 1)

                def weigh(v, x):
                    eng.wait_ge(gd_done, v + 1)
                    if past(v, 1):
                        eng.wait_ge(gt_done, v)
                    for h in range(H):
                        mm = eng.matmul(p_gt[0:WR, WN * h:WN * h + WN], pr[x % 3][:, h, :], gd[x % 3][:, h, :],
                                        start=True, stop=True)
                    mm.then_inc(gt_ps, 1)

                def gather(v, x):
                    eng.wait_ge(gt_done, v + 1)
                    eng.wait_ge(row_done, v + 1)
                    if past(v, 1):
                        eng.wait_ge(u_done, v)
                    for k in range(2):
                        mm = eng.matmul(p_u[:, H * WN * k:H * WN * k + H * WN], srow[x % 4][:, P * k:P * k + P], gt[x % 2][:, :],
                                        start=True, stop=True)
                    mm.then_inc(u_ps, 1)

                def superblock(i, par, first):
                    eng.wait_ge(agg_in[par], (i - par) * 16 + 32)
                    for n, kind, j in products(i, first):
                        product(i, par, n, kind, j, first)
                        if not first and kind == "sum" and j < 3:
                            if j < 2:
                                weigh(i * SBW - 2 + j, SBW - 2 + j)
                            gather(i * SBW - 3 + j, SBW - 3 + j)
                        if not first and kind == "sum" and j == 3:
                            eng.wait_ge(u_done, i * SBW)
                    eng.wait_ge(g_done, NG if first else i * NT - 6 + NT - 2)
                    for piece in range(3):
                        for c in range(4):
                            n = i * 12 + piece * 4 + c
                            if not (first and piece == 0 and c < 2):
                                eng.wait_ge(qk_done, n - 1)
                            for k in range(2):
                                mm = eng.matmul(p_qk[c % 2][:, 0:QP], wt[:, k, c, :],
                                                st[:, k, QP * piece:QP * piece + QP], start=(k == 0), stop=(k == 1))
                            mm.then_inc(qk_ps, 1)
                    eng.wait_ge(qk_done, i * 12 + 12)
                    eng.wait_ge(g_done, NG if first else i * NT - 6 + NT - 2)
                    for x in range(SBW):
                        scores(i * SBW + x, x)
                        if x >= 2:
                            weigh(i * SBW + x - 2, x - 2)
                        if x >= 3:
                            gather(i * SBW + x - 3, x - 3)

                each(eng, superblock)
                for j in range(3):
                    if j < 2:
                        weigh(NSB * SBW - 2 + j, SBW - 2 + j)
                    gather(NSB * SBW - 3 + j, SBW - 3 + j)
                eng.wait_ge(u_done, NSB * SBW)
                for n, kind, j in nodes_last():
                    product(NSB, 1, n, kind, j, False, between=0)

            @block.scalar
            def _(eng):
                act = nc.scalar.activation

                def copy_gt(v, x):
                    eng.wait_ge(gt_ps, v + 1)
                    if past(v, 2):
                        eng.wait_ge(u_ps, v - 1)
                    act(gt[x % 2][:, :], p_gt[0:WR, 0:H * WN], ACT.Copy).then_inc(gt_done, 1)

                def copy_u(v, x):
                    eng.wait_ge(u_ps, v + 1)
                    act(ut[:, :, :, WN * x:WN * x + WN],
                        p_u[:, 0:2 * H * WN].rearrange("p (k h n) -> p k h n", k=2, h=H),
                        ACT.Copy).then_inc(u_done, 1)

                def last_windows(i):
                    for j in range(3):
                        if j < 2:
                            copy_gt(i * SBW - 2 + j, SBW - 2 + j)
                        copy_u(i * SBW - 3 + j, SBW - 3 + j)

                def deviations(i):
                    eng.wait_ge(aggr, i * 2)
                    act(dev[:, :], mv[:, :, 1], ACT.Sqrt, bias=eps[0:HH, 0:1]).then_inc(dev_done, 1)

                def superblock(i, par, first):
                    if not first:
                        last_windows(i)
                    for piece in range(3):
                        for c in range(4):
                            eng.wait_ge(qk_ps, i * 12 + piece * 4 + c + 1)
                            act(qk[:, c, QP * piece:QP * piece + QP], p_qk[c % 2][:, 0:QP], ACT.Identity,
                                bias=qkv_b[:, c:c + 1]).then_inc(qk_done, 1)
                        if piece == 0 and not first:
                            deviations(i)
                    for x in range(SBW):
                        v = i * SBW + x
                        eng.wait_ge(ntop_done, v + 1)
                        if past(v, 3):
                            eng.wait_ge(gt_ps, v - 2)
                            eng.wait_ge(rden_done, v - 2)
                        for h in range(H):
                            ins = act(pr[x % 3][:, h, :], p_sc[h % 2][x % 2][0:WR, WR * (h // 2):WR * (h // 2) + WR], ACT.Exp,
                                      bias=ntop[x % 2][:, h:h + 1], scale=HD ** -0.5,
                                      accum_out=den[x % 3][:, h:h + 1])
                        ins.then_inc(pr_done, 1)
                        if x >= 2:
                            copy_gt(v - 2, x - 2)
                        if x >= 3:
                            copy_u(v - 3, x - 3)

                eng.wait_ge(mask_step, 4)
                each(eng, superblock)
                last_windows(NSB)
                deviations(NSB)

            @block.vector
            def _(eng):
                v_ = nc.vector
                for o in range(10):
                    eng.wait_ge(wt_ps, o + 1)
                    v_.tensor_copy(wt[:, :, o, :], p_g[o % 2][:, 0:D].rearrange("p (k c) -> p k c", k=2)
                                   ).then_inc(wt_done, 1)
                eng.wait_ge(mask_ps, 1)
                v_.memset(eps[:, :], EPS)
                v_.tensor_scalar(member6[:, :], member[:, :], 1.0 / R6, None, ALU.mult)
                v_.tensor_copy(member_t[:, :], p_sc[0][0][0:WN, 0:WR]).then_inc(mask_step, 1)
                eng.wait_ge(mask_ps, 2)
                v_.tensor_scalar(same[:, :], p_sc[0][1][0:WR, 0:WR], -1.0, BIG, ALU.add, ALU.mult).then_inc(mask_step, 1)
                eng.wait_ge(mask_step, 2)
                for h in range(2):
                    v_.tensor_copy(mask[:, WR * h:WR * h + WR], same[:, :]).then_inc(mask_step, 1)

                def take(i, par, n, kind, j):
                    o = p_g[j % 2]
                    eng.wait_ge(g_ps, n + 1)
                    if kind == "sum":
                        r, half = j // 2, j % 2
                        ins = v_.scalar_tensor_tensor(
                            st[:, half, r:SR:R6].rearrange("p (w n) -> p w n", w=SBW), agg[par][:, :, 2 * WR + r:3 * WR:R6],
                            b_in[:, r, half:half + 1], o[:, 0:SN].rearrange("p (w n) -> p w n", w=SBW),
                            ALU.mult, ALU.add)
                    elif kind == "att":
                        ins = v_.tensor_scalar(att[:, j, :], o[:, 0:SN], qkv_b[:, 4 + j:5 + j], None, ALU.add)
                    elif kind == "hid":
                        ins = v_.tensor_scalar(hid[:, j, :], o[:, 0:SN], out_b[:, j:j + 1], None, ALU.add)
                    else:
                        if j == 0:
                            eng.wait_ge(xb_done, i * 2)
                            if past(i, 2):
                                eng.wait_ge(y_done, i * 2 - 2)
                        ins = v_.tensor_tensor(z[:, j, :], o[0:HH, 0:D], xb[1 - par][:, j, :], ALU.add)
                    ins.then_inc(g_done, 1)

                def moments(i, n):
                    for half in range(2):
                        eng.wait_ge(g_done, n + half)
                        if half == 0 and past(i, 2):
                            eng.wait_ge(aggr, i * 2 - 2)
                        v_.bn_stats(stats[:, half, :], z[:, half, :]).then_inc(stat, 1)
                    for half in range(2):
                        eng.wait_ge(stat, i * 2 - 1 + half)
                        if half == 0 and past(i, 2):
                            eng.wait_ge(y_done, i * 2 - 2)
                        eng.sem_inc(dve_on, 1)
                        v_.bn_aggr(mv[:, half, :], stats[:, half, :]).then_inc(aggr, 1)

                def norm(i, par):
                    eng.wait_ge(dev_done, i)
                    v_.reciprocal(rdev[:, :], dev[:, :]).then_inc(rdev_done, 1)
                    eng.wait_ge(rdev_done, i)
                    if past(i, 3):
                        eng.wait_ge(y_out[par], (i - 1 - par) * 16)
                    for half in range(2):
                        v_.tensor_scalar(y[par][:, half, :], z[:, half, :], mv[:, half, 0:1], rdev[:, half:half + 1],
                                         ALU.subtract, ALU.mult).then_inc(y_done, 1)

                def maxima(v, x):
                    eng.wait_ge(sc_ps, v * 4 + 4)
                    if past(v, 2):
                        eng.wait_ge(ntop_done, v - 1)
                    for e in range(2):
                        v_.tensor_reduce(top[x % 2][:, e:H:2],
                                         p_sc[e][x % 2][0:WR, 0:2 * WR].rearrange("p (b m) -> p b m", b=2),
                                         AXX, ALU.max).then_inc(top_done, 1)

                def over(v, x):
                    eng.wait_ge(top_done, v * 2 + 2)
                    if past(v, 2):
                        eng.wait_ge(pr_done, v - 1)
                    v_.tensor_scalar(ntop[x % 2][:, :], top[x % 2][:, :], -HD ** -0.5, None,
                                     ALU.mult).then_inc(ntop_done, 1)

                def rows(v, x):
                    eng.wait_ge(row_ps, v + 1)
                    if past(v, 4):
                        eng.wait_ge(u_ps, v - 3)
                    v_.tensor_copy(srow[x % 4][:, :], p_g[x % 2][0:WR, 0:D]).then_inc(row_done, 1)

                def shares(v, x):
                    eng.wait_ge(pr_done, v + 1)
                    v_.reciprocal(rden[x % 3][:, :], den[x % 3][:, :]).then_inc(rden_done, 1)
                    eng.wait_ge(rden_done, v + 1)
                    if past(v, 3):
                        eng.wait_ge(gt_ps, v - 2)
                    v_.tensor_tensor(gd[x % 3][:, :, :], member6[:, :].unsqueeze(1).to_broadcast([WR, H, WN]),
                                     rden[x % 3][:, :].unsqueeze(2).to_broadcast([WR, H, WN]),
                                     ALU.mult).then_inc(gd_done, 1)

                def superblock(i, par, first):
                    eng.wait_ge(agg_in[par], (i - par) * 16 + 32)
                    for n, kind, j in products(i, first):
                        take(i, par, n, kind, j)
                    if not first:
                        moments(i, i * NT - 6 + NT - 1)
                    for x in range(SBW):
                        v = i * SBW + x
                        maxima(v, x)
                        over(v, x)
                        if x >= 1:
                            shares(v - 1, x - 1)
                        rows(v, x)
                        if x == 2 and not first:
                            norm(i, 1 - par)
                    shares(i * SBW + SBW - 1, SBW - 1)

                each(eng, superblock)
                for n, kind, j in nodes_last():
                    take(NSB, 1, n, kind, j)
                moments(NSB, NSB * NT - 6 + 5)
                norm(NSB, 0)


class Tensors:
    pass


def resnorm_gnn(nc, a, out):
    with ExitStack() as ctx:
        s = Scope(nc, ctx, "g")
        t = Tensors()
        t.pads = {n: nc.dram_tensor(f"pad_{n}", [EPAD], I32, kind="Internal").ap()
                  for n in ("src", "dst", "edge_type_6", "edge_type_64")}
        t.lastb = nc.dram_tensor("lastb", [G0 * P, H, 514], F32, kind="Internal").ap()
        t.kv = nc.dram_tensor("kv_rows", [NB * P, 2 * D], F32, kind="Internal").ap()
        t.q3 = nc.dram_tensor("q3_rows", [NB * P, 3 * D], BF16, kind="Internal").ap()
        t.tables1 = [nc.dram_tensor(f"tables1_{k}", [P if k < 3 else 1, G1 * P], dt, kind="Internal").ap()
                     for k, dt in enumerate((I32, F32, F32, I32, I32))]
        t.x1 = nc.dram_tensor("x1_rows", [NW * WN, D], F32, kind="Internal").ap()
        t.agg = nc.dram_tensor("agg_t", [NW * P, 3 * WR], F32, kind="Internal").ap()
        t.iota_i = s.sb("iota_i", [P, P], I32)
        t.iota = s.sb("iota", [P, P])
        t.iota_b = s.sb("iota_b", [P, R64], BF16)
        t.col = s.sb("col", [P, 1])
        t.ident = s.sb("ident", [P, P])
        t.ident_b = s.sb("ident_b", [P, P], BF16)
        t.ones = s.sb("ones", [P, P])
        with ExitStack() as layer0:
            s0 = Scope(nc, layer0, "g0")
            t.src0 = s0.sb("src0", [P, G0 * P * 4], I32)
            t.node0 = s0.sb("node0", [P, G0 * P * 4])
            t.type0 = s0.sb("type0", [P, G0 * P * 4], BF16)
            t.blk = s0.sb("blk", [P, G0 * P], I32)
            t.rel3 = s0.sb("rel3", [R64, 3, D], BF16)
            tables_phase(nc, a, t)
            project_phase(nc, a, t)
            t.sum0 = s0.sb("sum0", [P, NB * H * (HD + 1)])
            t.max0 = s0.sb("max0", [P, NB * H])
            attend_phase(nc, a, t)
            update_phase(nc, a, t)
        relate_phase(nc, a, t)
        mix_phase(nc, a, out, t)


_L0 = ["query_emb", "Wq", "bq", "Wk", "bk", "Wv", "bv", "rel_w", "Wo", "bo", "gamma", "beta"]
_L1 = ["W", "b", "in_proj_w", "in_proj_b", "attn_out_w", "attn_out_b", "proj_w", "proj_b"]
_INS = (["x", "src", "dst", "edge_type_6", "edge_type_64"] + [f"L0_gnn_{n}" for n in _L0] +
        [f"L1_gnn_{n}" for n in _L1])


def kernel(**inputs):
    import numpy as _np
    import concourse.bacc as _bacc
    from concourse import mybir as _mybir
    from concourse.bass_utils import run_bass_kernel_spmd as _run

    nc = _bacc.Bacc("TRN2", target_bir_lowering=False, num_devices=1)
    arrays, aps = {}, {}
    for name in _INS:
        arr = _np.ascontiguousarray(inputs[name])
        arrays[f"in_{name}_dram"] = arr
        aps[name] = nc.dram_tensor(f"in_{name}_dram", arr.shape, _mybir.dt.from_np(arr.dtype),
                                   kind="ExternalInput").ap()
    out = nc.dram_tensor("out_0_dram", (N, D), _mybir.dt.float32, kind="ExternalOutput").ap()
    resnorm_gnn(nc, aps, out)
    r = _run(nc, [arrays], core_ids=[0])
    return r.results[0]["out_0_dram"]
```

```python
from contextlib import ExitStack

import concourse.bass as bass
from concourse import mybir

ALU = mybir.AluOpType
ACT = mybir.ActivationFunctionType
AXX = mybir.AxisListType.X
F32 = mybir.dt.float32
BF16 = mybir.dt.bfloat16
I32 = mybir.dt.int32

P = 128
N = 6250
E = 200000
D = 256
H = 4
HD = D // H
R6 = 6
R64 = 64
EPAD = 392 * 512
HEADS = -(-E // 512)
FAR = 1 << 20
BIG = float(2 ** 100)
EPS = 1e-5

NB = -(-N // P)
C0 = 512
SUP = 4
K0 = -(-(E // C0 + NB + 1) // SUP) * SUP
NSUP = K0 // SUP
WN = 21
WR = WN * R6
SBW = 12
NSB = -(-N // (WN * SBW))
NW = NSB * SBW
C1 = 128
K1 = -(-(E // C1 + NW + 1) // 24) * 24
G0, G1 = -(-K0 // P), -(-(K1 + 8) // P)
GB0, GB1 = 1, -(-(NW + 1) // P)


class Scope:

    def __init__(self, nc, ctx, tag):
        self.nc, self.ctx, self.tag = nc, ctx, tag

    def sb(self, name, shape, dt=F32):
        return self.ctx.enter_context(self.nc.sbuf_tensor(f"{self.tag}_{name}", shape, dt))

    def ps(self, name, shape, dt=F32):
        return self.ctx.enter_context(self.nc.psum_tensor(f"{self.tag}_{name}", shape, dt))

    def sem(self, name):
        return self.ctx.enter_context(self.nc.semaphore(f"{self.tag}_{name}"))


class Count:

    def __init__(self, sem):
        self.sem, self.n = sem, 0

    def up(self, ins):
        self.n += 1
        ins.then_inc(self.sem, 1)
        return self.n


def past(i, n):
    return not isinstance(i, int) or i >= n


def tables_phase(nc, a, t):
    with ExitStack() as ctx:
        s = Scope(nc, ctx, "tab")
        src1 = s.sb("src1", [P, G1 * P], I32)
        row1 = s.sb("row1", [P, G1 * P])
        keep = s.sb("keep", [P, G1 * P])
        win = s.sb("win", [P, G1 * P], I32)
        last = s.sb("last", [P, G1 * P], I32)
        tables_out = s.sem("tables_out")
        pad_i = s.sb("pad_i", [2, EPAD - E], I32)
        heads_i = s.sb("heads_i", [1, HEADS], I32)
        heads_r = s.sb("heads_r", [1, HEADS])
        heads = s.sb("heads", [P, HEADS])
        junk = s.sb("junk", [P, 512])
        pcol_i = s.sb("pcol_i", [P, 1], I32)
        bounds = s.sb("bounds", [P, GB1])
        cnt = s.sb("cnt", [P, GB1])
        cnt2 = s.sb("cnt2", [P, GB1])
        crow_i = s.sb("crow_i", [P, GB1], I32)
        crow = s.sb("crow", [P, GB1])
        found_i = s.sb("found_i", [P, 512], I32)
        found = s.sb("found", [P, 512])
        start = s.sb("start", [P, GB1])
        diag = s.sb("diag", [P, P])
        srow = s.sb("srow", [P, GB1 * P])
        num_i = s.sb("num_i", [P, GB1 * P], I32)
        shr_i = s.sb("shr_i", [P, GB1 * P], I32)
        tiles = s.sb("tiles", [P, GB1 * P])
        zero = s.sb("zero", [P, GB1 * P])
        tend = s.sb("tend", [P, GB1 * P])
        tbeg = s.sb("tbeg", [P, GB1 * P])
        off = s.sb("off", [P, GB1 * P])
        doff = s.sb("doff", [P, GB1 * P])
        step = s.sb("step", [P, G1])
        rng = s.sb("rng", [P, G1])
        e0f = s.sb("e0f", [P, G1])
        e0i = s.sb("e0i", [P, G1], I32)
        rngneg = s.sb("rngneg", [P, G1])
        rows_i = s.sb("rows_i", [P, 2, 3, 512], I32)
        rows_f = s.sb("rows_f", [P, 3, 512])
        rows_b = s.sb("rows_b", [P, 2, C0], BF16)
        lastb = s.sb("lastb", [P, 514])
        rngrow = s.sb("rngrow", [P, G1 * P + 1])
        lastf = s.sb("lastf", [P, G1 * P])
        pb = s.ps("pb", [P, 512])
        pt = [s.ps(f"pt{i}", [P, 512]) for i in range(2)]

        pads_set = s.sem("pads_set")
        arrays_padded = s.sem("arrays_padded")
        heads_in = s.sem("heads_in")
        iota_done = s.sem("iota_done")
        dve = Count(s.sem("dve_done"))
        pe = Count(s.sem("pe_done"))
        gathered = s.sem("gathered")
        rows_in = [s.sem("rows_in0"), s.sem("rows_in1")]
        lastb_out = s.sem("lastb_out")
        rows0_out = s.sem("rows0_out")

        names = ("src", "dst", "edge_type_6", "edge_type_64")
        plan = {}

        def layer_plan():
            for L in (0, 1):
                gk = (G0, G1)[L]
                yield L, (P, WN)[L], (GB0, GB1)[L], (NB, NW)[L], (C0, C1)[L], gk

        def plan_rows(L, g):
            before = -(-G0 // 2) if g % 2 == 0 else G0 // 2
            return g // 2 + 1 + (before if L else 0)

        with nc.Block() as block:
            @block.vector
            def _(eng):
                v = nc.vector

                def link(ins):
                    eng.wait_ge(dve.sem, dve.up(ins))
                    return dve.n

                link(v.memset(pad_i[:, :], 0))
                plan["pad0"] = link(v.memset(pad_i[0:1, :], FAR))
                eng.wait_ge(iota_done, 4)
                link(v.tensor_copy(t.col[:, :], pcol_i[:, :]))
                link(v.tensor_copy(t.iota[:, :], t.iota_i[:, :]))
                link(v.tensor_scalar(t.ident[:, :], t.iota[:, :], t.col[:, 0:1], None, ALU.is_equal))
                link(v.tensor_copy(t.ident_b[:, :], t.ident[:, :]))
                link(v.memset(t.ones[:, :], 1.0))
                link(v.memset(zero[:, :], 0.0))
                link(v.memset(rngrow[:, :], -1.0))
                eng.wait_ge(heads_in, 16)
                plan["heads_r"] = link(v.tensor_copy(heads_r[:, :], heads_i[:, :]))
                eng.wait_ge(pe.sem, 1)
                link(v.tensor_copy(heads[:, :], pb[:, 0:HEADS]))
                pe_n = 1
                ptn = 0
                gath = 0
                for L, stride, gb, nr, cs, gk in layer_plan():
                    for g in range(gb):
                        link(v.tensor_scalar(bounds[:, g:g + 1], t.col[:, 0:1], float(P * g), float(stride),
                                             ALU.add, ALU.mult))
                        link(v.tensor_scalar(junk[:, 0:HEADS], heads[:, :], bounds[:, g:g + 1], 0.0,
                                             ALU.is_lt, ALU.add, accum_out=cnt[:, g:g + 1]))
                        link(v.tensor_scalar(crow[:, g:g + 1], cnt[:, g:g + 1], -1.0, 0.0, ALU.add, ALU.max))
                        plan["crow", L, g] = link(v.tensor_copy(crow_i[:, g:g + 1], crow[:, g:g + 1]))
                        gath += 1
                        eng.wait_ge(gathered, 16 * gath)
                        link(v.tensor_copy(found[:, :], found_i[:, :]))
                        link(v.tensor_scalar(junk[:, :], found[:, :], bounds[:, g:g + 1], 0.0,
                                             ALU.is_lt, ALU.add, accum_out=cnt2[:, g:g + 1]))
                        link(v.scalar_tensor_tensor(start[:, g:g + 1], crow[:, g:g + 1], 512.0,
                                                    cnt2[:, g:g + 1], ALU.mult, ALU.add))
                        plan["diag", L, g] = link(v.tensor_scalar(diag[:, :], t.ident[:, :], start[:, g:g + 1],
                                                                  None, ALU.mult))
                        pe_n += 1
                        eng.wait_ge(pe.sem, pe_n)
                        link(v.tensor_copy(srow[:, P * g:P * g + P], pb[:, 0:P]))
                    link(v.tensor_tensor(tiles[:, 0:nr], srow[:, 1:nr + 1], srow[:, 0:nr], ALU.subtract))
                    link(v.tensor_scalar(num_i[:, 0:nr], tiles[:, 0:nr], float(cs - 1), None, ALU.add))
                    link(v.tensor_scalar(shr_i[:, 0:nr], num_i[:, 0:nr], cs.bit_length() - 1, None,
                                         ALU.logical_shift_right))
                    link(v.tensor_scalar(tiles[:, 0:nr], shr_i[:, 0:nr], 1.0, None, ALU.max))
                    link(v.tensor_tensor_scan(tend[:, 0:nr], tiles[:, 0:nr], zero[:, 0:nr], 0.0, ALU.add, ALU.max))
                    link(v.tensor_tensor(tbeg[:, 0:nr], tend[:, 0:nr], tiles[:, 0:nr], ALU.subtract))
                    link(v.scalar_tensor_tensor(off[:, 0:nr], tbeg[:, 0:nr], float(-cs), srow[:, 0:nr],
                                                ALU.mult, ALU.add))
                    link(v.tensor_tensor(doff[:, 0:nr - 1], off[:, 1:nr], off[:, 0:nr - 1], ALU.subtract))
                    for g in range(gk):
                        link(v.tensor_scalar(step[:, g:g + 1], t.col[:, 0:1], float(P * g), None, ALU.add))
                        link(v.tensor_scalar(junk[:, 0:nr - 1], tend[:, 0:nr - 1], step[:, g:g + 1], 0.0,
                                             ALU.is_le, ALU.add, accum_out=rng[:, g:g + 1]))
                        link(v.scalar_tensor_tensor(junk[:, 0:nr - 1], tend[:, 0:nr - 1], step[:, g:g + 1],
                                                    doff[:, 0:nr - 1], ALU.is_le, ALU.mult,
                                                    accum_out=e0f[:, g:g + 1]))
                    link(v.scalar_tensor_tensor(e0f[:, 0:gk], step[:, 0:gk], float(cs), e0f[:, 0:gk],
                                                ALU.mult, ALU.add))
                    link(v.tensor_scalar(e0f[:, 0:gk], e0f[:, 0:gk], float(E), None, ALU.min))
                    plan["e0", L] = link(v.tensor_copy(e0i[:, 0:gk], e0f[:, 0:gk]))
                    link(v.tensor_scalar(rngneg[:, 0:gk], rng[:, 0:gk], float(-stride), None, ALU.mult))
                    for g in range(gk):
                        plan["rdiag", L, g] = link(v.tensor_scalar(diag[:, :], t.ident[:, :], rng[:, g:g + 1],
                                                                   None, ALU.mult))
                        pe_n += 1
                        eng.wait_ge(pe.sem, pe_n)
                        link(v.tensor_copy(rngrow[:, P * g:P * g + P], pb[:, 0:P]))
                    if L == 0:
                        link(v.tensor_copy(t.blk[:, :], rngrow[0:1, 0:G0 * P]))
                        link(v.memset(t.fresh0[:, 0:1], -BIG))
                        link(v.tensor_tensor(lastf[:, 0:G0 * P - 1], rngrow[:, 1:G0 * P], rngrow[:, 0:G0 * P - 1],
                                             ALU.not_equal))
                        link(v.tensor_scalar(t.fresh0[:, 1:G0 * P], lastf[:, 0:G0 * P - 1], -BIG, None, ALU.mult))
                        link(v.memset(rngrow[:, K0:K0 + 1], -1.0))
                        link(v.tensor_tensor(lastf[:, 0:K0], rngrow[:, 1:K0 + 1], rngrow[:, 0:K0],
                                             ALU.not_equal))
                        link(v.tensor_copy(t.last0[:, 0:K0], lastf[0:1, 0:K0]))
                    else:
                        link(v.tensor_copy(win[:, :], rngrow[:, 0:G1 * P]))
                        link(v.memset(keep[:, 0:1], 0.0))
                        link(v.tensor_tensor(keep[:, 1:G1 * P], rngrow[:, 1:G1 * P], rngrow[:, 0:G1 * P - 1],
                                             ALU.is_equal))
                        link(v.memset(rngrow[:, K1:K1 + 1], -1.0))
                        link(v.tensor_tensor(lastf[:, :], rngrow[:, 1:G1 * P + 1], rngrow[:, 0:G1 * P],
                                             ALU.not_equal))
                        link(v.tensor_copy(last[:, :], lastf[:, :]))
                    for g in range(gk):
                        ri = rows_i[:, g % 2, :, :]
                        eng.wait_ge(rows_in[g % 2], 48 * plan_rows(L, g))
                        link(v.tensor_copy(rows_f[:, :, 0:cs], ri[:, :, 0:cs]))
                        if L == 0:
                            if g:
                                eng.wait_ge(lastb_out, 64 * g)
                            link(v.memset(lastb[:, :], -BIG))
                            link(v.tensor_tensor(junk[:, 0:511], rows_f[:, 1, 0:511], rows_f[:, 1, 1:512],
                                                 ALU.not_equal))
                            plan["lastb", g] = link(v.tensor_scalar(lastb[:, 1:512], junk[:, 0:511], -BIG, None,
                                                                    ALU.mult))
                        link(v.tensor_scalar(rows_f[:, 1, 0:cs], rows_f[:, 1, 0:cs], rngneg[:, g:g + 1], None,
                                             ALU.add))
                        if L == 1:
                            link(v.scalar_tensor_tensor(rows_f[:, 1, 0:cs], rows_f[:, 1, 0:cs], float(R6),
                                                        rows_f[:, 2, 0:cs], ALU.mult, ALU.add))
                        if L == 0:
                            if g:
                                eng.wait_ge(rows0_out, 16 * g)
                            plan["rows_b", g] = link(v.tensor_copy(rows_b[:, :, :], rows_f[:, 1:3, :]))
                        plan["rows", L, g] = dve.n
                        pe_n += 1
                        eng.wait_ge(pe.sem, pe_n)
                        nj = cs // P
                        for dst, k in (((t.src0, 0), (t.node0, 1)) if L == 0 else
                                       ((src1, 0), (row1, 1))):
                            o = dst[:, P * g * nj:P * (g + 1) * nj].rearrange("p (s j) -> p j s", j=nj)
                            link(v.tensor_copy(o, pt[k][:, 0:cs].rearrange("p (j s) -> p j s", j=nj)))
                        plan["copied", L, g] = dve.n

            @block.gpsimd
            def _(eng):
                eng.iota(pcol_i[:, :], [[0, 1]], base=0, channel_multiplier=1).then_inc(iota_done, 2)
                eng.iota(t.iota_i[:, :], [[1, P]], base=0, channel_multiplier=0).then_inc(iota_done, 2)
                eng.wait_ge(arrays_padded, 16 * 8)
                n = 0
                for L, stride, gb, nr, cs, gk in layer_plan():
                    for g in range(gb):
                        eng.wait_ge(dve.sem, plan["crow", L, g])
                        eng.indirect_dma_start(
                            out=found_i[:, :], out_offset=None,
                            in_=t.pads["dst"].rearrange("(r c) -> r c", c=512),
                            in_offset=bass.IndirectOffsetOnAxis(ap=crow_i[:, g:g + 1], axis=0),
                        ).then_inc(gathered, 16)
                    eng.wait_ge(dve.sem, plan["e0", L])
                    for g in range(gk):
                        if g >= 2:
                            eng.wait_ge(dve.sem, plan["copied", L, g - 2])
                        elif L:
                            eng.wait_ge(dve.sem, plan["copied", 0, G0 - 1])
                        for k, name in enumerate(("src", "dst", ("edge_type_64", "edge_type_6")[L])):
                            eng.indirect_dma_start(
                                out=rows_i[:, g % 2, k, 0:cs], out_offset=None,
                                in_=t.pads[name].rearrange("(r c) -> r c", c=1),
                                in_offset=bass.IndirectOffsetOnAxis(ap=e0i[:, g:g + 1], axis=0),
                            ).then_inc(rows_in[g % 2], 16)

            @block.tensor
            def _(eng):
                eng.wait_ge(dve.sem, plan["heads_r"])
                pe.up(eng.matmul(pb[:, 0:HEADS], t.ones[0:1, :], heads_r[:, :], start=True, stop=True))
                for L, stride, gb, nr, cs, gk in layer_plan():
                    for g in range(gb):
                        eng.wait_ge(dve.sem, plan["diag", L, g])
                        pe.up(eng.matmul(pb[:, 0:P], t.ones[:, :], diag[:, :], start=True, stop=True))
                    for g in range(gk):
                        eng.wait_ge(dve.sem, plan["rdiag", L, g])
                        pe.up(eng.matmul(pb[:, 0:P], t.ones[:, :], diag[:, :], start=True, stop=True))
                    for g in range(gk):
                        eng.wait_ge(dve.sem, plan["rows", L, g])
                        for k in range(2):
                            for j in range(cs // P):
                                mm = eng.transpose(pt[k][:, P * j:P * j + P], rows_f[:, k, P * j:P * j + P],
                                                     t.ident[:, :])
                        pe.up(mm)

            @block.sync
            def _(eng):
                for name in names:
                    eng.dma_start(t.pads[name][0:E].rearrange("(p f) -> p f", p=160),
                                  a[name].rearrange("(p f) -> p f", p=160)).then_inc(arrays_padded, 16)
                eng.dma_start(heads_i[:, :], a["dst"].rearrange("(o e) -> o e", o=1)[:, 0:E:512],
                              allow_slow_non_contiguous=True).then_inc(heads_in, 16)
                eng.wait_ge(dve.sem, plan["pad0"])
                for name in names:
                    k = 0 if name == "dst" else 1
                    eng.dma_start(t.pads[name][E:EPAD].rearrange("(o e) -> o e", o=1),
                                  pad_i[k:k + 1, :]).then_inc(arrays_padded, 16)
                for g in range(G0):
                    eng.wait_ge(dve.sem, plan["lastb", g])
                    for h in range(H):
                        eng.dma_start(t.lastb[P * g:P * g + P, h, :], lastb[:, :]).then_inc(lastb_out, 16)
                    eng.wait_ge(dve.sem, plan["rows_b", g])
                    eng.dma_start(t.rows0[P * g:P * g + P, :], rows_b[:, :, :].rearrange("p k e -> p (k e)")
                                  ).then_inc(rows0_out, 16)
                eng.wait_ge(rows0_out, 16 * G0)
                eng.wait_ge(lastb_out, 64 * G0)
                eng.wait_ge(dve.sem, plan["copied", 1, G1 - 1])
                for k, of in enumerate((src1, row1, keep, win, last)):
                    rows = P if k < 3 else 1
                    eng.dma_start(t.tables1[k][0:rows, :], of[0:rows, :]).then_inc(tables_out, 16)
                eng.wait_ge(tables_out, 16 * 5)


def project_phase(nc, a, t):
    with ExitStack() as ctx:
        s = Scope(nc, ctx, "pr")
        w = s.sb("w", [P, 2, 3 * D])
        brow = s.sb("brow", [P, 3 * D])
        bq8 = s.sb("bq8", [P, D])
        qcol = s.sb("qcol", [P, 2])
        qcol01 = s.sb("qcol01", [P, 2])
        relw = s.sb("relw", [R64, HD])
        rel = s.sb("rel", [R64, HD])
        rrest = s.sb("rrest", [R64, 2, HD])
        x = [s.sb(f"x{i}", [P, D]) for i in range(2)]
        enh = [s.sb(f"enh{i}", [P, 2, P]) for i in range(2)]
        kv = [s.sb(f"kv{i}", [P, 2 * D]) for i in range(2)]
        q = [s.sb(f"q{i}", [P, D]) for i in range(2)]
        rest = [s.sb(f"rest{i}", [P, 2, D]) for i in range(2)]
        q3 = [s.sb(f"q3{i}", [P, 3, D], BF16) for i in range(2)]
        p_t = [s.ps(f"pt{i}", [P, 512]) for i in range(2)]
        p_kv = [s.ps(f"pkv{i}", [P, 512]) for i in range(2)]
        p_q = [s.ps(f"pq{i}", [P, 512]) for i in range(2)]

        w_in = s.sem("w_in")
        x_zero = s.sem("x_zero")
        x_in = [s.sem(f"x_in{i}") for i in range(2)]
        x_turned = s.sem("x_turned")
        enh_done = s.sem("enh_done")
        kv_ps = s.sem("kv_ps")
        q_ps = s.sem("q_ps")
        kv_done = s.sem("kv_done")
        q_done = s.sem("q_done")
        part = s.sem("part")
        rest_done = s.sem("rest_done")
        out_kv = [s.sem(f"out_kv{i}") for i in range(2)]
        out_q3 = [s.sem(f"out_q3{i}") for i in range(2)]
        setup = s.sem("setup")

        def each(eng, body):
            body(0, 0, True, P)
            body(1, 1, True, P)
            with eng.Fori(1, NB // 2) as k:
                body(k * 2, 0, False, P)
                body(k * 2 + 1, 1, False, P)
            body(NB - 1, 0, False, N - (NB - 1) * P)

        assert NB % 2 == 1
        with nc.Block() as block:
            @block.sync
            def _(eng):
                for k in range(2):
                    for j, name in enumerate(("L0_gnn_Wk", "L0_gnn_Wv", "L0_gnn_Wq")):
                        eng.dma_start(w[:, k, D * j:D * j + D], a[name][P * k:P * k + P, :]).then_inc(w_in, 16)
                for j, name in enumerate(("L0_gnn_bk", "L0_gnn_bv", "L0_gnn_bq")):
                    eng.dma_start(brow[:, D * j:D * j + D], a[name].partition_broadcast(P)).then_inc(w_in, 16)
                eng.dma_start(qcol[:, :], a["L0_gnn_query_emb"].rearrange("(k p) -> p k", p=P),
                              allow_slow_non_contiguous=True).then_inc(w_in, 16)
                eng.dma_start(relw[:, :], a["L0_gnn_rel_w"]).then_inc(w_in, 16)

                def load(i, par, first, rows):
                    if rows < P:
                        eng.wait_ge(x_zero, 1)
                    elif not first:
                        eng.wait_ge(x_turned, i - 1)
                    eng.dma_start(x[par][0:rows, :], a["x"][bass.ds(i * P, rows), :]).then_inc(x_in[par], 16)
                each(eng, load)

            @block.tensor
            def _(eng):
                eng.wait_ge(w_in, 16 * 11)

                def tile(i, par, first, rows):
                    eng.wait_ge(x_in[par], (i - par) * 8 + 16)
                    if not first:
                        eng.wait_ge(enh_done, (i - 1) * 2)
                    for k in range(2):
                        mm = eng.transpose(p_t[par][:, P * k:P * k + P], x[par][:, P * k:P * k + P], t.ident[:, :])
                    mm.then_inc(x_turned, 1)
                    eng.wait_ge(enh_done, i * 2 + 2)
                    if not first:
                        eng.wait_ge(kv_done, i - 1)
                        eng.wait_ge(q_done, i - 1)
                    for k in range(2):
                        mm = eng.matmul(p_kv[par][:, :], enh[par][:, k, :], w[:, k, 0:2 * D],
                                        start=(k == 0), stop=(k == 1))
                    mm.then_inc(kv_ps, 1)
                    for k in range(2):
                        mm = eng.matmul(p_q[par][:, 0:D], enh[par][:, k, :], w[:, k, 2 * D:3 * D],
                                        start=(k == 0), stop=(k == 1))
                    mm.then_inc(q_ps, 1)
                each(eng, tile)

            @block.vector
            def _(eng):
                v = nc.vector
                eng.wait_ge(w_in, 16 * 11)
                v.tensor_scalar(qcol01[:, :], qcol[:, :], 0.1, None, ALU.mult).then_inc(setup, 1)
                v.tensor_scalar(bq8[:, :], brow[:, 2 * D:3 * D], 0.125, None, ALU.mult).then_inc(setup, 1)
                v.tensor_scalar(rel[:, :], relw[:, :], 0.2, None, ALU.mult).then_inc(setup, 1)
                eng.wait_ge(setup, 3)
                rest_of, n = rel[:, :], 3
                for j in range(3):
                    for h in range(H):
                        v.tensor_copy(t.rel3[:, j, HD * h:HD * h + HD], rest_of).then_inc(setup, 1)
                        n += 1
                    eng.wait_ge(setup, n)
                    if j < 2:
                        v.tensor_tensor(rrest[:, j, :], rest_of, t.rel3[:, j, 0:HD], ALU.subtract).then_inc(setup, 1)
                        n += 1
                        eng.wait_ge(setup, n)
                        rest_of = rrest[:, j, :]

                def tile(i, par, first, rows):
                    if rows < P:
                        eng.wait_ge(x_turned, i - 1)
                        v.memset(x[par][:, :], 0.0).then_inc(x_zero, 1)
                    eng.wait_ge(x_turned, i + 1)
                    if not first:
                        eng.wait_ge(q_ps, i - 1)
                    for k in range(2):
                        v.tensor_scalar(enh[par][:, k, :], p_t[par][:, P * k:P * k + P], qcol01[:, k:k + 1], None,
                                        ALU.add).then_inc(enh_done, 1)
                    eng.wait_ge(kv_ps, i + 1)
                    if not first:
                        eng.wait_ge(out_kv[par], (i - par) * 8)
                    v.tensor_tensor(kv[par][:, :], p_kv[par][:, :], brow[:, 0:2 * D], ALU.add).then_inc(kv_done, 1)
                    eng.wait_ge(q_ps, i + 1)
                    if not first:
                        eng.wait_ge(part, (i - 1) * 3)
                        eng.wait_ge(rest_done, (i - 1) * 2)
                    v.scalar_tensor_tensor(q[par][:, :], p_q[par][:, 0:D], 0.125, bq8[:, :], ALU.mult,
                                           ALU.add).then_inc(q_done, 1)
                each(eng, tile)

            @block.scalar
            def _(eng):

                def tile(i, par, first, rows):
                    for j in range(3):
                        if j == 0:
                            eng.wait_ge(q_done, i + 1)
                            if not first:
                                eng.wait_ge(out_q3[par], (i - par) * 8)
                            of = q[par][:, :]
                        else:
                            eng.wait_ge(rest_done, i * 2 + j)
                            of = rest[par][:, j - 1, :]
                        nc.scalar.activation(q3[par][:, j, :], of, ACT.Copy).then_inc(part, 1)
                    eng.wait_ge(part, i * 3 + 3)
                    eng.dma_start(t.q3[bass.ds(i * P, P), :], q3[par][:, :, :].rearrange("p a b -> p (a b)")
                                  ).then_inc(out_q3[par], 16)
                    eng.wait_ge(kv_done, i + 1)
                    eng.dma_start(t.kv[bass.ds(i * P, P), :], kv[par][:, :]).then_inc(out_kv[par], 16)
                each(eng, tile)
                for par in range(2):
                    eng.wait_ge(out_q3[par], 16 * ((NB + 1 - par) // 2))
                    eng.wait_ge(out_kv[par], 16 * ((NB + 1 - par) // 2))

            @block.gpsimd
            def _(eng):

                def tile(i, par, first, rows):
                    for j in range(2):
                        of = q[par][:, :] if j == 0 else rest[par][:, 0, :]
                        eng.wait_ge(part, i * 3 + j + 1)
                        nc.gpsimd.tensor_tensor(rest[par][:, j, :], of, q3[par][:, j, :],
                                                ALU.subtract).then_inc(rest_done, 1)
                each(eng, tile)


def attend_phase(nc, a, t):
    with ExitStack() as ctx:
        s = Scope(nc, ctx, "at")
        T = 4 * SUP
        M = SUP * H
        VW = H * (HD + 1)
        AHEAD, PREP, SUM, MERGE = 3, 5, 6, 7
        kv = [s.sb(f"kv{i}", [P, T, 2 * D]) for i in range(2)]
        idx = [s.sb(f"idx{i}", [P, T], I32) for i in range(2)]
        hot = [s.sb(f"hot{i}", [P, SUP, 2 * C0], BF16) for i in range(2)]
        q3 = [s.sb(f"q3{i}", [P, 3, D], BF16) for i in range(SUP)]
        kr = s.sb("kr", [P, 4, D])
        sc = [s.sb(f"sc{i}", [P, 4, SUP, H]) for i in range(2)]
        lastb = [s.sb(f"lastb{i}", [M, 514]) for i in range(2)]
        fmax = s.sb("fmax", [M, 512])
        smax = s.sb("smax", [M, 512])
        ex = s.sb("ex", [M, 512])
        lmax = s.sb("lmax", [M, 512])
        wgt = s.sb("wgt", [P, 2, 4, SUP, H])
        vs = [s.sb(f"vs{i}", [P, 4, VW + H]) for i in range(2)]
        eh = [s.sb(f"eh{i}", [P, 4, P]) for i in range(2)]
        fresh = [s.sb(f"fresh{i}", [P, SUP]) for i in range(2)]
        absent = s.sb("absent", [P, H])
        cmax = s.sb("cmax", [P, H])
        top = [s.sb(f"top{i}", [P, H]) for i in range(SUP)]
        dmax = [s.sb(f"dmax{i}", [P, 2, H]) for i in range(2)]
        fac = [s.sb(f"fac{i}", [P, 2, H]) for i in range(2)]
        add = [s.sb(f"add{i}", [P, VW]) for i in range(2)]
        old = s.sb("old", [P, VW])
        acc = [s.sb(f"acc{i}", [P, VW]) for i in range(SUP)]
        p_q = [s.ps(f"p_q{i}", [P, 512]) for i in range(2)]
        p_r = [s.ps(f"p_r{i}", [P, 512]) for i in range(2)]
        p_x = s.ps("p_x", [P, 512])
        p_w = s.ps("p_w", [P, 512])
        p_s = [s.ps(f"p_s{i}", [P, 512]) for i in range(2)]

        kv_in = [[s.sem(f"kv_in{i}{c}") for c in range(SUP)] for i in range(2)]
        idx_set = s.sem("idx_set")
        pool_on = s.sem("pool_on")
        pe_on = s.sem("pe_on")
        q3_in = [s.sem(f"q3_in{c}") for c in range(SUP)]
        hot_in = [s.sem(f"hot_in{i}") for i in range(2)]
        lastb_in = [s.sem(f"lastb_in{i}") for i in range(2)]
        cleared = s.sem("cleared")
        hot_done = s.sem("hot_done")
        r_ps = s.sem("r_ps")
        q_ps = s.sem("q_ps")
        kr_sum = s.sem("kr_sum")
        kr_prod = s.sem("kr_prod")
        scored = s.sem("scored")
        sc_turned = s.sem("sc_turned")
        fwd = s.sem("fwd")
        bwd = s.sem("bwd")
        over = s.sem("over")
        lmax_done = s.sem("lmax_done")
        ex_done = s.sem("ex_done")
        w_turned = s.sem("w_turned")
        wgt_done = s.sem("wgt_done")
        eh_done = s.sem("eh_done")
        vs_w = s.sem("vs_w")
        vs_v = s.sem("vs_v")
        summed = s.sem("summed")
        fresh_in = s.sem("fresh_in")
        marked = s.sem("marked")
        cmax_done = s.sem("cmax_done")
        top_done = s.sem("top_done")
        dmax_done = s.sem("dmax_done")
        fac_done = s.sem("fac_done")
        add_done = s.sem("add_done")
        old_done = s.sem("old_done")
        acc_done = s.sem("acc_done")
        stored = [s.sem(f"stored{i}") for i in range(SUP)]

        def run(eng, body):
            for n in range(4):
                body(n, n % 2)
            with eng.Fori(2, NSUP // 2 - 1) as k:
                body(k * 2, 0)
                body(k * 2 + 1, 1)
            for n in range(NSUP - 2, NSUP + 2):
                body(n, n % 2)

        assert NSUP % 2 == 0

        def chunk(n, par, p, lag):
            return n * SUP + (p - lag), (p - lag) % SUP, n + (p - lag) // SUP, (par + (p - lag) // SUP) % 2

        def exists(i):
            return not isinstance(i, int) or 0 <= i < K0

        with nc.Block() as block:
            @block.gpsimd
            def _(eng):

                def gather(g, c, n, par):
                    if c == 0:
                        if past(n, 2):
                            eng.wait_ge(kv_in[par][SUP - 1], (n - par) * 32)
                        nc.gpsimd.tensor_copy(idx[par][:, :], t.src0[:, bass.ds(n * T, T)]).then_inc(idx_set, 1)
                        eng.wait_ge(idx_set, n + 1)
                        eng.sem_inc(pool_on, 1)
                    if past(n, 2):
                        eng.wait_ge(vs_v, g - 2 * SUP + 1)
                        eng.sem_inc(pool_on, 1)
                    for j in range(4):
                        eng.indirect_dma_start(
                            out=kv[par][:, 4 * c + j, :], out_offset=None, in_=t.kv,
                            in_offset=bass.IndirectOffsetOnAxis(ap=idx[par][:, 4 * c + j:4 * c + j + 1], axis=0),
                        ).then_inc(kv_in[par][c], 16)

                def merge(i, c, n):
                    eng.wait_ge(fac_done, i + 1)
                    if past(i, 1):
                        eng.wait_ge(acc_done, i)
                    nc.gpsimd.tensor_tensor(old[:, :].rearrange("p (h e) -> p h e", h=H),
                                            acc[c - 1][:, :].rearrange("p (h e) -> p h e", h=H),
                                            fac[c % 2][:, 0, :].unsqueeze(2).to_broadcast([P, H, HD + 1]),
                                            ALU.mult).then_inc(old_done, 1)
                    eng.wait_ge(old_done, i + 1)
                    eng.wait_ge(add_done, i + 1)
                    if past(n, 1):
                        eng.wait_ge(stored[c], n * 16)
                    nc.gpsimd.tensor_tensor(acc[c][:, :], old[:, :], add[c % 2][:, :], ALU.add).then_inc(acc_done, 1)

                def positions(n, par):
                    for p in range(SUP):
                        g, c, m, mpar = chunk(n, par, p, -AHEAD)
                        if exists(g):
                            gather(g, c, m, mpar)
                        i, c, m, _ = chunk(n, par, p, MERGE)
                        if exists(i):
                            merge(i, c, m)

                eng.wait_ge(cleared, 2)
                for c in range(AHEAD):
                    gather(c, c, 0, 0)
                run(eng, positions)

            @block.sync
            def _(eng):

                def load_hot(n, par):
                    eng.dma_start(hot[par][:, :, :].rearrange("p c e -> p (c e)"),
                                  t.rows0[bass.ds(n * SUP, SUP), :].rearrange("c e -> (c e)").partition_broadcast(P)
                                  ).then_inc(hot_in[par], 16)

                def load_lastb(n, par):
                    eng.dma_start(lastb[par][:, :], t.lastb[bass.ds(n * SUP, SUP), :, :].rearrange("c h e -> (c h) e")
                                  ).then_inc(lastb_in[par], 16)

                def load_q3(n, c):
                    b = eng.value_load(t.blk[0:1, bass.ds(n * SUP + c, 1)], min_val=0, max_val=NB - 1)
                    eng.dma_start(q3[c][:, :, :].rearrange("p a b -> p (a b)"), t.q3[bass.ds(b * P, P), :]
                                  ).then_inc(q3_in[c], 16)

                def store(i, c):
                    b = eng.value_load(t.blk[0:1, bass.ds(i, 1)], min_val=0, max_val=NB - 1)
                    z = eng.value_load(t.last0[0:1, bass.ds(i, 1)], min_val=0, max_val=1)
                    eng.wait_ge(acc_done, i + 1)
                    eng.dma_start(t.sums0[bass.ds(b * P, P), :], acc[c][:, :], cond=z).then_inc(stored[c], 16)

                def positions(n, par):
                    more = exists(n * SUP + SUP)
                    for p in range(SUP):
                        if p == 0 and more:
                            if past(n, 1):
                                eng.wait_ge(q_ps, n * 2 * SUP)
                            load_hot(n + 1, 1 - par)
                        if p == 1 and more:
                            if past(n, 1):
                                eng.wait_ge(lmax_done, n)
                            load_lastb(n + 1, 1 - par)
                        if more:
                            eng.wait_ge(q_ps, (n * SUP + p + 1) * 2)
                            load_q3(n + 1, p)
                        i, c, _, _ = chunk(n, par, p, MERGE + 1)
                        if exists(i):
                            store(i, c)

                load_hot(0, 0)
                load_lastb(0, 0)
                for c in range(SUP):
                    load_q3(0, c)
                run(eng, positions)
                for c in range(SUP):
                    eng.wait_ge(stored[c], NSUP * 16)

            @block.tensor
            def _(eng):

                def expand(g, c, n, par):
                    eng.wait_ge(hot_done, g + 1)
                    for half in range(2):
                        if past(g, 1):
                            eng.wait_ge(kr_sum, g * 2 + half - 1)
                        for j in range(2):
                            for m in range(3):
                                k = P * (2 * half + j)
                                mm = eng.matmul(p_r[half][:, D * j:D * j + D], hot[par][0:R64, c, C0 + k:C0 + k + P],
                                                t.rel3[:, m, :], start=(m == 0), stop=(m == 2))
                        mm.then_inc(r_ps, 1)
                        if half == 0:
                            eng.wait_ge(q3_in[c], n * 16 + 16)
                        if past(g, 1):
                            eng.wait_ge(kr_prod, g * 2 + half - 1)
                        for j in range(2):
                            for m in range(3):
                                k = P * (2 * half + j)
                                mm = eng.matmul(p_q[half][:, D * j:D * j + D], hot[par][:, c, k:k + P],
                                                q3[c][:, m, :], start=(m == 0), stop=(m == 2))
                        mm.then_inc(q_ps, 1)

                def turn_scores(u, par):
                    eng.wait_ge(scored, u * SUP + SUP)
                    if past(u, 1):
                        eng.wait_ge(lmax_done, u)
                    for j in range(4):
                        mm = eng.transpose(p_x[0:M, P * j:P * j + P],
                                           sc[par][:, j, :, :].rearrange("p c h -> p (c h)"), t.ident[:, :])
                    mm.then_inc(sc_turned, 1)

                def turn_weights(u):
                    eng.wait_ge(ex_done, u + 1)
                    eng.wait_ge(lmax_done, u + 1)
                    if past(u, 1):
                        eng.wait_ge(wgt_done, u)
                    eng.sem_inc(pe_on, 1)
                    for k, of in enumerate((ex, lmax)):
                        for j in range(4):
                            o = (4 * k + j) * M
                            mm = eng.transpose(p_w[:, o:o + M], of[:, P * j:P * j + P], t.ident[0:M, 0:M])
                    mm.then_inc(w_turned, 1)

                def sum_up(i, c):
                    eng.wait_ge(vs_v, i + 1)
                    eng.wait_ge(vs_w, i * 2 + 2)
                    eng.wait_ge(eh_done, i + 1)
                    if past(i, 2):
                        eng.wait_ge(add_done, i - 1)
                    for j in range(4):
                        mm = eng.matmul(p_s[c % 2][:, 0:VW + H], eh[c % 2][:, j, :], vs[c % 2][:, j, :],
                                        start=(j == 0), stop=(j == 3))
                    mm.then_inc(summed, 1)

                def positions(n, par):
                    u, softmax = n - 1, exists((n - 1) * SUP)
                    for p in range(SUP):
                        g = n * SUP + p
                        if exists(g):
                            expand(g, p, n, par)
                        if p == 0 and softmax:
                            turn_scores(u, 1 - par)
                        i, c, _, _ = chunk(n, par, p, SUM)
                        if exists(i):
                            sum_up(i, c)
                        if p == 1 and softmax:
                            turn_weights(u)
                run(eng, positions)

            @block.scalar
            def _(eng):
                act = nc.scalar.activation

                def expo(u):
                    eng.wait_ge(over, u + 1)
                    act(ex[:, :], ex[:, :], ACT.Exp).then_inc(ex_done, 1)

                def scale_v(i, c, n, par):
                    eng.wait_ge(wgt_done, n + 1)
                    if past(i, 2):
                        eng.wait_ge(summed, i - 1)
                    for j in range(4):
                        for h in range(H):
                            ins = act(vs[c % 2][:, j, 65 * h:65 * h + HD],
                                      kv[par][:, 4 * c + j, D + HD * h:D + HD * h + HD],
                                      ACT.Copy, scale=wgt[:, 0, j, c, h:h + 1])
                    ins.then_inc(vs_v, 1)

                def rescale(i, c):
                    b = c % 2
                    eng.wait_ge(dmax_done, i * 2 + 2)
                    if past(i, 2):
                        eng.wait_ge(acc_done, i - 1)
                    act(fac[b][:, :, :], dmax[b][:, :, :], ACT.Exp).then_inc(fac_done, 1)
                    eng.wait_ge(fac_done, i + 1)
                    for h in range(H):
                        ins = act(add[b][:, 65 * h:65 * h + 65], p_s[b][:, 65 * h:65 * h + 65], ACT.Copy,
                                  scale=fac[b][:, 1, h:h + 1])
                    ins.then_inc(add_done, 1)

                def positions(n, par):
                    for p in range(SUP):
                        prep, merge = chunk(n, par, p, PREP), chunk(n, par, p, MERGE)
                        if p != 1 and exists(prep[0]):
                            scale_v(*prep)
                        if exists(merge[0]):
                            rescale(*merge[:2])
                        if p == 1 and exists(prep[0]):
                            scale_v(*prep)
                        if p == 0 and exists((n - 1) * SUP):
                            expo(n - 1)
                run(eng, positions)

            @block.vector
            def _(eng):
                v = nc.vector

                def one_hots(g, c, n, par):
                    if c == 0:
                        eng.wait_ge(hot_in[par], (n - par) * 8 + 16)
                    v.tensor_scalar(hot[par][:, c, :], hot[par][:, c, :], t.col[:, 0:1], None,
                                    ALU.is_equal).then_inc(hot_done, 1)

                def add_relation(g, c, n, par, half):
                    if half == 0:
                        eng.wait_ge(kv_in[par][c], (n - par) * 32 + 64)
                        if past(g, 1):
                            eng.wait_ge(scored, g)
                    eng.wait_ge(r_ps, g * 2 + half + 1)
                    v.tensor_tensor(kr[:, 2 * half:2 * half + 2, :],
                                    kv[par][:, 4 * c + 2 * half:4 * c + 2 * half + 2, 0:D],
                                    p_r[half][:, :].rearrange("p (j d) -> p j d", j=2), ALU.add).then_inc(kr_sum, 1)

                def times_query(g, half):
                    o = kr[:, 2 * half:2 * half + 2, :]
                    eng.wait_ge(kr_sum, g * 2 + half + 1)
                    eng.wait_ge(q_ps, g * 2 + half + 1)
                    v.tensor_tensor(o, o, p_q[half][:, :].rearrange("p (j d) -> p j d", j=2),
                                    ALU.mult).then_inc(kr_prod, 1)

                def by_head(g, c, n, par):
                    eng.wait_ge(kr_prod, g * 2 + 2)
                    if past(n, 2):
                        eng.wait_ge(sc_turned, n - 1)
                    v.tensor_reduce(sc[par][:, :, c, :], kr[:, :, :].rearrange("p j (h d) -> p j h d", h=H),
                                    AXX, ALU.add).then_inc(scored, 1)

                def scan_forwards(u, par):
                    eng.wait_ge(lastb_in[par], (u - par) * 8 + 16)
                    eng.wait_ge(sc_turned, u + 1)
                    v.tensor_tensor_scan(fmax[:, :], lastb[par][:, 0:512], p_x[0:M, :], -BIG, ALU.add,
                                         ALU.max).then_inc(fwd, 1)

                def scan_backwards(u, par):
                    eng.wait_ge(fwd, u + 1)
                    if past(u, 1):
                        eng.wait_ge(w_turned, u)
                    v.tensor_tensor_scan(smax[:, ::-1], lastb[par][:, 1:513][:, ::-1], fmax[:, ::-1], -BIG,
                                         ALU.add, ALU.max).then_inc(bwd, 1)

                def take_off_maximum(u, par):
                    eng.wait_ge(bwd, u + 1)
                    v.tensor_tensor(ex[:, :], p_x[0:M, :], smax[:, :], ALU.subtract).then_inc(over, 1)
                    v.scalar_tensor_tensor(lmax[:, :], lastb[par][:, 1:513], -1.0 / BIG, smax[:, :], ALU.mult,
                                           ALU.mult).then_inc(lmax_done, 1)

                def weights(u):
                    eng.wait_ge(w_turned, u + 1)
                    if past(u, 1):
                        eng.wait_ge(vs_v, u * SUP)
                        eng.wait_ge(vs_w, u * 2 * SUP)
                    v.tensor_copy(wgt[:, :, :, :, :].rearrange("p k j c h -> p (k j c h)"),
                                  p_w[:, 0:8 * M]).then_inc(wgt_done, 1)

                def edge_one_hots(i, c):
                    if past(i, 2):
                        eng.wait_ge(summed, i - 1)
                    v.tensor_tensor(eh[c % 2][:, :, :], t.iota[:, :].unsqueeze(1).to_broadcast([P, 4, P]),
                                    t.node0[:, bass.ds(i * 4, 4)].unsqueeze(2).to_broadcast([P, 4, P]),
                                    ALU.is_equal).then_inc(eh_done, 1)

                def place(i, c, n):
                    eng.wait_ge(wgt_done, n + 1)
                    if past(i, 2):
                        eng.wait_ge(summed, i - 1)
                    o = vs[c % 2]
                    v.tensor_copy(o[:, :, 0:VW].rearrange("p j (h e) -> p j h e", h=H)[:, :, :, HD],
                                  wgt[:, 0, :, c, :]).then_inc(vs_w, 1)
                    v.tensor_copy(o[:, :, VW:VW + H], wgt[:, 1, :, c, :]).then_inc(vs_w, 1)

                def new_max(i, c, n, par, step):
                    b = c % 2
                    f = fresh[par][:, c:c + 1]
                    if step == 0:
                        if c == 0:
                            v.tensor_copy(fresh[par][:, :], t.fresh0[:, bass.ds(i, SUP)]).then_inc(fresh_in, 1)
                        eng.wait_ge(summed, i + 1)
                        if past(i, 1):
                            eng.wait_ge(cmax_done, i)
                        den = p_s[b][:, 0:VW].rearrange("p (h e) -> p h e", h=H)[:, :, HD]
                        v.tensor_scalar(absent[:, :], den, 0.5, -BIG, ALU.is_lt, ALU.mult).then_inc(marked, 1)
                    elif step == 1:
                        eng.wait_ge(marked, i + 1)
                        if past(i, 1):
                            eng.wait_ge(dmax_done, i * 2)
                        v.tensor_tensor(cmax[:, :], absent[:, :], p_s[b][:, VW:VW + H], ALU.add).then_inc(cmax_done, 1)
                    elif step == 2:
                        eng.wait_ge(cmax_done, i + 1)
                        eng.wait_ge(fresh_in, n + 1)
                        v.scalar_tensor_tensor(top[c][:, :], top[c - 1][:, :], f, cmax[:, :], ALU.add,
                                               ALU.max).then_inc(top_done, 1)
                    else:
                        eng.wait_ge(top_done, i + 1)
                        if past(i, 2):
                            eng.wait_ge(fac_done, i - 1)
                        v.scalar_tensor_tensor(dmax[b][:, 0, :], top[c - 1][:, :], f, top[c][:, :], ALU.add,
                                               ALU.subtract).then_inc(dmax_done, 1)
                        v.tensor_tensor(dmax[b][:, 1, :], cmax[:, :], top[c][:, :], ALU.subtract).then_inc(dmax_done, 1)

                def positions(n, par):
                    u, softmax = n - 1, exists((n - 1) * SUP)
                    for p in range(SUP):
                        g = n * SUP + p
                        merge, prep = chunk(n, par, p, MERGE), chunk(n, par, p, PREP)
                        score, merging, preparing = exists(g), exists(merge[0]), exists(prep[0])
                        after = chunk(n, par, p, -1)
                        if exists(after[0]):
                            one_hots(*after)
                        if score:
                            add_relation(g, p, n, par, 0)
                        if merging:
                            new_max(*merge, 0)
                        if score:
                            add_relation(g, p, n, par, 1)
                        if merging:
                            new_max(*merge, 1)
                        if score:
                            times_query(g, 0)
                        if merging:
                            new_max(*merge, 2)
                        if score:
                            times_query(g, 1)
                        if merging:
                            new_max(*merge, 3)
                        if p == 0 and preparing:
                            place(*prep[:3])
                        if score:
                            by_head(g, p, n, par)
                        if p == 0 and softmax:
                            scan_forwards(u, 1 - par)
                        if preparing:
                            edge_one_hots(*prep[:2])
                        if p == 0 and softmax:
                            scan_backwards(u, 1 - par)
                            take_off_maximum(u, 1 - par)
                        if p == 1 and softmax:
                            weights(u)
                        if p != 0 and preparing:
                            place(*prep[:3])

                v.memset(acc[SUP - 1][:, :], 0.0).then_inc(cleared, 1)
                v.memset(top[SUP - 1][:, :], 0.0).then_inc(cleared, 1)
                eng.wait_ge(cleared, 2)
                one_hots(0, 0, 0, 0)
                run(eng, positions)


def update_phase(nc, a, t):
    with ExitStack() as ctx:
        s = Scope(nc, ctx, "up")
        wo = s.sb("wo", [P, 2, D])
        gamma, beta, bo = (s.sb(n, [P, D]) for n in ("gamma", "beta", "bo"))
        eps = s.sb("eps", [P, 1])
        zero = s.sb("zero", [P, D])
        x = [s.sb(f"x{i}", [P, D]) for i in range(2)]
        vown = [s.sb(f"vown{i}", [P, D]) for i in range(2)]
        sums = [s.sb(f"sums{i}", [P, H * (HD + 1)]) for i in range(2)]
        xb = [s.sb(f"xb{i}", [P, D]) for i in range(2)]
        none = s.sb("none", [P, H])
        den = s.sb("den", [P, H])
        rden = s.sb("rden", [P, H])
        own = s.sb("own", [P, D])
        mean = s.sb("mean", [P, D])
        msg = s.sb("msg", [P, D])
        msg_t = [s.sb(f"msg_t{i}", [P, 2, P]) for i in range(2)]
        z = s.sb("z", [P, D])
        stats = s.sb("stats", [P, 2, 6])
        mv = s.sb("mv", [P, 2, 2])
        dev = s.sb("dev", [P, 2])
        rdev = s.sb("rdev", [P, 2])
        y = s.sb("y", [P, D])
        yg = s.sb("yg", [P, D])
        yb = s.sb("yb", [P, D])
        z2 = s.sb("z2", [P, D])
        x1 = [s.sb(f"x1{i}", [P, D]) for i in range(2)]
        p_t = [s.ps(f"pt{i}", [P, 512]) for i in range(2)]
        p_o = [s.ps(f"po{i}", [P, 512]) for i in range(2)]

        w_in = s.sem("w_in")
        x_zero = s.sem("x_zero")
        x_in = [s.sem(f"x_in{i}") for i in range(2)]
        xb_done = s.sem("xb_done")
        step = s.sem("step")
        turned = s.sem("turned")
        msg_t_done = s.sem("msg_t_done")
        out_ps = s.sem("out_ps")
        dev_done = s.sem("dev_done")
        dve_on = s.sem("dve_on")
        x1_out = [s.sem(f"x1_out{i}") for i in range(2)]
        pad_out = s.sem("pad_out")
        STEPS = 21
        MSG, Z, VAR1, VAR2, X1 = 7, 8, 10, 18, 20

        def each(eng, body):
            body(0, 0, True, P)
            body(1, 1, True, P)
            with eng.Fori(1, NB // 2) as k:
                body(k * 2, 0, False, P)
                body(k * 2 + 1, 1, False, P)
            body(NB - 1, 0, False, N - (NB - 1) * P)

        with nc.Block() as block:
            @block.sync
            def _(eng):
                eng.dma_start(wo[:, :, :], a["L0_gnn_Wo"].rearrange("(k p) n -> p k n", p=P)).then_inc(w_in, 16)
                for dst, name in ((gamma, "gamma"), (beta, "beta"), (bo, "bo")):
                    eng.dma_start(dst[:, :], a[f"L0_gnn_{name}"].partition_broadcast(P)).then_inc(w_in, 16)

                def load(i, par, first, rows):
                    if rows < P:
                        eng.wait_ge(x_zero, 3)
                    elif not first:
                        eng.wait_ge(step, (i - 1) * STEPS)
                        eng.wait_ge(xb_done, i - 1)
                    eng.dma_start(x[par][0:rows, :], a["x"][bass.ds(i * P, rows), :]).then_inc(x_in[par], 16)
                    eng.dma_start(sums[par][:, :], t.sums0[bass.ds(i * P, P), :]).then_inc(x_in[par], 16)
                    eng.dma_start(vown[par][:, :], t.kv[bass.ds(i * P, P), D:2 * D]).then_inc(x_in[par], 16)
                each(eng, load)

            @block.gpsimd
            def _(eng):
                eng.wait_ge(w_in, 64)

                def tile(i, par, first, rows):
                    eng.wait_ge(x_in[par], (i - par) * 24 + 48)
                    if not first:
                        eng.wait_ge(step, (i - 2) * STEPS + Z)
                    nc.gpsimd.tensor_tensor(xb[par][:, :], x[par][:, :], bo[:, :], ALU.add).then_inc(xb_done, 1)
                each(eng, tile)

            @block.tensor
            def _(eng):
                def tile(i, par, first, rows):
                    eng.wait_ge(step, i * STEPS + MSG)
                    if not first:
                        eng.wait_ge(msg_t_done, (i - 1) * 2)
                    for k in range(2):
                        mm = eng.transpose(p_t[par][:, P * k:P * k + P], msg[:, P * k:P * k + P], t.ident[:, :])
                    mm.then_inc(turned, 1)
                    eng.wait_ge(msg_t_done, i * 2 + 2)
                    if not first:
                        eng.wait_ge(step, (i - 2) * STEPS + Z)
                    for k in range(2):
                        mm = eng.matmul(p_o[par][:, 0:D], msg_t[par][:, k, :], wo[:, k, :],
                                        start=(k == 0), stop=(k == 1))
                    mm.then_inc(out_ps, 1)
                eng.wait_ge(w_in, 64)
                each(eng, tile)

            @block.scalar
            def _(eng):
                act = nc.scalar.activation

                def tile(i, par, first, rows):
                    eng.wait_ge(turned, i + 1)
                    if not first:
                        eng.wait_ge(out_ps, i - 1)
                    for k in range(2):
                        act(msg_t[par][:, k, :], p_t[par][:, P * k:P * k + P], ACT.Copy).then_inc(msg_t_done, 1)
                    for m, var in enumerate((VAR1, VAR2)):
                        eng.wait_ge(step, i * STEPS + var)
                        act(dev[:, m:m + 1], mv[:, m, 1:2], ACT.Sqrt, bias=eps[:, 0:1]).then_inc(dev_done, 1)
                    eng.wait_ge(step, i * STEPS + X1 + 1)
                    eng.dma_start(t.x1[bass.ds(i * P, P), :], x1[par][:, :]).then_inc(x1_out[par], 16)
                eng.wait_ge(x_zero, 2)
                each(eng, tile)
                eng.dma_start(t.x1[NB * P:NW * WN, :], zero[0:NW * WN - NB * P, :]).then_inc(pad_out, 16)
                for par in range(2):
                    eng.wait_ge(x1_out[par], 16 * ((NB + 1 - par) // 2))
                eng.wait_ge(pad_out, 16)

            @block.vector
            def _(eng):
                v = nc.vector

                def tile(i, par, first, rows):
                    n = [0]

                    def link(ins):
                        n[0] += 1
                        ins.then_inc(step, 1)
                        eng.wait_ge(step, i * STEPS + n[0])

                    if rows < P:
                        eng.wait_ge(xb_done, i - 1)
                        v.memset(x[par][:, :], 0.0).then_inc(x_zero, 1)
                    eng.wait_ge(x_in[par], (i - par) * 24 + 48)
                    if not first:
                        eng.wait_ge(turned, i)
                    by_head = sums[par][:, :].rearrange("p (h e) -> p h e", h=H)
                    link(v.tensor_scalar(none[:, :], by_head[:, :, HD], 0.5, None, ALU.is_lt))
                    link(v.tensor_tensor(den[:, :], by_head[:, :, HD], none[:, :], ALU.add))
                    link(v.reciprocal(rden[:, :], den[:, :]))
                    link(v.tensor_tensor(mean[:, :].rearrange("p (h d) -> p h d", h=H), by_head[:, :, 0:HD],
                                         rden[:, :].unsqueeze(2).to_broadcast([P, H, HD]), ALU.mult))
                    link(v.tensor_scalar(own[:, :], vown[par][:, :], none[:, 0:1], None, ALU.mult))
                    link(v.tensor_copy(rdev[:, 0:1], none[:, 0:1]))
                    link(v.tensor_tensor(msg[:, :], mean[:, :], own[:, :], ALU.add))
                    assert n[0] == MSG
                    eng.wait_ge(out_ps, i + 1)
                    eng.wait_ge(xb_done, i + 1)
                    link(v.tensor_tensor(z[:, :], p_o[par][:, 0:D], xb[par][:, :], ALU.add))
                    link(v.bn_stats(stats[:, 0, :], z[:, :]))
                    eng.sem_inc(dve_on, 1)
                    link(v.bn_aggr(mv[:, 0, :], stats[:, 0, :]))
                    assert n[0] == VAR1
                    eng.wait_ge(dev_done, i * 2 + 1)
                    link(v.reciprocal(rdev[:, 0:1], dev[:, 0:1]))
                    link(v.tensor_scalar(y[:, :], z[:, :], mv[:, 0, 0:1], rdev[:, 0:1], ALU.subtract, ALU.mult))
                    link(v.tensor_tensor(yg[:, :], y[:, :], gamma[:, :], ALU.mult))
                    link(v.tensor_tensor(yb[:, :], yg[:, :], beta[:, :], ALU.add))
                    link(v.tensor_tensor(z2[:, :], yb[:, :], x[par][:, :], ALU.add))
                    link(v.bn_stats(stats[:, 1, :], z2[:, :]))
                    link(v.tensor_copy(rdev[:, 1:2], rdev[:, 0:1]))
                    eng.sem_inc(dve_on, 1)
                    link(v.bn_aggr(mv[:, 1, :], stats[:, 1, :]))
                    assert n[0] == VAR2
                    eng.wait_ge(dev_done, i * 2 + 2)
                    link(v.reciprocal(rdev[:, 1:2], dev[:, 1:2]))
                    if not first:
                        eng.wait_ge(x1_out[par], (i - par) * 8)
                    link(v.tensor_scalar(x1[par][:, :], z2[:, :], mv[:, 1, 0:1], rdev[:, 1:2], ALU.subtract,
                                         ALU.mult))
                    assert n[0] == X1
                    link(v.tensor_copy(rdev[:, 0:1], rdev[:, 1:2]))
                    assert n[0] == STEPS

                v.memset(eps[:, :], EPS).then_inc(x_zero, 1)
                v.memset(zero[:, :], 0.0).then_inc(x_zero, 1)
                eng.wait_ge(w_in, 64)
                each(eng, tile)


def relate_phase(nc, a, t):
    with ExitStack() as ctx:
        s = Scope(nc, ctx, "re")
        GS = 8
        R = 3
        WA = 2 * WR + WR
        src = s.sb("src", [P, G1 * P], I32)
        row = s.sb("row", [P, G1 * P])
        keep = s.sb("keep", [P, G1 * P])
        win = s.sb("win", [1, G1 * P], I32)
        last = s.sb("last", [1, G1 * P], I32)
        idx = [s.sb(f"idx{i}", [P, GS], I32) for i in range(R)]
        kp = [s.sb(f"kp{i}", [P, GS]) for i in range(R)]
        xg = [s.sb(f"xg{i}", [P, GS, D]) for i in range(R)]
        oh = [s.sb(f"oh{i}", [P, GS, WR]) for i in range(R)]
        acc = [s.sb(f"acc{i}", [P, WA]) for i in range(GS)]
        p_a = [s.ps(f"pa{i}", [P, 512]) for i in range(4)]

        tables_in = s.sem("tables_in")
        idx_set = s.sem("idx_set")
        pool_on = s.sem("pool_on")
        x_in = [[s.sem(f"x_in{i}{g}") for g in range(2)] for i in range(R)]
        hot = s.sem("hot")
        kept = s.sem("kept")
        summed = s.sem("summed")
        acc_done = s.sem("acc_done")
        stored = [s.sem(f"stored{i}") for i in range(GS)]
        acc_zero = s.sem("acc_zero")

        def each(eng, body):
            for j in range(R):
                body(j, j, 0, True)
            with eng.Fori(1, K1 // GS // R) as k:
                for j in range(R):
                    body(k * R + j, j, k, False)
        assert K1 % (GS * R) == 0

        def store(eng, n, odd):
            for g in range(odd, GS, 2):
                w = eng.value_load(win[0:1, bass.ds(n * GS + g, 1)], min_val=0, max_val=NW - 1)
                z = eng.value_load(last[0:1, bass.ds(n * GS + g, 1)], min_val=0, max_val=1)
                eng.wait_ge(acc_done, n * GS + g + 1)
                eng.dma_start(t.agg[bass.ds(w * P, P), :], acc[g][:, :], cond=z).then_inc(stored[g], 16)

        with nc.Block() as block:
            @block.gpsimd
            def _(eng):
                def gather(n, par, k, first):
                    if not first:
                        eng.wait_ge(x_in[par][1], k * 64)
                    nc.gpsimd.tensor_copy(idx[par][:, :], src[:, bass.ds(n * GS, GS)]).then_inc(idx_set, 1)
                    eng.wait_ge(idx_set, n + 1)
                    eng.sem_inc(pool_on, 1)
                    for g in range(GS):
                        if g % 4 == 0 and not first:
                            eng.wait_ge(summed, (n - R) * GS + g + 4)
                            eng.sem_inc(pool_on, 1)
                        eng.indirect_dma_start(
                            out=xg[par][:, g, :], out_offset=None, in_=t.x1,
                            in_offset=bass.IndirectOffsetOnAxis(ap=idx[par][:, g:g + 1], axis=0),
                        ).then_inc(x_in[par][g // 4], 16)
                eng.wait_ge(tables_in, 16 * 5)
                each(eng, gather)

            @block.tensor
            def _(eng):
                def sums(n, par, k, first):
                    eng.wait_ge(hot, n + 1)
                    for g in range(GS):
                        i = n * GS + g
                        if g % 4 == 0:
                            eng.wait_ge(x_in[par][g // 4], k * 64 + 64)
                        if not (first and par == 0 and g < 4):
                            eng.wait_ge(acc_done, i - 3)
                        o = p_a[g % 4]
                        for half in range(2):
                            eng.matmul(o[:, WR * half:WR * half + WR], xg[par][:, g, P * half:P * half + P], oh[par][:, g, :],
                                       start=True, stop=True)
                        eng.matmul(o[:, 2 * WR:WA], t.ones[:, :], oh[par][:, g, :],
                                   start=True, stop=True).then_inc(summed, 1)
                each(eng, sums)

            @block.vector
            def _(eng):
                v = nc.vector

                def one_hots(n, par, first):
                    if not first:
                        eng.wait_ge(summed, (n - R + 1) * GS)
                    v.tensor_tensor(oh[par][:, :, :], t.iota[:, 0:WR].unsqueeze(1).to_broadcast([P, GS, WR]),
                                    row[:, bass.ds(n * GS, GS)].unsqueeze(2).to_broadcast([P, GS, WR]),
                                    ALU.is_equal).then_inc(hot, 1)

                def group(n, par, k, first):
                    if par == 0 and first:
                        one_hots(0, 0, True)
                    one_hots(n + 1, (par + 1) % R, first and par < R - 1)
                    if not first:
                        eng.wait_ge(acc_done, (n - R + 1) * GS)
                    v.tensor_copy(kp[par][:, :], keep[:, bass.ds(n * GS, GS)]).then_inc(kept, 1)
                    eng.wait_ge(kept, n + 1)
                    for g in range(GS):
                        i = n * GS + g
                        eng.wait_ge(summed, i + 1)
                        if not (first and par == 0):
                            eng.wait_ge(stored[g], n * 16)
                        if not (first and par == 0 and g == 0):
                            eng.wait_ge(acc_done, i)
                        v.scalar_tensor_tensor(acc[g][:, :], acc[(g - 1) % GS][:, :], kp[par][:, g:g + 1],
                                               p_a[g % 4][:, 0:WA], ALU.mult, ALU.add).then_inc(acc_done, 1)
                eng.wait_ge(tables_in, 16 * 5)
                v.memset(acc[GS - 1][:, :], 0.0).then_inc(acc_zero, 1)
                eng.wait_ge(acc_zero, 1)
                each(eng, group)

            @block.sync
            def _(eng):
                for j, of in enumerate((src, row, keep, win, last)):
                    eng.dma_start(of[:, :], t.tables1[j][:, :]).then_inc(tables_in, 16)
                eng.wait_ge(tables_in, 16 * 5)

                each(eng, lambda n, par, k, first: store(eng, n, 0))
                for g in range(0, GS, 2):
                    eng.wait_ge(stored[g], K1 // GS * 16)

            @block.scalar
            def _(eng):
                eng.wait_ge(tables_in, 16 * 5)
                each(eng, lambda n, par, k, first: store(eng, n, 1))
                for g in range(1, GS, 2):
                    eng.wait_ge(stored[g], K1 // GS * 16)


def mix_phase(nc, a, out, t):
    with ExitStack() as ctx:
        s = Scope(nc, ctx, "mx")
        SN = SBW * WN
        SR = SBW * WR
        QP = 4 * WR
        HH = SN // 2
        w = s.sb("w", [P, R6, 2, D])
        wrow = s.sb("wrow", [P, 10, D])
        wt = s.sb("wt", [P, 2, 10, P])
        b_in = s.sb("b_in", [P, R6, 2])
        qkv_b = s.sb("qkv_b", [P, 6])
        out_b = s.sb("out_b", [P, 2])
        proj_b = s.sb("proj_b", [P, D])
        eps = s.sb("eps", [P, 1])
        one = s.sb("one", [WR, WN])
        member0 = s.sb("member0", [WR, WN])
        member = s.sb("member", [WR, WN])
        member6 = s.sb("member6", [WR, WN])
        member_t = s.sb("member_t", [WN, WR])
        same = s.sb("same", [WR, WR])
        mask = s.sb("mask", [WR, 2 * WR], BF16)
        agg = [s.sb(f"agg{i}", [P, SBW, 3 * WR]) for i in range(2)]
        x1 = [s.sb(f"x1{i}", [HH, 2, D]) for i in range(2)]
        xb = [s.sb(f"xb{i}", [HH, 2, D]) for i in range(2)]
        st = s.sb("st", [P, 2, SR])
        qk = s.sb("qk", [P, 4, SR])
        top = [s.sb(f"top{i}", [WR, H]) for i in range(2)]
        ntop = [s.sb(f"ntop{i}", [WR, H]) for i in range(2)]
        pr = [s.sb(f"pr{i}", [WR, H, WR]) for i in range(3)]
        den = [s.sb(f"den{i}", [WR, H]) for i in range(3)]
        rden = [s.sb(f"rden{i}", [WR, H]) for i in range(3)]
        gd = [s.sb(f"gd{i}", [WR, H, WN]) for i in range(3)]
        gt = [s.sb(f"gt{i}", [WR, H * WN]) for i in range(2)]
        srow = [s.sb(f"srow{i}", [WR, D]) for i in range(4)]
        ut = s.sb("ut", [P, 2, H, SN])
        att = s.sb("att", [P, 2, SN])
        hid = s.sb("hid", [P, 2, SN])
        z = s.sb("z", [HH, 2, D])
        stats = s.sb("stats", [HH, 2, 6])
        mv = s.sb("mv", [HH, 2, 2])
        dev = s.sb("dev", [HH, 2])
        rdev = s.sb("rdev", [HH, 2])
        y = [s.sb(f"y{i}", [HH, 2, D]) for i in range(2)]
        p_g = [s.ps(f"pg{i}", [P, 512]) for i in range(2)]
        p_qk = [s.ps(f"pqk{i}", [P, 512]) for i in range(2)]
        p_sc = [[s.ps(f"psc{i}", [P, 512]) for i in range(2)], p_qk]
        p_gt = s.ps("pgt", [P, 512])
        p_u = s.ps("pu", [P, 512])

        w_in = s.sem("w_in")
        made = s.sem("made")
        mask_step = s.sem("mask_step")
        mask_ps = s.sem("mask_ps")
        wt_ps = s.sem("wt_ps")
        wt_done = s.sem("wt_done")
        agg_in = [s.sem(f"agg_in{i}") for i in range(2)]
        xb_done = s.sem("xb_done")
        g_ps = s.sem("g_ps")
        g_done = s.sem("g_done")
        qk_ps = s.sem("qk_ps")
        qk_done = s.sem("qk_done")
        sc_ps = s.sem("sc_ps")
        top_done = s.sem("top_done")
        ntop_done = s.sem("ntop_done")
        pr_done = s.sem("pr_done")
        rden_done = s.sem("rden_done")
        gd_done = s.sem("gd_done")
        row_ps = s.sem("row_ps")
        row_done = s.sem("row_done")
        gt_ps = s.sem("gt_ps")
        gt_done = s.sem("gt_done")
        u_ps = s.sem("u_ps")
        u_done = s.sem("u_done")
        stat = s.sem("stat")
        aggr = s.sem("aggr")
        dve_on = s.sem("dve_on")
        dev_done = s.sem("dev_done")
        rdev_done = s.sem("rdev_done")
        y_done = s.sem("y_done")
        y_out = [s.sem(f"y_out{i}") for i in range(2)]

        NG = 2 * R6
        NT = NG + 6
        W_LOADS = 7
        plan = ([("sum", k) for k in range(4)] + [("att", 0), ("att", 1)] + [("sum", k) for k in range(4, 8)] +
                [("hid", 0), ("hid", 1)] + [("sum", k) for k in range(8, NG)] + [("y", 0), ("y", 1)])

        def products(i, first):
            if first:
                return [(k, "sum", k) for k in range(NG)]
            return [(i * NT - 6 + k, kind, j) for k, (kind, j) in enumerate(plan)]

        def nodes_last():
            rest = [p for p in plan if p[0] != "sum"]
            return [(NSB * NT - 6 + k, kind, j) for k, (kind, j) in enumerate(rest)]

        def each(eng, body):
            body(0, 0, True)
            body(1, 1, False)
            with eng.Fori(1, NSB // 2) as k:
                body(k * 2, 0, False)
                body(k * 2 + 1, 1, False)
            body(NSB - 1, 0, False)
        assert NSB % 2 == 1

        with nc.Block() as block:
            @block.sync
            def _(eng):
                eng.dma_start(w[:, :, :, :].rearrange("p r k n -> p (r k) n"),
                              a["L1_gnn_W"].rearrange("r (k p) n -> p (r k) n", p=P)).then_inc(w_in, 16)
                for o, n, name in ((0, 6, "in_proj_w"), (6, 2, "attn_out_w"), (8, 2, "proj_w")):
                    eng.dma_start(wrow[:, o:o + n, :], a[f"L1_gnn_{name}"].rearrange("(k p) n -> p k n", p=P)
                                  ).then_inc(w_in, 16)
                eng.dma_start(qkv_b[:, :], a["L1_gnn_in_proj_b"].rearrange("(k p) -> p k", p=P),
                              allow_slow_non_contiguous=True).then_inc(w_in, 16)
                eng.dma_start(out_b[:, :], a["L1_gnn_attn_out_b"].rearrange("(k p) -> p k", p=P),
                              allow_slow_non_contiguous=True).then_inc(w_in, 16)
                eng.dma_start(proj_b[:, :], a["L1_gnn_proj_b"].partition_broadcast(P)).then_inc(w_in, 16)
                for r in range(R6):
                    eng.dma_start(b_in[:, r, :], a["L1_gnn_b"][r, :].rearrange("(k p) -> p k", p=P),
                                  allow_slow_non_contiguous=True).then_inc(w_in, 16)

                def store(i, par):
                    eng.wait_ge(y_done, i * 2 + 2)
                    full = not (past(i, NSB - 1) and isinstance(i, int))
                    for half in range(2):
                        rows = HH if full else min(HH, N - i * SN - half * HH)
                        eng.dma_start(out[bass.ds(i * SN + half * HH, rows), :],
                                      y[par][0:rows, half, :]).then_inc(y_out[par], 16)

                def load(i, par, first):
                    if past(i, 2):
                        eng.wait_ge(g_ps, i * NT - NG)
                        eng.wait_ge(xb_done, i * 2 - 2)
                    eng.dma_start(agg[par][:, :, :], t.agg[bass.ds(i * (SBW * P), SBW * P), :].rearrange(
                        "(w p) c -> p w c", p=P)).then_inc(agg_in[par], 16)
                    eng.dma_start(x1[par][:, :, :], t.x1[bass.ds(i * SN, SN), :].rearrange("(h p) c -> p h c", p=HH)
                                  ).then_inc(agg_in[par], 16)
                    if past(i, 2):
                        store(i - 2, par)
                each(eng, load)
                store(NSB - 2, 1)
                store(NSB - 1, 0)
                for par in range(2):
                    eng.wait_ge(y_out[par], 32 * ((NSB + 1 - par) // 2))

            @block.gpsimd
            def _(eng):
                eng.memset(one[:, :], 1.0).then_inc(made, 1)
                eng.wait_ge(made, 1)
                eng.affine_select(member0[:, :], one[:, :], [[-R6, WN]], ALU.is_ge, 0.0, base=0,
                                  channel_multiplier=1).then_inc(made, 1)
                eng.wait_ge(made, 2)
                eng.affine_select(member[:, :], member0[:, :], [[R6, WN]], ALU.is_ge, 0.0, base=R6 - 1,
                                  channel_multiplier=-1).then_inc(made, 1)
                eng.wait_ge(w_in, 16 * (W_LOADS + R6))

                def add_bias(i, par, first):
                    eng.wait_ge(agg_in[par], (i - par) * 16 + 32)
                    if past(i, 2):
                        eng.wait_ge(g_done, (i - 1) * NT - 6 + NT)
                    for half in range(2):
                        nc.gpsimd.tensor_tensor(xb[par][:, half, :], x1[par][:, half, :], proj_b[0:HH, :],
                                                ALU.add).then_inc(xb_done, 1)
                each(eng, add_bias)

            @block.tensor
            def _(eng):
                eng.wait_ge(w_in, 16 * (W_LOADS + R6))
                for o in range(10):
                    if o >= 2:
                        eng.wait_ge(wt_done, o - 1)
                    for k in range(2):
                        mm = eng.transpose(p_g[o % 2][:, P * k:P * k + P], wrow[:, o, P * k:P * k + P], t.ident[:, :])
                    mm.then_inc(wt_ps, 1)
                eng.wait_ge(made, 3)
                eng.transpose(p_sc[0][0][0:WN, 0:WR], member[:, :], t.ident[0:WR, 0:WR]).then_inc(mask_ps, 1)
                eng.wait_ge(mask_step, 1)
                eng.matmul(p_sc[0][1][0:WR, 0:WR], member_t[:, :], member_t[:, :], start=True,
                           stop=True).then_inc(mask_ps, 1)
                eng.wait_ge(mask_step, 4)
                eng.wait_ge(wt_done, 10)

                def product(i, par, n, kind, j, first, between=4):
                    o = p_g[j % 2]
                    if kind == "sum" and j < 2:
                        if not first:
                            eng.wait_ge(row_done, i * SBW - 1 + j)
                    else:
                        eng.wait_ge(g_done, n - 1)
                    if kind == "sum":
                        r, half = j // 2, j % 2
                        for k in range(2):
                            mm = eng.matmul(o[:, 0:SN], w[:, r, k, P * half:P * half + P],
                                            agg[par][:, :, k * WR + r:(k + 1) * WR:R6], start=(k == 0), stop=(k == 1))
                    elif kind == "att":
                        for e in range(2):
                            for k in range(2):
                                mm = eng.matmul(o[HD * e:HD * e + HD, 0:SN], wt[:, k, 4 + j, HD * e:HD * e + HD],
                                                ut[:, k, 2 * j + e, :], start=(k == 0), stop=(k == 1))
                    elif kind == "hid":
                        if j == 0:
                            eng.wait_ge(g_done, n - between)
                        for k in range(2):
                            eng.matmul(o[:, 0:SN], wt[:, k, 6 + j, :], att[:, k, :], start=(k == 0), stop=False)
                        for half in range(2):
                            mm = eng.matmul(o[:, HH * half:HH * half + HH], x1[1 - par][:, half, P * j:P * j + P],
                                            t.ident[0:HH, 0:HH], start=False, stop=(half == 1))
                    else:
                        if j == 0:
                            eng.wait_ge(g_done, n - between)
                        for k in range(2):
                            mm = eng.matmul(o[0:HH, 0:D], hid[:, k, HH * j:HH * j + HH],
                                            wt[:, k, 8:10, :].rearrange("p o c -> p (o c)"),
                                            start=(k == 0), stop=(k == 1))
                    mm.then_inc(g_ps, 1)

                def scores(v, x):
                    if past(v, 2):
                        eng.wait_ge(pr_done, v - 1)
                    for e in range(2):
                        o = p_sc[e][x % 2]
                        eng.matmul(o[0:WR, 0:2 * WR], t.ident_b[0:WR, 0:WR], mask[:, :], start=True, stop=False)
                    for b in range(2):
                        for e in range(2):
                            rows = slice(HD * e, HD * e + HD)
                            eng.matmul(p_sc[e][x % 2][0:WR, WR * b:WR * b + WR], qk[rows, b, WR * x:WR * x + WR],
                                       qk[rows, 2 + b, WR * x:WR * x + WR], start=False, stop=(b == 1)
                                       ).then_inc(sc_ps, 1)
                    if past(v, 2):
                        eng.wait_ge(row_done, v - 1)
                    for k in range(2):
                        mm = eng.transpose(p_g[x % 2][0:WR, P * k:P * k + P], st[:, k, WR * x:WR * x + WR], t.ident[:, :])
                    mm.then_inc(row_ps, 1)

                def weigh(v, x):
                    eng.wait_ge(gd_done, v + 1)
                    if past(v, 1):
                        eng.wait_ge(gt_done, v)
                    for h in range(H):
                        mm = eng.matmul(p_gt[0:WR, WN * h:WN * h + WN], pr[x % 3][:, h, :], gd[x % 3][:, h, :],
                                        start=True, stop=True)
                    mm.then_inc(gt_ps, 1)

                def gather(v, x):
                    eng.wait_ge(gt_done, v + 1)
                    eng.wait_ge(row_done, v + 1)
                    if past(v, 1):
                        eng.wait_ge(u_done, v)
                    for k in range(2):
                        mm = eng.matmul(p_u[:, H * WN * k:H * WN * k + H * WN], srow[x % 4][:, P * k:P * k + P], gt[x % 2][:, :],
                                        start=True, stop=True)
                    mm.then_inc(u_ps, 1)

                def superblock(i, par, first):
                    eng.wait_ge(agg_in[par], (i - par) * 16 + 32)
                    for n, kind, j in products(i, first):
                        product(i, par, n, kind, j, first)
                        if not first and kind == "sum" and j < 3:
                            if j < 2:
                                weigh(i * SBW - 2 + j, SBW - 2 + j)
                            gather(i * SBW - 3 + j, SBW - 3 + j)
                        if not first and kind == "sum" and j == 3:
                            eng.wait_ge(u_done, i * SBW)
                    eng.wait_ge(g_done, NG if first else i * NT - 6 + NT - 2)
                    for piece in range(3):
                        for c in range(4):
                            n = i * 12 + piece * 4 + c
                            if not (first and piece == 0 and c < 2):
                                eng.wait_ge(qk_done, n - 1)
                            for k in range(2):
                                mm = eng.matmul(p_qk[c % 2][:, 0:QP], wt[:, k, c, :],
                                                st[:, k, QP * piece:QP * piece + QP], start=(k == 0), stop=(k == 1))
                            mm.then_inc(qk_ps, 1)
                    eng.wait_ge(qk_done, i * 12 + 12)
                    eng.wait_ge(g_done, NG if first else i * NT - 6 + NT - 2)
                    for x in range(SBW):
                        scores(i * SBW + x, x)
                        if x >= 2:
                            weigh(i * SBW + x - 2, x - 2)
                        if x >= 3:
                            gather(i * SBW + x - 3, x - 3)

                each(eng, superblock)
                for j in range(3):
                    if j < 2:
                        weigh(NSB * SBW - 2 + j, SBW - 2 + j)
                    gather(NSB * SBW - 3 + j, SBW - 3 + j)
                eng.wait_ge(u_done, NSB * SBW)
                for n, kind, j in nodes_last():
                    product(NSB, 1, n, kind, j, False, between=0)

            @block.scalar
            def _(eng):
                act = nc.scalar.activation

                def copy_gt(v, x):
                    eng.wait_ge(gt_ps, v + 1)
                    if past(v, 2):
                        eng.wait_ge(u_ps, v - 1)
                    act(gt[x % 2][:, :], p_gt[0:WR, 0:H * WN], ACT.Copy).then_inc(gt_done, 1)

                def copy_u(v, x):
                    eng.wait_ge(u_ps, v + 1)
                    act(ut[:, :, :, WN * x:WN * x + WN],
                        p_u[:, 0:2 * H * WN].rearrange("p (k h n) -> p k h n", k=2, h=H),
                        ACT.Copy).then_inc(u_done, 1)

                def last_windows(i):
                    for j in range(3):
                        if j < 2:
                            copy_gt(i * SBW - 2 + j, SBW - 2 + j)
                        copy_u(i * SBW - 3 + j, SBW - 3 + j)

                def deviations(i):
                    eng.wait_ge(aggr, i * 2)
                    act(dev[:, :], mv[:, :, 1], ACT.Sqrt, bias=eps[0:HH, 0:1]).then_inc(dev_done, 1)

                def superblock(i, par, first):
                    if not first:
                        last_windows(i)
                    for piece in range(3):
                        for c in range(4):
                            eng.wait_ge(qk_ps, i * 12 + piece * 4 + c + 1)
                            act(qk[:, c, QP * piece:QP * piece + QP], p_qk[c % 2][:, 0:QP], ACT.Identity,
                                bias=qkv_b[:, c:c + 1]).then_inc(qk_done, 1)
                        if piece == 0 and not first:
                            deviations(i)
                    for x in range(SBW):
                        v = i * SBW + x
                        eng.wait_ge(ntop_done, v + 1)
                        if past(v, 3):
                            eng.wait_ge(gt_ps, v - 2)
                            eng.wait_ge(rden_done, v - 2)
                        for h in range(H):
                            ins = act(pr[x % 3][:, h, :], p_sc[h % 2][x % 2][0:WR, WR * (h // 2):WR * (h // 2) + WR], ACT.Exp,
                                      bias=ntop[x % 2][:, h:h + 1], scale=HD ** -0.5,
                                      accum_out=den[x % 3][:, h:h + 1])
                        ins.then_inc(pr_done, 1)
                        if x >= 2:
                            copy_gt(v - 2, x - 2)
                        if x >= 3:
                            copy_u(v - 3, x - 3)

                eng.wait_ge(mask_step, 4)
                each(eng, superblock)
                last_windows(NSB)
                deviations(NSB)

            @block.vector
            def _(eng):
                v_ = nc.vector
                for o in range(10):
                    eng.wait_ge(wt_ps, o + 1)
                    v_.tensor_copy(wt[:, :, o, :], p_g[o % 2][:, 0:D].rearrange("p (k c) -> p k c", k=2)
                                   ).then_inc(wt_done, 1)
                eng.wait_ge(mask_ps, 1)
                v_.memset(eps[:, :], EPS)
                v_.tensor_scalar(member6[:, :], member[:, :], 1.0 / R6, None, ALU.mult)
                v_.tensor_copy(member_t[:, :], p_sc[0][0][0:WN, 0:WR]).then_inc(mask_step, 1)
                eng.wait_ge(mask_ps, 2)
                v_.tensor_scalar(same[:, :], p_sc[0][1][0:WR, 0:WR], -1.0, BIG, ALU.add, ALU.mult).then_inc(mask_step, 1)
                eng.wait_ge(mask_step, 2)
                for h in range(2):
                    v_.tensor_copy(mask[:, WR * h:WR * h + WR], same[:, :]).then_inc(mask_step, 1)

                def take(i, par, n, kind, j):
                    o = p_g[j % 2]
                    eng.wait_ge(g_ps, n + 1)
                    if kind == "sum":
                        r, half = j // 2, j % 2
                        ins = v_.scalar_tensor_tensor(
                            st[:, half, r:SR:R6].rearrange("p (w n) -> p w n", w=SBW), agg[par][:, :, 2 * WR + r:3 * WR:R6],
                            b_in[:, r, half:half + 1], o[:, 0:SN].rearrange("p (w n) -> p w n", w=SBW),
                            ALU.mult, ALU.add)
                    elif kind == "att":
                        ins = v_.tensor_scalar(att[:, j, :], o[:, 0:SN], qkv_b[:, 4 + j:5 + j], None, ALU.add)
                    elif kind == "hid":
                        ins = v_.tensor_scalar(hid[:, j, :], o[:, 0:SN], out_b[:, j:j + 1], None, ALU.add)
                    else:
                        if j == 0:
                            eng.wait_ge(xb_done, i * 2)
                            if past(i, 2):
                                eng.wait_ge(y_done, i * 2 - 2)
                        ins = v_.tensor_tensor(z[:, j, :], o[0:HH, 0:D], xb[1 - par][:, j, :], ALU.add)
                    ins.then_inc(g_done, 1)

                def moments(i, n):
                    for half in range(2):
                        eng.wait_ge(g_done, n + half)
                        if half == 0 and past(i, 2):
                            eng.wait_ge(aggr, i * 2 - 2)
                        v_.bn_stats(stats[:, half, :], z[:, half, :]).then_inc(stat, 1)
                    for half in range(2):
                        eng.wait_ge(stat, i * 2 - 1 + half)
                        if half == 0 and past(i, 2):
                            eng.wait_ge(y_done, i * 2 - 2)
                        eng.sem_inc(dve_on, 1)
                        v_.bn_aggr(mv[:, half, :], stats[:, half, :]).then_inc(aggr, 1)

                def norm(i, par):
                    eng.wait_ge(dev_done, i)
                    v_.reciprocal(rdev[:, :], dev[:, :]).then_inc(rdev_done, 1)
                    eng.wait_ge(rdev_done, i)
                    if past(i, 3):
                        eng.wait_ge(y_out[par], (i - 1 - par) * 16)
                    for half in range(2):
                        v_.tensor_scalar(y[par][:, half, :], z[:, half, :], mv[:, half, 0:1], rdev[:, half:half + 1],
                                         ALU.subtract, ALU.mult).then_inc(y_done, 1)

                def maxima(v, x):
                    eng.wait_ge(sc_ps, v * 4 + 4)
                    if past(v, 2):
                        eng.wait_ge(ntop_done, v - 1)
                    for e in range(2):
                        v_.tensor_reduce(top[x % 2][:, e:H:2],
                                         p_sc[e][x % 2][0:WR, 0:2 * WR].rearrange("p (b m) -> p b m", b=2),
                                         AXX, ALU.max).then_inc(top_done, 1)

                def over(v, x):
                    eng.wait_ge(top_done, v * 2 + 2)
                    if past(v, 2):
                        eng.wait_ge(pr_done, v - 1)
                    v_.tensor_scalar(ntop[x % 2][:, :], top[x % 2][:, :], -HD ** -0.5, None,
                                     ALU.mult).then_inc(ntop_done, 1)

                def rows(v, x):
                    eng.wait_ge(row_ps, v + 1)
                    if past(v, 4):
                        eng.wait_ge(u_ps, v - 3)
                    v_.tensor_copy(srow[x % 4][:, :], p_g[x % 2][0:WR, 0:D]).then_inc(row_done, 1)

                def shares(v, x):
                    eng.wait_ge(pr_done, v + 1)
                    v_.reciprocal(rden[x % 3][:, :], den[x % 3][:, :]).then_inc(rden_done, 1)
                    eng.wait_ge(rden_done, v + 1)
                    if past(v, 3):
                        eng.wait_ge(gt_ps, v - 2)
                    v_.tensor_tensor(gd[x % 3][:, :, :], member6[:, :].unsqueeze(1).to_broadcast([WR, H, WN]),
                                     rden[x % 3][:, :].unsqueeze(2).to_broadcast([WR, H, WN]),
                                     ALU.mult).then_inc(gd_done, 1)

                def superblock(i, par, first):
                    eng.wait_ge(agg_in[par], (i - par) * 16 + 32)
                    for n, kind, j in products(i, first):
                        take(i, par, n, kind, j)
                    if not first:
                        moments(i, i * NT - 6 + NT - 1)
                    for x in range(SBW):
                        v = i * SBW + x
                        maxima(v, x)
                        over(v, x)
                        if x >= 1:
                            shares(v - 1, x - 1)
                        rows(v, x)
                        if x == 2 and not first:
                            norm(i, 1 - par)
                    shares(i * SBW + SBW - 1, SBW - 1)

                each(eng, superblock)
                for n, kind, j in nodes_last():
                    take(NSB, 1, n, kind, j)
                moments(NSB, NSB * NT - 6 + 5)
                norm(NSB, 0)


class Tensors:
    pass


def resnorm_gnn(nc, a, out):
    with ExitStack() as ctx:
        s = Scope(nc, ctx, "g")
        t = Tensors()
        t.pads = {n: nc.dram_tensor(f"pad_{n}", [EPAD], I32, kind="Internal").ap()
                  for n in ("src", "dst", "edge_type_6", "edge_type_64")}
        t.lastb = nc.dram_tensor("lastb", [G0 * P, H, 514], F32, kind="Internal").ap()
        t.kv = nc.dram_tensor("kv_rows", [NB * P, 2 * D], F32, kind="Internal").ap()
        t.rows0 = nc.dram_tensor("rows0", [G0 * P, 2 * C0], BF16, kind="Internal").ap()
        t.sums0 = nc.dram_tensor("sums0", [NB * P, H * (HD + 1)], F32, kind="Internal").ap()
        t.q3 = nc.dram_tensor("q3_rows", [NB * P, 3 * D], BF16, kind="Internal").ap()
        t.tables1 = [nc.dram_tensor(f"tables1_{k}", [P if k < 3 else 1, G1 * P], dt, kind="Internal").ap()
                     for k, dt in enumerate((I32, F32, F32, I32, I32))]
        t.x1 = nc.dram_tensor("x1_rows", [NW * WN, D], F32, kind="Internal").ap()
        t.agg = nc.dram_tensor("agg_t", [NW * P, 3 * WR], F32, kind="Internal").ap()
        t.iota_i = s.sb("iota_i", [P, P], I32)
        t.iota = s.sb("iota", [P, P])
        t.col = s.sb("col", [P, 1])
        t.ident = s.sb("ident", [P, P])
        t.ident_b = s.sb("ident_b", [P, P], BF16)
        t.ones = s.sb("ones", [P, P])
        with ExitStack() as layer0:
            s0 = Scope(nc, layer0, "g0")
            t.src0 = s0.sb("src0", [P, G0 * P * 4], I32)
            t.node0 = s0.sb("node0", [P, G0 * P * 4])
            t.blk = s0.sb("blk", [1, G0 * P], I32)
            t.last0 = s0.sb("last0", [1, G0 * P], I32)
            t.fresh0 = s0.sb("fresh0", [P, G0 * P])
            t.rel3 = s0.sb("rel3", [R64, 3, D], BF16)
            tables_phase(nc, a, t)
            project_phase(nc, a, t)
            attend_phase(nc, a, t)
            update_phase(nc, a, t)
        relate_phase(nc, a, t)
        mix_phase(nc, a, out, t)


_L0 = ["query_emb", "Wq", "bq", "Wk", "bk", "Wv", "bv", "rel_w", "Wo", "bo", "gamma", "beta"]
_L1 = ["W", "b", "in_proj_w", "in_proj_b", "attn_out_w", "attn_out_b", "proj_w", "proj_b"]
_INS = (["x", "src", "dst", "edge_type_6", "edge_type_64"] + [f"L0_gnn_{n}" for n in _L0] +
        [f"L1_gnn_{n}" for n in _L1])


def kernel(**inputs):
    import numpy as _np
    import concourse.bacc as _bacc
    from concourse import mybir as _mybir
    from concourse.bass_utils import run_bass_kernel_spmd as _run

    nc = _bacc.Bacc("TRN2", target_bir_lowering=False, num_devices=1)
    arrays, aps = {}, {}
    for name in _INS:
        arr = _np.ascontiguousarray(inputs[name])
        arrays[f"in_{name}_dram"] = arr
        aps[name] = nc.dram_tensor(f"in_{name}_dram", arr.shape, _mybir.dt.from_np(arr.dtype),
                                   kind="ExternalInput").ap()
    out = nc.dram_tensor("out_0_dram", (N, D), _mybir.dt.float32, kind="ExternalOutput").ap()
    resnorm_gnn(nc, aps, out)
    r = _run(nc, [arrays], core_ids=[0])
    return r.results[0]["out_0_dram"]
```

```python
from contextlib import ExitStack

import concourse.bass as bass
from concourse import mybir

ALU = mybir.AluOpType
ACT = mybir.ActivationFunctionType
AXX = mybir.AxisListType.X
F32 = mybir.dt.float32
BF16 = mybir.dt.bfloat16
I32 = mybir.dt.int32

P = 128
N = 6250
E = 200000
D = 256
H = 4
HD = D // H
R6 = 6
R64 = 64
EPAD = 392 * 512
HEADS = -(-E // 512)
FAR = 1 << 20
BIG = float(2 ** 100)
EPS = 1e-5

NB = -(-N // P)
C0 = 512
SUP = 4
K0 = -(-(E // C0 + NB + 1) // SUP) * SUP
NSUP = K0 // SUP
WN = 21
WR = WN * R6
SBW = 12
NSB = -(-N // (WN * SBW))
NW = NSB * SBW
C1 = 128
K1 = -(-(E // C1 + NW + 1) // 24) * 24
G0, G1 = -(-K0 // P), -(-(K1 + 24) // P)
GB0, GB1 = 1, -(-(NW + 1) // P)


class Scope:

    def __init__(self, nc, ctx, tag):
        self.nc, self.ctx, self.tag = nc, ctx, tag

    def sb(self, name, shape, dt=F32):
        return self.ctx.enter_context(self.nc.sbuf_tensor(f"{self.tag}_{name}", shape, dt))

    def ps(self, name, shape, dt=F32):
        return self.ctx.enter_context(self.nc.psum_tensor(f"{self.tag}_{name}", shape, dt))

    def sem(self, name):
        return self.ctx.enter_context(self.nc.semaphore(f"{self.tag}_{name}"))


class Count:

    def __init__(self, sem):
        self.sem, self.n = sem, 0

    def up(self, ins):
        self.n += 1
        ins.then_inc(self.sem, 1)
        return self.n


def past(i, n):
    return not isinstance(i, int) or i >= n


def tables_phase(nc, a, t):
    with ExitStack() as ctx:
        s = Scope(nc, ctx, "tab")
        src1 = s.sb("src1", [P, G1 * P], I32)
        row1 = s.sb("row1", [P, G1 * P])
        keep = s.sb("keep", [P, G1 * P])
        win = s.sb("win", [P, G1 * P], I32)
        last = s.sb("last", [P, G1 * P], I32)
        tables_out = s.sem("tables_out")
        pad_i = s.sb("pad_i", [2, EPAD - E], I32)
        heads_i = s.sb("heads_i", [1, HEADS], I32)
        heads_r = s.sb("heads_r", [1, HEADS])
        heads = s.sb("heads", [P, HEADS])
        junk = s.sb("junk", [P, 512])
        pcol_i = s.sb("pcol_i", [P, 1], I32)
        bounds = s.sb("bounds", [P, GB1])
        cnt = s.sb("cnt", [P, GB1])
        cnt2 = s.sb("cnt2", [P, GB1])
        crow_i = s.sb("crow_i", [P, GB1], I32)
        crow = s.sb("crow", [P, GB1])
        found_i = s.sb("found_i", [P, 512], I32)
        found = s.sb("found", [P, 512])
        start = s.sb("start", [P, GB1])
        diag = s.sb("diag", [P, P])
        srow = s.sb("srow", [P, GB1 * P])
        num_i = s.sb("num_i", [P, GB1 * P], I32)
        shr_i = s.sb("shr_i", [P, GB1 * P], I32)
        tiles = s.sb("tiles", [P, GB1 * P])
        zero = s.sb("zero", [P, GB1 * P])
        tend = s.sb("tend", [P, GB1 * P])
        tbeg = s.sb("tbeg", [P, GB1 * P])
        off = s.sb("off", [P, GB1 * P])
        doff = s.sb("doff", [P, GB1 * P])
        step = s.sb("step", [P, G1])
        rng = s.sb("rng", [P, G1])
        e0f = s.sb("e0f", [P, G1])
        e0i = s.sb("e0i", [P, G1], I32)
        rngneg = s.sb("rngneg", [P, G1])
        rows_i = s.sb("rows_i", [P, 2, 3, 512], I32)
        rows_f = s.sb("rows_f", [P, 3, 512])
        rows_b = s.sb("rows_b", [P, 2, C0], BF16)
        lastb = s.sb("lastb", [P, 514])
        rngrow = s.sb("rngrow", [P, G1 * P + 1])
        lastf = s.sb("lastf", [P, G1 * P])
        pb = s.ps("pb", [P, 512])
        pt = [s.ps(f"pt{i}", [P, 512]) for i in range(2)]

        pads_set = s.sem("pads_set")
        arrays_padded = s.sem("arrays_padded")
        heads_in = s.sem("heads_in")
        iota_done = s.sem("iota_done")
        dve = Count(s.sem("dve_done"))
        pe = Count(s.sem("pe_done"))
        gathered = s.sem("gathered")
        rows_in = [s.sem("rows_in0"), s.sem("rows_in1")]
        lastb_out = s.sem("lastb_out")
        rows0_out = s.sem("rows0_out")

        names = ("src", "dst", "edge_type_6", "edge_type_64")
        plan = {}

        def layer_plan():
            for L in (0, 1):
                gk = (G0, G1)[L]
                yield L, (P, WN)[L], (GB0, GB1)[L], (NB, NW)[L], (C0, C1)[L], gk

        def plan_rows(L, g):
            before = -(-G0 // 2) if g % 2 == 0 else G0 // 2
            return g // 2 + 1 + (before if L else 0)

        with nc.Block() as block:
            @block.vector
            def _(eng):
                v = nc.vector

                def link(ins):
                    eng.wait_ge(dve.sem, dve.up(ins))
                    return dve.n

                link(v.memset(pad_i[:, :], 0))
                plan["pad0"] = link(v.memset(pad_i[0:1, :], FAR))
                eng.wait_ge(iota_done, 4)
                link(v.tensor_copy(t.col[:, :], pcol_i[:, :]))
                link(v.tensor_copy(t.iota[:, :], t.iota_i[:, :]))
                link(v.tensor_scalar(t.ident[:, :], t.iota[:, :], t.col[:, 0:1], None, ALU.is_equal))
                link(v.tensor_copy(t.ident_b[:, :], t.ident[:, :]))
                link(v.memset(t.ones[:, :], 1.0))
                link(v.memset(zero[:, :], 0.0))
                link(v.memset(rngrow[:, :], -1.0))
                eng.wait_ge(heads_in, 16)
                plan["heads_r"] = link(v.tensor_copy(heads_r[:, :], heads_i[:, :]))
                eng.wait_ge(pe.sem, 1)
                link(v.tensor_copy(heads[:, :], pb[:, 0:HEADS]))
                pe_n = 1
                ptn = 0
                gath = 0
                for L, stride, gb, nr, cs, gk in layer_plan():
                    for g in range(gb):
                        link(v.tensor_scalar(bounds[:, g:g + 1], t.col[:, 0:1], float(P * g), float(stride),
                                             ALU.add, ALU.mult))
                        link(v.tensor_scalar(junk[:, 0:HEADS], heads[:, :], bounds[:, g:g + 1], 0.0,
                                             ALU.is_lt, ALU.add, accum_out=cnt[:, g:g + 1]))
                        link(v.tensor_scalar(crow[:, g:g + 1], cnt[:, g:g + 1], -1.0, 0.0, ALU.add, ALU.max))
                        plan["crow", L, g] = link(v.tensor_copy(crow_i[:, g:g + 1], crow[:, g:g + 1]))
                        gath += 1
                        eng.wait_ge(gathered, 16 * gath)
                        link(v.tensor_copy(found[:, :], found_i[:, :]))
                        link(v.tensor_scalar(junk[:, :], found[:, :], bounds[:, g:g + 1], 0.0,
                                             ALU.is_lt, ALU.add, accum_out=cnt2[:, g:g + 1]))
                        link(v.scalar_tensor_tensor(start[:, g:g + 1], crow[:, g:g + 1], 512.0,
                                                    cnt2[:, g:g + 1], ALU.mult, ALU.add))
                        plan["diag", L, g] = link(v.tensor_scalar(diag[:, :], t.ident[:, :], start[:, g:g + 1],
                                                                  None, ALU.mult))
                        pe_n += 1
                        eng.wait_ge(pe.sem, pe_n)
                        link(v.tensor_copy(srow[:, P * g:P * g + P], pb[:, 0:P]))
                    link(v.tensor_tensor(tiles[:, 0:nr], srow[:, 1:nr + 1], srow[:, 0:nr], ALU.subtract))
                    link(v.tensor_scalar(num_i[:, 0:nr], tiles[:, 0:nr], float(cs - 1), None, ALU.add))
                    link(v.tensor_scalar(shr_i[:, 0:nr], num_i[:, 0:nr], cs.bit_length() - 1, None,
                                         ALU.logical_shift_right))
                    link(v.tensor_scalar(tiles[:, 0:nr], shr_i[:, 0:nr], 1.0, None, ALU.max))
                    link(v.tensor_tensor_scan(tend[:, 0:nr], tiles[:, 0:nr], zero[:, 0:nr], 0.0, ALU.add, ALU.max))
                    link(v.tensor_tensor(tbeg[:, 0:nr], tend[:, 0:nr], tiles[:, 0:nr], ALU.subtract))
                    link(v.scalar_tensor_tensor(off[:, 0:nr], tbeg[:, 0:nr], float(-cs), srow[:, 0:nr],
                                                ALU.mult, ALU.add))
                    link(v.tensor_tensor(doff[:, 0:nr - 1], off[:, 1:nr], off[:, 0:nr - 1], ALU.subtract))
                    for g in range(gk):
                        link(v.tensor_scalar(step[:, g:g + 1], t.col[:, 0:1], float(P * g), None, ALU.add))
                        link(v.tensor_scalar(junk[:, 0:nr - 1], tend[:, 0:nr - 1], step[:, g:g + 1], 0.0,
                                             ALU.is_le, ALU.add, accum_out=rng[:, g:g + 1]))
                        link(v.scalar_tensor_tensor(junk[:, 0:nr - 1], tend[:, 0:nr - 1], step[:, g:g + 1],
                                                    doff[:, 0:nr - 1], ALU.is_le, ALU.mult,
                                                    accum_out=e0f[:, g:g + 1]))
                    link(v.scalar_tensor_tensor(e0f[:, 0:gk], step[:, 0:gk], float(cs), e0f[:, 0:gk],
                                                ALU.mult, ALU.add))
                    link(v.tensor_scalar(e0f[:, 0:gk], e0f[:, 0:gk], float(E), None, ALU.min))
                    plan["e0", L] = link(v.tensor_copy(e0i[:, 0:gk], e0f[:, 0:gk]))
                    link(v.tensor_scalar(rngneg[:, 0:gk], rng[:, 0:gk], float(-stride), None, ALU.mult))
                    for g in range(gk):
                        plan["rdiag", L, g] = link(v.tensor_scalar(diag[:, :], t.ident[:, :], rng[:, g:g + 1],
                                                                   None, ALU.mult))
                        pe_n += 1
                        eng.wait_ge(pe.sem, pe_n)
                        link(v.tensor_copy(rngrow[:, P * g:P * g + P], pb[:, 0:P]))
                    if L == 0:
                        link(v.tensor_copy(t.blk[:, :], rngrow[0:1, 0:G0 * P]))
                        link(v.memset(t.fresh0[:, 0:1], -BIG))
                        link(v.tensor_tensor(lastf[:, 0:G0 * P - 1], rngrow[:, 1:G0 * P], rngrow[:, 0:G0 * P - 1],
                                             ALU.not_equal))
                        link(v.tensor_scalar(t.fresh0[:, 1:G0 * P], lastf[:, 0:G0 * P - 1], -BIG, None, ALU.mult))
                        link(v.memset(rngrow[:, K0:K0 + 1], -1.0))
                        link(v.tensor_tensor(lastf[:, 0:K0], rngrow[:, 1:K0 + 1], rngrow[:, 0:K0],
                                             ALU.not_equal))
                        link(v.tensor_copy(t.last0[:, 0:K0], lastf[0:1, 0:K0]))
                    else:
                        link(v.tensor_copy(win[:, :], rngrow[:, 0:G1 * P]))
                        link(v.memset(keep[:, 0:1], 0.0))
                        link(v.tensor_tensor(keep[:, 1:G1 * P], rngrow[:, 1:G1 * P], rngrow[:, 0:G1 * P - 1],
                                             ALU.is_equal))
                        link(v.memset(rngrow[:, K1:K1 + 1], -1.0))
                        link(v.tensor_tensor(lastf[:, :], rngrow[:, 1:G1 * P + 1], rngrow[:, 0:G1 * P],
                                             ALU.not_equal))
                        link(v.tensor_copy(last[:, :], lastf[:, :]))
                    for g in range(gk):
                        ri = rows_i[:, g % 2, :, :]
                        eng.wait_ge(rows_in[g % 2], 48 * plan_rows(L, g))
                        link(v.tensor_copy(rows_f[:, :, 0:cs], ri[:, :, 0:cs]))
                        if L == 0:
                            if g:
                                eng.wait_ge(lastb_out, 64 * g)
                            link(v.memset(lastb[:, :], -BIG))
                            link(v.tensor_tensor(junk[:, 0:511], rows_f[:, 1, 0:511], rows_f[:, 1, 1:512],
                                                 ALU.not_equal))
                            plan["lastb", g] = link(v.tensor_scalar(lastb[:, 1:512], junk[:, 0:511], -BIG, None,
                                                                    ALU.mult))
                        link(v.tensor_scalar(rows_f[:, 1, 0:cs], rows_f[:, 1, 0:cs], rngneg[:, g:g + 1], None,
                                             ALU.add))
                        if L == 1:
                            link(v.scalar_tensor_tensor(rows_f[:, 1, 0:cs], rows_f[:, 1, 0:cs], float(R6),
                                                        rows_f[:, 2, 0:cs], ALU.mult, ALU.add))
                        if L == 0:
                            if g:
                                eng.wait_ge(rows0_out, 16 * g)
                            plan["rows_b", g] = link(v.tensor_copy(rows_b[:, :, :], rows_f[:, 1:3, :]))
                        plan["rows", L, g] = dve.n
                        pe_n += 1
                        eng.wait_ge(pe.sem, pe_n)
                        nj = cs // P
                        for dst, k in (((t.src0, 0), (t.node0, 1)) if L == 0 else
                                       ((src1, 0), (row1, 1))):
                            o = dst[:, P * g * nj:P * (g + 1) * nj].rearrange("p (s j) -> p j s", j=nj)
                            link(v.tensor_copy(o, pt[k][:, 0:cs].rearrange("p (j s) -> p j s", j=nj)))
                        plan["copied", L, g] = dve.n

            @block.gpsimd
            def _(eng):
                eng.iota(pcol_i[:, :], [[0, 1]], base=0, channel_multiplier=1).then_inc(iota_done, 2)
                eng.iota(t.iota_i[:, :], [[1, P]], base=0, channel_multiplier=0).then_inc(iota_done, 2)
                eng.wait_ge(arrays_padded, 16 * 8)
                n = 0
                for L, stride, gb, nr, cs, gk in layer_plan():
                    for g in range(gb):
                        eng.wait_ge(dve.sem, plan["crow", L, g])
                        eng.indirect_dma_start(
                            out=found_i[:, :], out_offset=None,
                            in_=t.pads["dst"].rearrange("(r c) -> r c", c=512),
                            in_offset=bass.IndirectOffsetOnAxis(ap=crow_i[:, g:g + 1], axis=0),
                        ).then_inc(gathered, 16)
                    eng.wait_ge(dve.sem, plan["e0", L])
                    for g in range(gk):
                        if g >= 2:
                            eng.wait_ge(dve.sem, plan["copied", L, g - 2])
                        elif L:
                            eng.wait_ge(dve.sem, plan["copied", 0, G0 - 1])
                        for k, name in enumerate(("src", "dst", ("edge_type_64", "edge_type_6")[L])):
                            eng.indirect_dma_start(
                                out=rows_i[:, g % 2, k, 0:cs], out_offset=None,
                                in_=t.pads[name].rearrange("(r c) -> r c", c=1),
                                in_offset=bass.IndirectOffsetOnAxis(ap=e0i[:, g:g + 1], axis=0),
                            ).then_inc(rows_in[g % 2], 16)

            @block.tensor
            def _(eng):
                eng.wait_ge(dve.sem, plan["heads_r"])
                pe.up(eng.matmul(pb[:, 0:HEADS], t.ones[0:1, :], heads_r[:, :], start=True, stop=True))
                for L, stride, gb, nr, cs, gk in layer_plan():
                    for g in range(gb):
                        eng.wait_ge(dve.sem, plan["diag", L, g])
                        pe.up(eng.matmul(pb[:, 0:P], t.ones[:, :], diag[:, :], start=True, stop=True))
                    for g in range(gk):
                        eng.wait_ge(dve.sem, plan["rdiag", L, g])
                        pe.up(eng.matmul(pb[:, 0:P], t.ones[:, :], diag[:, :], start=True, stop=True))
                    for g in range(gk):
                        eng.wait_ge(dve.sem, plan["rows", L, g])
                        for k in range(2):
                            for j in range(cs // P):
                                mm = eng.transpose(pt[k][:, P * j:P * j + P], rows_f[:, k, P * j:P * j + P],
                                                     t.ident[:, :])
                        pe.up(mm)

            @block.sync
            def _(eng):
                for name in names:
                    eng.dma_start(t.pads[name][0:E].rearrange("(p f) -> p f", p=160),
                                  a[name].rearrange("(p f) -> p f", p=160)).then_inc(arrays_padded, 16)
                eng.dma_start(heads_i[:, :], a["dst"].rearrange("(o e) -> o e", o=1)[:, 0:E:512],
                              allow_slow_non_contiguous=True).then_inc(heads_in, 16)
                eng.wait_ge(dve.sem, plan["pad0"])
                for name in names:
                    k = 0 if name == "dst" else 1
                    eng.dma_start(t.pads[name][E:EPAD].rearrange("(o e) -> o e", o=1),
                                  pad_i[k:k + 1, :]).then_inc(arrays_padded, 16)
                for g in range(G0):
                    eng.wait_ge(dve.sem, plan["lastb", g])
                    for h in range(H):
                        eng.dma_start(t.lastb[P * g:P * g + P, h, :], lastb[:, :]).then_inc(lastb_out, 16)
                    eng.wait_ge(dve.sem, plan["rows_b", g])
                    eng.dma_start(t.rows0[P * g:P * g + P, :], rows_b[:, :, :].rearrange("p k e -> p (k e)")
                                  ).then_inc(rows0_out, 16)
                eng.wait_ge(rows0_out, 16 * G0)
                eng.wait_ge(lastb_out, 64 * G0)
                eng.wait_ge(dve.sem, plan["copied", 1, G1 - 1])
                for k, of in enumerate((src1, row1, keep, win, last)):
                    rows = P if k < 3 else 1
                    eng.dma_start(t.tables1[k][0:rows, :], of[0:rows, :]).then_inc(tables_out, 16)
                eng.wait_ge(tables_out, 16 * 5)


def project_phase(nc, a, t):
    with ExitStack() as ctx:
        s = Scope(nc, ctx, "pr")
        w = s.sb("w", [P, 2, 3 * D])
        brow = s.sb("brow", [P, 3 * D])
        bq8 = s.sb("bq8", [P, D])
        qcol = s.sb("qcol", [P, 2])
        qcol01 = s.sb("qcol01", [P, 2])
        relw = s.sb("relw", [R64, HD])
        rel = s.sb("rel", [R64, HD])
        rrest = s.sb("rrest", [R64, 2, HD])
        x = [s.sb(f"x{i}", [P, D]) for i in range(2)]
        enh = [s.sb(f"enh{i}", [P, 2, P]) for i in range(2)]
        kv = [s.sb(f"kv{i}", [P, 2 * D]) for i in range(2)]
        q = [s.sb(f"q{i}", [P, D]) for i in range(2)]
        rest = [s.sb(f"rest{i}", [P, 2, D]) for i in range(2)]
        q3 = [s.sb(f"q3{i}", [P, 3, D], BF16) for i in range(2)]
        p_t = [s.ps(f"pt{i}", [P, 512]) for i in range(2)]
        p_kv = [s.ps(f"pkv{i}", [P, 512]) for i in range(2)]
        p_q = [s.ps(f"pq{i}", [P, 512]) for i in range(2)]

        w_in = s.sem("w_in")
        x_zero = s.sem("x_zero")
        x_in = [s.sem(f"x_in{i}") for i in range(2)]
        x_turned = s.sem("x_turned")
        enh_done = s.sem("enh_done")
        kv_ps = s.sem("kv_ps")
        q_ps = s.sem("q_ps")
        kv_done = s.sem("kv_done")
        q_done = s.sem("q_done")
        part = s.sem("part")
        rest_done = s.sem("rest_done")
        out_kv = [s.sem(f"out_kv{i}") for i in range(2)]
        out_q3 = [s.sem(f"out_q3{i}") for i in range(2)]
        setup = s.sem("setup")

        def each(eng, body):
            body(0, 0, True, P)
            body(1, 1, True, P)
            with eng.Fori(1, NB // 2 - 1) as k:
                body(k * 2, 0, False, P)
                body(k * 2 + 1, 1, False, P)
            body(NB - 3, 0, False, P)
            body(NB - 2, 1, False, P)
            body(NB - 1, 0, False, N - (NB - 1) * P)

        def another(i):
            return not (isinstance(i, int) and i == NB - 1)

        assert NB % 2 == 1
        with nc.Block() as block:
            @block.sync
            def _(eng):
                for k in range(2):
                    for j, name in enumerate(("L0_gnn_Wk", "L0_gnn_Wv", "L0_gnn_Wq")):
                        eng.dma_start(w[:, k, D * j:D * j + D], a[name][P * k:P * k + P, :]).then_inc(w_in, 16)
                for j, name in enumerate(("L0_gnn_bk", "L0_gnn_bv", "L0_gnn_bq")):
                    eng.dma_start(brow[:, D * j:D * j + D], a[name].partition_broadcast(P)).then_inc(w_in, 16)
                eng.dma_start(qcol[:, :], a["L0_gnn_query_emb"].rearrange("(k p) -> p k", p=P),
                              allow_slow_non_contiguous=True).then_inc(w_in, 16)
                eng.dma_start(relw[:, :], a["L0_gnn_rel_w"]).then_inc(w_in, 16)

                def load(i, par, first, rows):
                    if rows < P:
                        eng.wait_ge(x_zero, 1)
                    elif not first:
                        eng.wait_ge(x_turned, i - 1)
                    eng.dma_start(x[par][0:rows, :], a["x"][bass.ds(i * P, rows), :]).then_inc(x_in[par], 16)
                    if past(i, 2):
                        store(i - 2, par)

                def store(i, par):
                    eng.wait_ge(kv_done, i + 1)
                    eng.sem_inc(t.sp_on, 1)
                    eng.dma_start(t.kv[bass.ds(i * P, P), :], kv[par][:, :]).then_inc(out_kv[par], 16)
                each(eng, load)
                store(NB - 2, 1)
                store(NB - 1, 0)
                for par in range(2):
                    eng.wait_ge(out_kv[par], 16 * ((NB + 1 - par) // 2))

            @block.tensor
            def _(eng):
                eng.wait_ge(w_in, 16 * 11)

                def turn(i, par):
                    eng.wait_ge(x_in[par], (i - par) * 8 + 16)
                    if past(i, 2):
                        eng.wait_ge(enh_done, (i - 1) * 2)
                    for k in range(2):
                        mm = eng.transpose(p_t[par][:, P * k:P * k + P], x[par][:, P * k:P * k + P], t.ident[:, :])
                    mm.then_inc(x_turned, 1)

                def tile(i, par, first, rows):
                    if another(i):
                        turn(i + 1, 1 - par)
                    eng.wait_ge(enh_done, i * 2 + 2)
                    if not first:
                        eng.wait_ge(kv_done, i - 1)
                        eng.wait_ge(q_done, i - 1)
                    for k in range(2):
                        mm = eng.matmul(p_kv[par][:, :], enh[par][:, k, :], w[:, k, 0:2 * D],
                                        start=(k == 0), stop=(k == 1))
                    mm.then_inc(kv_ps, 1)
                    for k in range(2):
                        mm = eng.matmul(p_q[par][:, 0:D], enh[par][:, k, :], w[:, k, 2 * D:3 * D],
                                        start=(k == 0), stop=(k == 1))
                    mm.then_inc(q_ps, 1)
                turn(0, 0)
                each(eng, tile)

            @block.vector
            def _(eng):
                v = nc.vector
                eng.wait_ge(w_in, 16 * 11)
                v.tensor_scalar(qcol01[:, :], qcol[:, :], 0.1, None, ALU.mult).then_inc(setup, 1)
                v.tensor_scalar(bq8[:, :], brow[:, 2 * D:3 * D], 0.125, None, ALU.mult).then_inc(setup, 1)
                v.tensor_scalar(rel[:, :], relw[:, :], 0.2, None, ALU.mult).then_inc(setup, 1)
                eng.wait_ge(setup, 3)
                rest_of, n = rel[:, :], 3
                for j in range(3):
                    for h in range(H):
                        v.tensor_copy(t.rel3[:, j, HD * h:HD * h + HD], rest_of).then_inc(setup, 1)
                        n += 1
                    eng.wait_ge(setup, n)
                    if j < 2:
                        v.tensor_tensor(rrest[:, j, :], rest_of, t.rel3[:, j, 0:HD], ALU.subtract).then_inc(setup, 1)
                        n += 1
                        eng.wait_ge(setup, n)
                        rest_of = rrest[:, j, :]

                def enhance(i, par):
                    if isinstance(i, int) and i == NB - 1:
                        eng.wait_ge(x_turned, i - 1)
                        v.memset(x[par][:, :], 0.0).then_inc(x_zero, 1)
                    eng.wait_ge(x_turned, i + 1)
                    if past(i, 2):
                        eng.wait_ge(q_ps, i - 1)
                    for k in range(2):
                        v.tensor_scalar(enh[par][:, k, :], p_t[par][:, P * k:P * k + P], qcol01[:, k:k + 1], None,
                                        ALU.add).then_inc(enh_done, 1)

                def tile(i, par, first, rows):
                    if another(i):
                        enhance(i + 1, 1 - par)
                    eng.wait_ge(kv_ps, i + 1)
                    if not first:
                        eng.wait_ge(out_kv[par], (i - par) * 8)
                    v.tensor_tensor(kv[par][:, :], p_kv[par][:, :], brow[:, 0:2 * D], ALU.add).then_inc(kv_done, 1)
                    eng.wait_ge(q_ps, i + 1)
                    if not first:
                        eng.wait_ge(part, (i - 1) * 3)
                        eng.wait_ge(rest_done, (i - 1) * 2)
                    v.scalar_tensor_tensor(q[par][:, :], p_q[par][:, 0:D], 0.125, bq8[:, :], ALU.mult,
                                           ALU.add).then_inc(q_done, 1)
                enhance(0, 0)
                each(eng, tile)

            @block.scalar
            def _(eng):

                def tile(i, par, first, rows):
                    for j in range(3):
                        if j == 0:
                            eng.wait_ge(q_done, i + 1)
                            if not first:
                                eng.wait_ge(out_q3[par], (i - par) * 8)
                            of = q[par][:, :]
                        else:
                            eng.wait_ge(rest_done, i * 2 + j)
                            of = rest[par][:, j - 1, :]
                        nc.scalar.activation(q3[par][:, j, :], of, ACT.Copy).then_inc(part, 1)
                    eng.wait_ge(part, i * 3 + 3)
                    eng.dma_start(t.q3[bass.ds(i * P, P), :], q3[par][:, :, :].rearrange("p a b -> p (a b)")
                                  ).then_inc(out_q3[par], 16)
                each(eng, tile)
                for par in range(2):
                    eng.wait_ge(out_q3[par], 16 * ((NB + 1 - par) // 2))

            @block.gpsimd
            def _(eng):

                def tile(i, par, first, rows):
                    for j in range(2):
                        of = q[par][:, :] if j == 0 else rest[par][:, 0, :]
                        eng.wait_ge(part, i * 3 + j + 1)
                        nc.gpsimd.tensor_tensor(rest[par][:, j, :], of, q3[par][:, j, :],
                                                ALU.subtract).then_inc(rest_done, 1)
                each(eng, tile)


def attend_phase(nc, a, t):
    with ExitStack() as ctx:
        s = Scope(nc, ctx, "at")
        T = 4 * SUP
        M = SUP * H
        VW = H * (HD + 1)
        AHEAD, PREP, SUM, MERGE = 2, 6, 7, 8
        kv = [s.sb(f"kv{i}", [P, T, 2 * D]) for i in range(2)]
        idx = [s.sb(f"idx{i}", [P, T], I32) for i in range(2)]
        hot = [s.sb(f"hot{i}", [P, SUP, 2 * C0], BF16) for i in range(2)]
        q3 = [s.sb(f"q3{i}", [P, 3, D], BF16) for i in range(SUP)]
        kr = s.sb("kr", [P, 4, D])
        sc = [s.sb(f"sc{i}", [P, 4, SUP, H]) for i in range(2)]
        lastb = [s.sb(f"lastb{i}", [M, 514]) for i in range(2)]
        fmax = s.sb("fmax", [M, 512])
        smax = s.sb("smax", [M, 512])
        ex = s.sb("ex", [M, 512])
        lmax = s.sb("lmax", [M, 512])
        wgt = [s.sb(f"wgt{i}", [P, 2, 4, SUP, H]) for i in range(2)]
        vs = [s.sb(f"vs{i}", [P, 4, VW + H]) for i in range(2)]
        eh = [s.sb(f"eh{i}", [P, 4, P]) for i in range(2)]
        fresh = [s.sb(f"fresh{i}", [P, SUP]) for i in range(2)]
        absent = s.sb("absent", [P, H])
        cmax = s.sb("cmax", [P, H])
        top = [s.sb(f"top{i}", [P, H]) for i in range(SUP)]
        dmax = [s.sb(f"dmax{i}", [P, 2, H]) for i in range(2)]
        fac = [s.sb(f"fac{i}", [P, 2, H]) for i in range(2)]
        add = [s.sb(f"add{i}", [P, VW]) for i in range(2)]
        old = s.sb("old", [P, VW])
        acc = [s.sb(f"acc{i}", [P, VW]) for i in range(SUP)]
        p_q = [s.ps(f"p_q{i}", [P, 512]) for i in range(2)]
        p_r = [s.ps(f"p_r{i}", [P, 512]) for i in range(2)]
        p_x = s.ps("p_x", [P, 512])
        p_w = s.ps("p_w", [P, 512])
        p_s = [s.ps(f"p_s{i}", [P, 512]) for i in range(2)]

        kv_in = [[s.sem(f"kv_in{i}{c}") for c in range(SUP)] for i in range(2)]
        idx_set = s.sem("idx_set")
        q3_in = [s.sem(f"q3_in{c}") for c in range(SUP)]
        hot_in = [s.sem(f"hot_in{i}") for i in range(2)]
        lastb_in = [s.sem(f"lastb_in{i}") for i in range(2)]
        cleared = s.sem("cleared")
        hot_done = s.sem("hot_done")
        r_ps = s.sem("r_ps")
        q_ps = s.sem("q_ps")
        kr_sum = s.sem("kr_sum")
        kr_prod = s.sem("kr_prod")
        scored = s.sem("scored")
        sc_turned = s.sem("sc_turned")
        scanned = s.sem("scanned")
        over = s.sem("over")
        lmax_done = s.sem("lmax_done")
        ex_done = s.sem("ex_done")
        w_turned = s.sem("w_turned")
        wgt_done = s.sem("wgt_done")
        eh_done = s.sem("eh_done")
        vs_w = s.sem("vs_w")
        vs_v = s.sem("vs_v")
        summed = s.sem("summed")
        fresh_in = s.sem("fresh_in")
        marked = s.sem("marked")
        cmax_done = s.sem("cmax_done")
        top_done = s.sem("top_done")
        dmax_done = s.sem("dmax_done")
        fac_done = s.sem("fac_done")
        add_done = s.sem("add_done")
        old_done = s.sem("old_done")
        acc_done = s.sem("acc_done")
        stored = [s.sem(f"stored{i}") for i in range(SUP)]

        def run(eng, body):
            for n in range(4):
                body(n, n % 2)
            with eng.Fori(2, NSUP // 2 - 1) as k:
                body(k * 2, 0)
                body(k * 2 + 1, 1)
            for n in range(NSUP - 2, NSUP + 2):
                body(n, n % 2)

        assert NSUP % 2 == 0

        def chunk(n, par, p, lag):
            return n * SUP + (p - lag), (p - lag) % SUP, n + (p - lag) // SUP, (par + (p - lag) // SUP) % 2

        def exists(i):
            return not isinstance(i, int) or 0 <= i < K0

        with nc.Block() as block:
            @block.gpsimd
            def _(eng):

                def gather(g, c, n, par):
                    if c == 0:
                        if past(n, 2):
                            eng.wait_ge(kv_in[par][SUP - 1], (n - par) * 32)
                        nc.gpsimd.tensor_copy(idx[par][:, :], t.src0[:, bass.ds(n * T, T)]).then_inc(idx_set, 1)
                        eng.wait_ge(idx_set, n + 1)
                        eng.sem_inc(t.pool_on, 1)
                    if past(n, 2):
                        eng.wait_ge(vs_v, g - 2 * SUP + 1)
                        eng.sem_inc(t.pool_on, 1)
                    for j in range(4):
                        eng.indirect_dma_start(
                            out=kv[par][:, 4 * c + j, :], out_offset=None, in_=t.kv,
                            in_offset=bass.IndirectOffsetOnAxis(ap=idx[par][:, 4 * c + j:4 * c + j + 1], axis=0),
                        ).then_inc(kv_in[par][c], 16)

                def merge(i, c, n):
                    eng.wait_ge(fac_done, i + 1)
                    if past(i, 1):
                        eng.wait_ge(acc_done, i)
                    nc.gpsimd.tensor_tensor(old[:, :].rearrange("p (h e) -> p h e", h=H),
                                            acc[c - 1][:, :].rearrange("p (h e) -> p h e", h=H),
                                            fac[c % 2][:, 0, :].unsqueeze(2).to_broadcast([P, H, HD + 1]),
                                            ALU.mult).then_inc(old_done, 1)
                    eng.wait_ge(old_done, i + 1)
                    eng.wait_ge(add_done, i + 1)
                    if past(n, 1):
                        eng.wait_ge(stored[c], n * 16)
                    nc.gpsimd.tensor_tensor(acc[c][:, :], old[:, :], add[c % 2][:, :], ALU.add).then_inc(acc_done, 1)

                def positions(n, par):
                    for p in range(SUP):
                        g, c, m, mpar = chunk(n, par, p, -AHEAD)
                        if exists(g):
                            gather(g, c, m, mpar)
                        i, c, m, _ = chunk(n, par, p, MERGE)
                        if exists(i):
                            merge(i, c, m)

                eng.wait_ge(cleared, 2)
                for c in range(AHEAD):
                    gather(c, c, 0, 0)
                run(eng, positions)

            @block.sync
            def _(eng):

                def load_hot(n, par):
                    eng.dma_start(hot[par][:, :, :].rearrange("p c e -> p (c e)"),
                                  t.rows0[bass.ds(n * SUP, SUP), :].rearrange("c e -> (c e)").partition_broadcast(P)
                                  ).then_inc(hot_in[par], 16)

                def load_lastb(n, par):
                    eng.dma_start(lastb[par][:, :], t.lastb[bass.ds(n * SUP, SUP), :, :].rearrange("c h e -> (c h) e")
                                  ).then_inc(lastb_in[par], 16)

                def load_q3(n, c):
                    b = eng.value_load(t.blk[0:1, bass.ds(n * SUP + c, 1)], min_val=0, max_val=NB - 1)
                    eng.dma_start(q3[c][:, :, :].rearrange("p a b -> p (a b)"), t.q3[bass.ds(b * P, P), :]
                                  ).then_inc(q3_in[c], 16)

                def store(i, c):
                    b = eng.value_load(t.blk[0:1, bass.ds(i, 1)], min_val=0, max_val=NB - 1)
                    z = eng.value_load(t.last0[0:1, bass.ds(i, 1)], min_val=0, max_val=1)
                    eng.wait_ge(acc_done, i + 1)
                    eng.dma_start(t.sums0[bass.ds(b * P, P), :], acc[c][:, :], cond=z).then_inc(stored[c], 16)

                def positions(n, par):
                    more = exists(n * SUP + SUP)
                    for p in range(SUP):
                        if p == 0 and more:
                            if past(n, 1):
                                eng.wait_ge(q_ps, n * 2 * SUP)
                            load_hot(n + 1, 1 - par)
                        if p == 1 and more:
                            if past(n, 1):
                                eng.wait_ge(lmax_done, n)
                            load_lastb(n + 1, 1 - par)
                        if more:
                            eng.wait_ge(q_ps, (n * SUP + p + 1) * 2)
                            load_q3(n + 1, p)
                        i, c, _, _ = chunk(n, par, p, MERGE)
                        if exists(i):
                            store(i, c)

                load_hot(0, 0)
                load_lastb(0, 0)
                for c in range(SUP):
                    load_q3(0, c)
                run(eng, positions)
                for c in range(SUP):
                    eng.wait_ge(stored[c], NSUP * 16)

            @block.tensor
            def _(eng):

                def expand(g, c, n, par):
                    eng.wait_ge(hot_done, g + 1)
                    for half in range(2):
                        if past(g, 1):
                            eng.wait_ge(kr_sum, g * 2 + half - 1)
                        for j in range(2):
                            for m in range(3):
                                k = P * (2 * half + j)
                                mm = eng.matmul(p_r[half][:, D * j:D * j + D], hot[par][0:R64, c, C0 + k:C0 + k + P],
                                                t.rel3[:, m, :], start=(m == 0), stop=(m == 2))
                        mm.then_inc(r_ps, 1)
                        if half == 0:
                            eng.wait_ge(q3_in[c], n * 16 + 16)
                        if past(g, 1):
                            eng.wait_ge(kr_prod, g * 2 + half - 1)
                        for j in range(2):
                            for m in range(3):
                                k = P * (2 * half + j)
                                mm = eng.matmul(p_q[half][:, D * j:D * j + D], hot[par][:, c, k:k + P],
                                                q3[c][:, m, :], start=(m == 0), stop=(m == 2))
                        mm.then_inc(q_ps, 1)

                def turn_scores(u, par):
                    eng.wait_ge(scored, u * SUP + SUP)
                    if past(u, 1):
                        eng.wait_ge(lmax_done, u)
                    for j in range(4):
                        mm = eng.transpose(p_x[0:M, P * j:P * j + P],
                                           sc[par][:, j, :, :].rearrange("p c h -> p (c h)"), t.ident[:, :])
                    mm.then_inc(sc_turned, 1)

                def turn_weights(u):
                    eng.wait_ge(ex_done, u + 1)
                    eng.wait_ge(lmax_done, u + 1)
                    if past(u, 1):
                        eng.wait_ge(wgt_done, u)
                    eng.sem_inc(t.pe_on, 1)
                    for k, of in enumerate((ex, lmax)):
                        for j in range(4):
                            o = (4 * k + j) * M
                            mm = eng.transpose(p_w[:, o:o + M], of[:, P * j:P * j + P], t.ident[0:M, 0:M])
                    mm.then_inc(w_turned, 1)

                def sum_up(i, c):
                    eng.wait_ge(vs_v, i + 1)
                    eng.wait_ge(vs_w, i * 2 + 2)
                    eng.wait_ge(eh_done, i + 1)
                    if past(i, 2):
                        eng.wait_ge(add_done, i - 1)
                    for j in range(4):
                        mm = eng.matmul(p_s[c % 2][:, 0:VW + H], eh[c % 2][:, j, :], vs[c % 2][:, j, :],
                                        start=(j == 0), stop=(j == 3))
                    mm.then_inc(summed, 1)

                def positions(n, par):
                    u, softmax = n - 1, exists((n - 1) * SUP)
                    for p in range(SUP):
                        g = n * SUP + p
                        if exists(g):
                            expand(g, p, n, par)
                        if p == 0 and softmax:
                            turn_scores(u, 1 - par)
                        i, c, _, _ = chunk(n, par, p, SUM)
                        if exists(i):
                            sum_up(i, c)
                        if p == 1 and softmax:
                            turn_weights(u)
                run(eng, positions)

            @block.scalar
            def _(eng):
                act = nc.scalar.activation

                def expo(u):
                    eng.wait_ge(over, u + 1)
                    act(ex[:, :], ex[:, :], ACT.Exp).then_inc(ex_done, 1)

                def scale_v(i, c, n, par):
                    eng.wait_ge(wgt_done, n + 1)
                    if past(i, 2):
                        eng.wait_ge(summed, i - 1)
                    for j in range(4):
                        for h in range(H):
                            ins = act(vs[c % 2][:, j, 65 * h:65 * h + HD],
                                      kv[par][:, 4 * c + j, D + HD * h:D + HD * h + HD],
                                      ACT.Copy, scale=wgt[par][:, 0, j, c, h:h + 1])
                    ins.then_inc(vs_v, 1)

                def rescale(i, c):
                    b = c % 2
                    eng.wait_ge(dmax_done, i * 2 + 2)
                    if past(i, 2):
                        eng.wait_ge(acc_done, i - 1)
                    act(fac[b][:, :, :], dmax[b][:, :, :], ACT.Exp).then_inc(fac_done, 1)
                    eng.wait_ge(fac_done, i + 1)
                    for h in range(H):
                        ins = act(add[b][:, 65 * h:65 * h + 65], p_s[b][:, 65 * h:65 * h + 65], ACT.Copy,
                                  scale=fac[b][:, 1, h:h + 1])
                    ins.then_inc(add_done, 1)

                def positions(n, par):
                    for p in range(SUP):
                        prep, merge = chunk(n, par, p, PREP), chunk(n, par, p, MERGE)
                        if exists(prep[0]):
                            scale_v(*prep)
                        if exists(merge[0]):
                            rescale(*merge[:2])
                        if p == 0 and exists((n - 1) * SUP):
                            expo(n - 1)
                run(eng, positions)

            @block.vector
            def _(eng):
                v = nc.vector

                def one_hots(g, c, n, par):
                    if c == 0:
                        eng.wait_ge(hot_in[par], (n - par) * 8 + 16)
                    v.tensor_scalar(hot[par][:, c, :], hot[par][:, c, :], t.col[:, 0:1], None,
                                    ALU.is_equal).then_inc(hot_done, 1)

                def add_relation(g, c, n, par, half):
                    if half == 0:
                        eng.wait_ge(kv_in[par][c], (n - par) * 32 + 64)
                        if past(g, 1):
                            eng.wait_ge(scored, g)
                    eng.wait_ge(r_ps, g * 2 + half + 1)
                    v.tensor_tensor(kr[:, 2 * half:2 * half + 2, :],
                                    kv[par][:, 4 * c + 2 * half:4 * c + 2 * half + 2, 0:D],
                                    p_r[half][:, :].rearrange("p (j d) -> p j d", j=2), ALU.add).then_inc(kr_sum, 1)

                def times_query(g, half):
                    o = kr[:, 2 * half:2 * half + 2, :]
                    eng.wait_ge(kr_sum, g * 2 + half + 1)
                    eng.wait_ge(q_ps, g * 2 + half + 1)
                    v.tensor_tensor(o, o, p_q[half][:, :].rearrange("p (j d) -> p j d", j=2),
                                    ALU.mult).then_inc(kr_prod, 1)

                def by_head(g, c, n, par):
                    eng.wait_ge(kr_prod, g * 2 + 2)
                    if past(n, 2):
                        eng.wait_ge(sc_turned, n - 1)
                    v.tensor_reduce(sc[par][:, :, c, :], kr[:, :, :].rearrange("p j (h d) -> p j h d", h=H),
                                    AXX, ALU.add).then_inc(scored, 1)

                def scan_forwards(u, par):
                    eng.wait_ge(lastb_in[par], (u - par) * 8 + 16)
                    eng.wait_ge(sc_turned, u + 1)
                    v.tensor_tensor_scan(fmax[:, :], lastb[par][:, 0:512], p_x[0:M, :], -BIG, ALU.add,
                                         ALU.max).then_inc(scanned, 1)

                def scan_backwards(u, par):
                    eng.wait_ge(scanned, u * 2 + 1)
                    if past(u, 1):
                        eng.wait_ge(w_turned, u)
                    v.tensor_tensor_scan(smax[:, ::-1], lastb[par][:, 1:513][:, ::-1], fmax[:, ::-1], -BIG,
                                         ALU.add, ALU.max).then_inc(scanned, 1)

                def take_off_maximum(u, par):
                    eng.wait_ge(scanned, u * 2 + 2)
                    v.tensor_tensor(ex[:, :], p_x[0:M, :], smax[:, :], ALU.subtract).then_inc(over, 1)
                    v.scalar_tensor_tensor(lmax[:, :], lastb[par][:, 1:513], -1.0 / BIG, smax[:, :], ALU.mult,
                                           ALU.mult).then_inc(lmax_done, 1)

                def weights(u, par):
                    eng.wait_ge(w_turned, u + 1)
                    if past(u, 2):
                        eng.wait_ge(vs_v, u * SUP - SUP)
                        eng.wait_ge(vs_w, (u * SUP - SUP) * 2)
                    v.tensor_copy(wgt[par][:, :, :, :, :].rearrange("p k j c h -> p (k j c h)"),
                                  p_w[:, 0:8 * M]).then_inc(wgt_done, 1)

                def edge_one_hots(i, c):
                    if past(i, 2):
                        eng.wait_ge(summed, i - 1)
                    v.tensor_tensor(eh[c % 2][:, :, :], t.iota[:, :].unsqueeze(1).to_broadcast([P, 4, P]),
                                    t.node0[:, bass.ds(i * 4, 4)].unsqueeze(2).to_broadcast([P, 4, P]),
                                    ALU.is_equal).then_inc(eh_done, 1)

                def place(i, c, n, par):
                    eng.wait_ge(wgt_done, n + 1)
                    if past(i, 2):
                        eng.wait_ge(summed, i - 1)
                    o = vs[c % 2]
                    v.tensor_copy(o[:, :, 0:VW].rearrange("p j (h e) -> p j h e", h=H)[:, :, :, HD],
                                  wgt[par][:, 0, :, c, :]).then_inc(vs_w, 1)
                    v.tensor_copy(o[:, :, VW:VW + H], wgt[par][:, 1, :, c, :]).then_inc(vs_w, 1)

                def new_max(i, c, n, par, step):
                    b = c % 2
                    f = fresh[par][:, c:c + 1]
                    if step == 0:
                        if c == 0:
                            v.tensor_copy(fresh[par][:, :], t.fresh0[:, bass.ds(i, SUP)]).then_inc(fresh_in, 1)
                        eng.wait_ge(summed, i + 1)
                        if past(i, 1):
                            eng.wait_ge(cmax_done, i)
                        den = p_s[b][:, 0:VW].rearrange("p (h e) -> p h e", h=H)[:, :, HD]
                        v.tensor_scalar(absent[:, :], den, 0.5, -BIG, ALU.is_lt, ALU.mult).then_inc(marked, 1)
                    elif step == 1:
                        eng.wait_ge(marked, i + 1)
                        if past(i, 1):
                            eng.wait_ge(dmax_done, i * 2)
                        v.tensor_tensor(cmax[:, :], absent[:, :], p_s[b][:, VW:VW + H], ALU.add).then_inc(cmax_done, 1)
                    elif step == 2:
                        eng.wait_ge(cmax_done, i + 1)
                        eng.wait_ge(fresh_in, n + 1)
                        v.scalar_tensor_tensor(top[c][:, :], top[c - 1][:, :], f, cmax[:, :], ALU.add,
                                               ALU.max).then_inc(top_done, 1)
                    else:
                        eng.wait_ge(top_done, i + 1)
                        if past(i, 2):
                            eng.wait_ge(fac_done, i - 1)
                        v.scalar_tensor_tensor(dmax[b][:, 0, :], top[c - 1][:, :], f, top[c][:, :], ALU.add,
                                               ALU.subtract).then_inc(dmax_done, 1)
                        v.tensor_tensor(dmax[b][:, 1, :], cmax[:, :], top[c][:, :], ALU.subtract).then_inc(dmax_done, 1)

                def positions(n, par):
                    u, softmax = n - 1, exists((n - 1) * SUP)
                    for p in range(SUP):
                        g = n * SUP + p
                        merge, prep = chunk(n, par, p, MERGE), chunk(n, par, p, PREP)
                        score, merging, preparing = exists(g), exists(merge[0]), exists(prep[0])
                        after = chunk(n, par, p, -1)
                        if exists(after[0]):
                            one_hots(*after)
                        if score:
                            add_relation(g, p, n, par, 0)
                        if merging:
                            new_max(*merge, 0)
                        if score:
                            add_relation(g, p, n, par, 1)
                        if merging:
                            new_max(*merge, 1)
                        if score:
                            times_query(g, 0)
                        if merging:
                            new_max(*merge, 2)
                        if score:
                            times_query(g, 1)
                        if merging:
                            new_max(*merge, 3)
                        if p == 0 and preparing:
                            place(*prep)
                        if score:
                            by_head(g, p, n, par)
                        if p == 0 and softmax:
                            scan_forwards(u, 1 - par)
                        if preparing:
                            edge_one_hots(*prep[:2])
                        if p == 0 and softmax:
                            scan_backwards(u, 1 - par)
                            take_off_maximum(u, 1 - par)
                        if p == 1 and softmax:
                            weights(u, 1 - par)
                        if p != 0 and preparing:
                            place(*prep)

                v.memset(acc[SUP - 1][:, :], 0.0).then_inc(cleared, 1)
                v.memset(top[SUP - 1][:, :], 0.0).then_inc(cleared, 1)
                eng.wait_ge(cleared, 2)
                one_hots(0, 0, 0, 0)
                run(eng, positions)


def update_phase(nc, a, t):
    with ExitStack() as ctx:
        s = Scope(nc, ctx, "up")
        R = 3
        VW = H * (HD + 1)
        wo = s.sb("wo", [P, 2, D])
        gamma, beta, bo = (s.sb(n, [P, D]) for n in ("gamma", "beta", "bo"))
        eps = s.sb("eps", [P, 1])
        zero = s.sb("zero", [P, D])
        x = [s.sb(f"x{i}", [P, D]) for i in range(R)]
        vown = [s.sb(f"vown{i}", [P, D]) for i in range(R)]
        sums = [s.sb(f"sums{i}", [P, VW]) for i in range(R)]
        xb = [s.sb(f"xb{i}", [P, D]) for i in range(R)]
        none = s.sb("none", [P, H])
        den = s.sb("den", [P, H])
        rden = s.sb("rden", [P, H])
        own = s.sb("own", [P, D])
        mean = s.sb("mean", [P, D])
        msg = s.sb("msg", [P, D])
        msg_t = [s.sb(f"msg_t{i}", [P, 2, P]) for i in range(R)]
        z = s.sb("z", [P, D])
        stats = s.sb("stats", [P, 2, 6])
        mv = s.sb("mv", [P, 2, 2])
        dev = s.sb("dev", [P, 2])
        rdev = s.sb("rdev", [P, 2])
        y = [s.sb(f"y{i}", [P, D]) for i in range(R)]
        yg = s.sb("yg", [P, D])
        yb = s.sb("yb", [P, D])
        z2 = [s.sb(f"z2{i}", [P, D]) for i in range(R)]
        x1 = [s.sb(f"x1{i}", [P, D]) for i in range(R)]
        p_t = [s.ps(f"pt{i}", [P, 512]) for i in range(R)]
        p_o = [s.ps(f"po{i}", [P, 512]) for i in range(R)]

        w_in = s.sem("w_in")
        zeroed = s.sem("zeroed")
        x_in = [s.sem(f"x_in{i}") for i in range(R)]
        xb_done, msg_done, turned, out_ps, z_done, dev0, dev1 = (
            s.sem(n) for n in ("xb_done", "msg_done", "turned", "out_ps", "z_done", "dev0", "dev1"))
        row_step = s.sem("row_step")
        outer_step = s.sem("outer_step")
        msg_t_done = s.sem("msg_t_done")
        var0, var1 = s.sem("var0"), s.sem("var1")
        y_done, x1_done = s.sem("y_done"), s.sem("x1_done")
        x1_out = [s.sem(f"x1_out{i}") for i in range(R)]
        pad_out = s.sem("pad_out")

        def each(eng, body):
            for j in range(2 * R):
                body(j, j % R, j // R, P)
            with eng.Fori(2, NB // R) as k:
                for j in range(R):
                    body(k * R + j, j, k, P)
            body(NB - 1, 0, NB // R, N - (NB - 1) * P)
        assert NB % R == 1

        with nc.Block() as block:
            @block.sync
            def _(eng):
                eng.dma_start(wo[:, :, :], a["L0_gnn_Wo"].rearrange("(k p) n -> p k n", p=P)).then_inc(w_in, 16)
                for dst, name in ((gamma, "gamma"), (beta, "beta"), (bo, "bo")):
                    eng.dma_start(dst[:, :], a[f"L0_gnn_{name}"].partition_broadcast(P)).then_inc(w_in, 16)

                def store(i, b):
                    eng.wait_ge(x1_done, i * 2 + 2)
                    eng.sem_inc(t.sp_on, 1)
                    eng.dma_start(t.x1[bass.ds(i * P, P), :], x1[b][:, :]).then_inc(x1_out[b], 16)

                def tile(i, b, k, rows):
                    if past(i, R):
                        eng.wait_ge(outer_step, (i - R) * 3 + 3)
                        eng.sem_inc(t.sp_on, 1)
                        eng.wait_ge(msg_done, i - R + 1)
                        eng.sem_inc(t.sp_on, 1)
                    if rows < P:
                        eng.wait_ge(zeroed, 3)
                    eng.dma_start(x[b][0:rows, :], a["x"][bass.ds(i * P, rows), :]).then_inc(x_in[b], 16)
                    eng.dma_start(sums[b][:, :], t.sums0[bass.ds(i * P, P), :]).then_inc(x_in[b], 16)
                    eng.dma_start(vown[b][:, :], t.kv[bass.ds(i * P, P), D:2 * D]).then_inc(x_in[b], 16)
                    if past(i, R):
                        store(i - R, b)
                each(eng, tile)
                for i in range(NB - R, NB):
                    store(i, i % R)
                eng.wait_ge(zeroed, 2)
                eng.dma_start(t.x1[NB * P:NW * WN, :], zero[0:NW * WN - NB * P, :]).then_inc(pad_out, 16)
                for b in range(R):
                    eng.wait_ge(x1_out[b], 16 * ((NB + R - 1 - b) // R))
                eng.wait_ge(pad_out, 16)

            @block.gpsimd
            def _(eng):
                tt = nc.gpsimd.tensor_tensor

                def affine(i, b):
                    if past(i, 1):
                        eng.wait_ge(outer_step, i * 3 - 1)
                    eng.wait_ge(y_done, i * 2 + 2)
                    tt(yg[:, :], y[b][:, :], gamma[:, :], ALU.mult).then_inc(outer_step, 1)
                    if past(i, 1):
                        eng.wait_ge(outer_step, i * 3)
                    eng.wait_ge(outer_step, i * 3 + 1)
                    tt(yb[:, :], yg[:, :], beta[:, :], ALU.add).then_inc(outer_step, 1)
                    if past(i, R):
                        eng.wait_ge(var1, (i - R) * 2 + 1)
                        eng.wait_ge(x1_done, (i - R) * 2 + 2)
                    eng.wait_ge(outer_step, i * 3 + 2)
                    tt(z2[b][:, :], yb[:, :], x[b][:, :], ALU.add).then_inc(outer_step, 1)

                def tile(i, b, k, rows):
                    eng.wait_ge(x_in[b], k * 48 + 48)
                    if past(i, R):
                        eng.wait_ge(z_done, i - R + 1)
                    tt(xb[b][:, :], x[b][:, :], bo[:, :], ALU.add).then_inc(xb_done, 1)
                    if past(i, 1):
                        affine(i - 1, (b - 1) % R)
                eng.wait_ge(w_in, 64)
                each(eng, tile)
                affine(NB - 1, (NB - 1) % R)

            @block.tensor
            def _(eng):
                def tile(i, b, k, rows):
                    eng.wait_ge(msg_done, i + 1)
                    if past(i, R):
                        eng.wait_ge(msg_t_done, (i - R + 1) * 2)
                    for h in range(2):
                        mm = eng.transpose(p_t[b][:, P * h:P * h + P], msg[:, P * h:P * h + P], t.ident[:, :])
                    mm.then_inc(turned, 1)
                    eng.wait_ge(msg_t_done, i * 2 + 2)
                    if past(i, R):
                        eng.wait_ge(z_done, i - R + 1)
                    for h in range(2):
                        mm = eng.matmul(p_o[b][:, 0:D], msg_t[b][:, h, :], wo[:, h, :], start=(h == 0), stop=(h == 1))
                    mm.then_inc(out_ps, 1)
                eng.wait_ge(w_in, 64)
                each(eng, tile)

            @block.scalar
            def _(eng):
                act = nc.scalar.activation

                def deviation(i, m, var, done):
                    eng.wait_ge(var, i * 2 + 2)
                    act(dev[:, m:m + 1], mv[:, m, 1:2], ACT.Sqrt, bias=eps[:, 0:1]).then_inc(done, 1)

                def tile(i, b, k, rows):
                    if past(i, 2):
                        deviation(i - 2, 1, var1, dev1)
                    if past(i, 1):
                        deviation(i - 1, 0, var0, dev0)
                    eng.wait_ge(turned, i + 1)
                    if past(i, R):
                        eng.wait_ge(out_ps, i - R + 1)
                    for h in range(2):
                        act(msg_t[b][:, h, :], p_t[b][:, P * h:P * h + P], ACT.Copy).then_inc(msg_t_done, 1)
                eng.wait_ge(zeroed, 2)
                each(eng, tile)
                deviation(NB - 2, 1, var1, dev1)
                deviation(NB - 1, 0, var0, dev0)
                deviation(NB - 1, 1, var1, dev1)

            @block.vector
            def _(eng):
                v = nc.vector

                def mean_row(i, b, k):
                    by_head = sums[b][:, :].rearrange("p (h e) -> p h e", h=H)
                    if past(i, 1):
                        eng.wait_ge(msg_done, i)
                    eng.wait_ge(x_in[b], k * 48 + 48)
                    v.tensor_scalar(none[:, :], by_head[:, :, HD], 0.5, None, ALU.is_lt).then_inc(row_step, 1)
                    yield
                    eng.wait_ge(row_step, i * 5 + 1)
                    v.tensor_tensor(den[:, :], by_head[:, :, HD], none[:, :], ALU.add).then_inc(row_step, 1)
                    yield
                    eng.wait_ge(row_step, i * 5 + 2)
                    v.reciprocal(rden[:, :], den[:, :]).then_inc(row_step, 1)
                    v.tensor_scalar(own[:, :], vown[b][:, :], none[:, 0:1], None, ALU.mult).then_inc(row_step, 1)
                    yield
                    eng.wait_ge(row_step, i * 5 + 3)
                    v.tensor_tensor(mean[:, :].rearrange("p (h d) -> p h d", h=H), by_head[:, :, 0:HD],
                                    rden[:, :].unsqueeze(2).to_broadcast([P, H, HD]), ALU.mult).then_inc(row_step, 1)
                    yield
                    eng.wait_ge(row_step, i * 5 + 5)
                    eng.wait_ge(row_step, i * 5 + 4)
                    if past(i, 1):
                        eng.wait_ge(turned, i)
                    v.tensor_tensor(msg[:, :], mean[:, :], own[:, :], ALU.add).then_inc(msg_done, 1)

                def sum_rows(i, b):
                    eng.wait_ge(out_ps, i + 1)
                    eng.wait_ge(xb_done, i + 1)
                    if past(i, 1):
                        eng.wait_ge(y_done, i * 2)
                    v.tensor_tensor(z[:, :], p_o[b][:, 0:D], xb[b][:, :], ALU.add).then_inc(z_done, 1)

                def moments(i, m, of, of_done, of_count):
                    eng.wait_ge(of_done, of_count)
                    if past(i, 1):
                        eng.wait_ge((var0, var1)[m], i * 2)
                    v.bn_stats(stats[:, m, :], of[:, :]).then_inc((var0, var1)[m], 1)

                def variance(i, m, last_used):
                    if past(i, 1):
                        eng.wait_ge(last_used, i * 2)
                    eng.wait_ge((var0, var1)[m], i * 2 + 1)
                    eng.sem_inc(t.dve_on, 1)
                    v.bn_aggr(mv[:, m, :], stats[:, m, :]).then_inc((var0, var1)[m], 1)

                def norm(i, m, out, of, dev_done, done):
                    eng.wait_ge(dev_done, i + 1)
                    if past(i, 1):
                        eng.wait_ge(done, i * 2)
                    v.reciprocal(rdev[:, m:m + 1], dev[:, m:m + 1]).then_inc(done, 1)
                    yield
                    eng.wait_ge(done, i * 2 + 1)
                    v.tensor_scalar(out[:, :], of[:, :], mv[:, m, 0:1], rdev[:, m:m + 1], ALU.subtract,
                                    ALU.mult).then_inc(done, 1)

                def stages(i, b, k, mean, first, second):
                    b1, b2 = (b - 1) % R, (b - 2) % R
                    row = mean_row(i, b, k) if mean else iter(())
                    if second:
                        moments(i - 2, 1, z2[b2], outer_step, i * 3 - 3)
                    next(row, None)
                    if first:
                        sum_rows(i - 1, b1)
                    next(row, None)
                    if second:
                        variance(i - 2, 1, x1_done)
                    if first:
                        moments(i - 1, 0, z, z_done, i)
                    next(row, None)
                    if first:
                        variance(i - 1, 0, y_done)
                    next(row, None)
                    if past(i - 2, R) and second:
                        eng.wait_ge(x1_out[b2], slot_uses(i, k, b) * 16)
                    last = norm(i - 2, 1, x1[b2], z2[b2], dev1, x1_done) if second else iter(())
                    next(last, None)
                    next(row, None)
                    if past(i - 1, R) and first:
                        eng.wait_ge(outer_step, (i - 1 - R) * 3 + 1)
                    mid = norm(i - 1, 0, y[b1], z, dev0, y_done) if first else iter(())
                    next(mid, None)
                    next(last, None)
                    next(mid, None)

                def slot_uses(i, k, b):
                    return k if b == 2 else k - 1

                def tile(i, b, k, rows):
                    if rows < P:
                        eng.wait_ge(outer_step, (i - R) * 3 + 3)
                        v.memset(x[b][:, :], 0.0).then_inc(zeroed, 1)
                    stages(i, b, k, True, past(i, 1), past(i, 2))

                v.memset(eps[:, :], EPS).then_inc(zeroed, 1)
                v.memset(zero[:, :], 0.0).then_inc(zeroed, 1)
                eng.wait_ge(w_in, 64)
                each(eng, tile)
                stages(NB, NB % R, NB // R, False, True, True)
                stages(NB + 1, (NB + 1) % R, (NB + 1) // R, False, False, True)


def relate_phase(nc, a, t):
    with ExitStack() as ctx:
        s = Scope(nc, ctx, "re")
        GS = 8
        R = 3
        WA = 2 * WR + WR
        src = s.sb("src", [P, G1 * P], I32)
        row = s.sb("row", [P, G1 * P])
        keep = s.sb("keep", [P, G1 * P])
        win = s.sb("win", [1, G1 * P], I32)
        last = s.sb("last", [1, G1 * P], I32)
        idx = [s.sb(f"idx{i}", [P, GS], I32) for i in range(R)]
        kp = [s.sb(f"kp{i}", [P, GS]) for i in range(R)]
        xg = [s.sb(f"xg{i}", [P, GS, D]) for i in range(R)]
        oh = [s.sb(f"oh{i}", [P, GS, WR]) for i in range(R)]
        acc = [s.sb(f"acc{i}", [P, WA]) for i in range(GS)]
        p_a = [s.ps(f"pa{i}", [P, 512]) for i in range(4)]

        tables_in = s.sem("tables_in")
        idx_set = s.sem("idx_set")
        x_in = [[s.sem(f"x_in{i}{g}") for g in range(2)] for i in range(R)]
        hot = s.sem("hot")
        kept = s.sem("kept")
        summed = s.sem("summed")
        acc_done = s.sem("acc_done")
        stored = [s.sem(f"stored{i}") for i in range(GS)]
        acc_zero = s.sem("acc_zero")

        def each(eng, body):
            for j in range(R):
                body(j, j, 0, True)
            with eng.Fori(1, K1 // GS // R) as k:
                for j in range(R):
                    body(k * R + j, j, k, False)
        assert K1 % (GS * R) == 0

        def store(eng, n, odd):
            for g in range(odd, GS, 2):
                w = eng.value_load(win[0:1, bass.ds(n * GS + g, 1)], min_val=0, max_val=NW - 1)
                z = eng.value_load(last[0:1, bass.ds(n * GS + g, 1)], min_val=0, max_val=1)
                eng.wait_ge(acc_done, n * GS + g + 1)
                eng.dma_start(t.agg[bass.ds(w * P, P), :], acc[g][:, :], cond=z).then_inc(stored[g], 16)

        with nc.Block() as block:
            @block.gpsimd
            def _(eng):
                def gather(n, par, k, first):
                    eng.wait_ge(idx_set, n + 1)
                    eng.sem_inc(t.pool_on, 1)
                    for g in range(GS):
                        if g % 4 == 0 and not first:
                            eng.wait_ge(summed, (n - R) * GS + g + 4)
                            eng.sem_inc(t.pool_on, 1)
                        eng.indirect_dma_start(
                            out=xg[par][:, g, :], out_offset=None, in_=t.x1,
                            in_offset=bass.IndirectOffsetOnAxis(ap=idx[par][:, g:g + 1], axis=0),
                        ).then_inc(x_in[par][g // 4], 16)
                eng.wait_ge(tables_in, 16 * 5)
                each(eng, gather)

            @block.tensor
            def _(eng):
                def sums(n, par, k, first):
                    eng.wait_ge(hot, n + 1)
                    for g in range(GS):
                        i = n * GS + g
                        if g % 4 == 0:
                            eng.wait_ge(x_in[par][g // 4], k * 64 + 64)
                        if not (first and par == 0 and g < 4):
                            eng.wait_ge(acc_done, i - 3)
                        o = p_a[g % 4]
                        for half in range(2):
                            eng.matmul(o[:, WR * half:WR * half + WR], xg[par][:, g, P * half:P * half + P], oh[par][:, g, :],
                                       start=True, stop=True)
                        eng.matmul(o[:, 2 * WR:WA], t.ones[:, :], oh[par][:, g, :],
                                   start=True, stop=True).then_inc(summed, 1)
                each(eng, sums)

            @block.vector
            def _(eng):
                v = nc.vector

                def one_hots(n, par, first):
                    if not first:
                        eng.wait_ge(summed, (n - R + 1) * GS)
                    v.tensor_tensor(oh[par][:, :, :], t.iota[:, 0:WR].unsqueeze(1).to_broadcast([P, GS, WR]),
                                    row[:, bass.ds(n * GS, GS)].unsqueeze(2).to_broadcast([P, GS, WR]),
                                    ALU.is_equal).then_inc(hot, 1)

                def set_rows(n, par):
                    v.tensor_copy(idx[par][:, :], src[:, bass.ds(n * GS, GS)]).then_inc(idx_set, 1)

                def group(n, par, k, first):
                    if par == 0 and first:
                        one_hots(0, 0, True)
                    one_hots(n + 1, (par + 1) % R, first and par < R - 1)
                    if not first:
                        eng.wait_ge(acc_done, (n - R + 1) * GS)
                    v.tensor_copy(kp[par][:, :], keep[:, bass.ds(n * GS, GS)]).then_inc(kept, 1)
                    eng.wait_ge(kept, n + 1)
                    for g in range(GS):
                        i = n * GS + g
                        eng.wait_ge(summed, i + 1)
                        if not (first and par == 0):
                            eng.wait_ge(stored[g], n * 16)
                        if not (first and par == 0 and g == 0):
                            eng.wait_ge(acc_done, i)
                        v.scalar_tensor_tensor(acc[g][:, :], acc[(g - 1) % GS][:, :], kp[par][:, g:g + 1],
                                               p_a[g % 4][:, 0:WA], ALU.mult, ALU.add).then_inc(acc_done, 1)
                    eng.wait_ge(x_in[par][1], k * 64 + 64)
                    eng.sem_inc(t.dve_on, 1)
                    set_rows(n + R, par)
                eng.wait_ge(tables_in, 16 * 5)
                v.memset(acc[GS - 1][:, :], 0.0).then_inc(acc_zero, 1)
                eng.wait_ge(acc_zero, 1)
                for j in range(R):
                    set_rows(j, j)
                each(eng, group)

            @block.sync
            def _(eng):
                for j, of in enumerate((src, row, keep, win, last)):
                    eng.dma_start(of[:, :], t.tables1[j][:, :]).then_inc(tables_in, 16)
                eng.wait_ge(tables_in, 16 * 5)

                each(eng, lambda n, par, k, first: store(eng, n, 0))
                for g in range(0, GS, 2):
                    eng.wait_ge(stored[g], K1 // GS * 16)

            @block.scalar
            def _(eng):
                eng.wait_ge(tables_in, 16 * 5)
                each(eng, lambda n, par, k, first: store(eng, n, 1))
                for g in range(1, GS, 2):
                    eng.wait_ge(stored[g], K1 // GS * 16)


def mix_phase(nc, a, out, t):
    with ExitStack() as ctx:
        s = Scope(nc, ctx, "mx")
        SN = SBW * WN
        SR = SBW * WR
        QP = 4 * WR
        HH = SN // 2
        w = s.sb("w", [P, R6, 2, D])
        wrow = s.sb("wrow", [P, 10, D])
        wt = s.sb("wt", [P, 2, 10, P])
        b_in = s.sb("b_in", [P, R6, 2])
        qkv_b = s.sb("qkv_b", [P, 6])
        out_b = s.sb("out_b", [P, 2])
        proj_b = s.sb("proj_b", [P, D])
        eps = s.sb("eps", [P, 1])
        one = s.sb("one", [WR, WN])
        member0 = s.sb("member0", [WR, WN])
        member = s.sb("member", [WR, WN])
        member6 = s.sb("member6", [WR, WN])
        member_t = s.sb("member_t", [WN, WR])
        same = s.sb("same", [WR, WR])
        mask = s.sb("mask", [WR, 2 * WR], BF16)
        agg = [s.sb(f"agg{i}", [P, SBW, 3 * WR]) for i in range(2)]
        x1 = [s.sb(f"x1{i}", [HH, 2, D]) for i in range(2)]
        xb = [s.sb(f"xb{i}", [HH, 2, D]) for i in range(2)]
        st = s.sb("st", [P, 2, SR])
        qk = s.sb("qk", [P, 4, SR])
        top = [s.sb(f"top{i}", [WR, H]) for i in range(2)]
        ntop = [s.sb(f"ntop{i}", [WR, H]) for i in range(2)]
        pr = [s.sb(f"pr{i}", [WR, H, WR]) for i in range(4)]
        den = [s.sb(f"den{i}", [WR, H]) for i in range(4)]
        rden = [s.sb(f"rden{i}", [WR, H]) for i in range(4)]
        gd = [s.sb(f"gd{i}", [WR, H, WN]) for i in range(4)]
        gt = [s.sb(f"gt{i}", [WR, H * WN]) for i in range(2)]
        srow = [s.sb(f"srow{i}", [WR, D]) for i in range(6)]
        ut = s.sb("ut", [P, 2, H, SN])
        att = s.sb("att", [P, 2, SN])
        hid = s.sb("hid", [P, 2, SN])
        z = s.sb("z", [HH, 2, D])
        stats = s.sb("stats", [HH, 2, 6])
        mv = s.sb("mv", [HH, 2, 2])
        dev = s.sb("dev", [HH, 2])
        rdev = s.sb("rdev", [HH, 2])
        y = [s.sb(f"y{i}", [HH, 2, D]) for i in range(2)]
        p_g = [s.ps(f"pg{i}", [P, 512]) for i in range(2)]
        p_qk = [s.ps(f"pqk{i}", [P, 512]) for i in range(2)]
        p_sc = [[s.ps(f"psc{i}", [P, 512]) for i in range(2)], p_qk]
        p_gt = s.ps("pgt", [P, 512])
        p_u = s.ps("pu", [P, 512])

        w_in = s.sem("w_in")
        made = s.sem("made")
        mask_step = s.sem("mask_step")
        mask_ps = s.sem("mask_ps")
        wt_ps = s.sem("wt_ps")
        wt_done = s.sem("wt_done")
        agg_in = [s.sem(f"agg_in{i}") for i in range(2)]
        xb_done = s.sem("xb_done")
        g_ps = s.sem("g_ps")
        g_done = s.sem("g_done")
        qk_ps = s.sem("qk_ps")
        qk_done = s.sem("qk_done")
        sc_ps = s.sem("sc_ps")
        top_done = s.sem("top_done")
        ntop_done = s.sem("ntop_done")
        pr_done = s.sem("pr_done")
        rden_done = s.sem("rden_done")
        gd_done = s.sem("gd_done")
        row_ps = s.sem("row_ps")
        row_done = s.sem("row_done")
        gt_ps = s.sem("gt_ps")
        gt_done = s.sem("gt_done")
        u_ps = s.sem("u_ps")
        u_done = s.sem("u_done")
        stat = s.sem("stat")
        aggr = s.sem("aggr")
        dev_done = s.sem("dev_done")
        rdev_done = s.sem("rdev_done")
        y_done = s.sem("y_done")
        y_out = [s.sem(f"y_out{i}") for i in range(2)]

        NG = 2 * R6
        NT = NG + 6
        W_LOADS = 7
        plan = ([("sum", k) for k in range(6)] + [("att", 0), ("att", 1)] + [("sum", k) for k in range(6, 8)] +
                [("hid", 0), ("hid", 1)] + [("sum", k) for k in range(8, NG)] + [("y", 0), ("y", 1)])

        def qk_bank(j):
            return p_qk[j % 2] if j < 4 else (p_g[1], p_u)[j % 2]

        def products(i, first):
            if first:
                return [(k, "sum", k) for k in range(NG)]
            return [(i * NT - 6 + k, kind, j) for k, (kind, j) in enumerate(plan)]

        def nodes_last():
            rest = [p for p in plan if p[0] != "sum"]
            return [(NSB * NT - 6 + k, kind, j) for k, (kind, j) in enumerate(rest)]

        def each(eng, body):
            for i in range(4):
                body(i, i % 2, i == 0)
            with eng.Fori(2, NSB // 2) as k:
                body(k * 2, 0, False)
                body(k * 2 + 1, 1, False)
            body(NSB - 1, 0, False)
        assert NSB % 2 == 1

        with nc.Block() as block:
            @block.sync
            def _(eng):
                eng.dma_start(w[:, :, :, :].rearrange("p r k n -> p (r k) n"),
                              a["L1_gnn_W"].rearrange("r (k p) n -> p (r k) n", p=P)).then_inc(w_in, 16)
                for o, n, name in ((0, 6, "in_proj_w"), (6, 2, "attn_out_w"), (8, 2, "proj_w")):
                    eng.dma_start(wrow[:, o:o + n, :], a[f"L1_gnn_{name}"].rearrange("(k p) n -> p k n", p=P)
                                  ).then_inc(w_in, 16)
                eng.dma_start(qkv_b[:, :], a["L1_gnn_in_proj_b"].rearrange("(k p) -> p k", p=P),
                              allow_slow_non_contiguous=True).then_inc(w_in, 16)
                eng.dma_start(out_b[:, :], a["L1_gnn_attn_out_b"].rearrange("(k p) -> p k", p=P),
                              allow_slow_non_contiguous=True).then_inc(w_in, 16)
                eng.dma_start(proj_b[:, :], a["L1_gnn_proj_b"].partition_broadcast(P)).then_inc(w_in, 16)
                for r in range(R6):
                    eng.dma_start(b_in[:, r, :], a["L1_gnn_b"][r, :].rearrange("(k p) -> p k", p=P),
                                  allow_slow_non_contiguous=True).then_inc(w_in, 16)

                def store(i, par):
                    eng.wait_ge(y_done, i * 2 + 2)
                    full = not (past(i, NSB - 1) and isinstance(i, int))
                    for half in range(2):
                        rows = HH if full else min(HH, N - i * SN - half * HH)
                        eng.dma_start(out[bass.ds(i * SN + half * HH, rows), :],
                                      y[par][0:rows, half, :]).then_inc(y_out[par], 16)

                def load(i, par, first):
                    if past(i, 2):
                        eng.wait_ge(g_ps, i * NT - NG)
                        eng.wait_ge(xb_done, i * 2 - 2)
                    eng.dma_start(agg[par][:, :, :], t.agg[bass.ds(i * (SBW * P), SBW * P), :].rearrange(
                        "(w p) c -> p w c", p=P)).then_inc(agg_in[par], 16)
                    eng.dma_start(x1[par][:, :, :], t.x1[bass.ds(i * SN, SN), :].rearrange("(h p) c -> p h c", p=HH)
                                  ).then_inc(agg_in[par], 16)
                    if past(i, 2):
                        store(i - 2, par)
                each(eng, load)
                store(NSB - 2, 1)
                store(NSB - 1, 0)
                for par in range(2):
                    eng.wait_ge(y_out[par], 32 * ((NSB + 1 - par) // 2))

            @block.gpsimd
            def _(eng):
                eng.memset(one[:, :], 1.0).then_inc(made, 1)
                eng.wait_ge(made, 1)
                eng.affine_select(member0[:, :], one[:, :], [[-R6, WN]], ALU.is_ge, 0.0, base=0,
                                  channel_multiplier=1).then_inc(made, 1)
                eng.wait_ge(made, 2)
                eng.affine_select(member[:, :], member0[:, :], [[R6, WN]], ALU.is_ge, 0.0, base=R6 - 1,
                                  channel_multiplier=-1).then_inc(made, 1)
                eng.wait_ge(w_in, 16 * (W_LOADS + R6))

                def add_bias(i, par, first):
                    eng.wait_ge(agg_in[par], (i - par) * 16 + 32)
                    if past(i, 2):
                        eng.wait_ge(g_done, (i - 1) * NT - 6 + NT)
                    for half in range(2):
                        nc.gpsimd.tensor_tensor(xb[par][:, half, :], x1[par][:, half, :], proj_b[0:HH, :],
                                                ALU.add).then_inc(xb_done, 1)
                each(eng, add_bias)

            @block.tensor
            def _(eng):
                eng.wait_ge(w_in, 16 * (W_LOADS + R6))
                for o in range(10):
                    if o >= 2:
                        eng.wait_ge(wt_done, o - 1)
                    for k in range(2):
                        mm = eng.transpose(p_g[o % 2][:, P * k:P * k + P], wrow[:, o, P * k:P * k + P], t.ident[:, :])
                    mm.then_inc(wt_ps, 1)
                eng.wait_ge(made, 3)
                eng.transpose(p_sc[0][0][0:WN, 0:WR], member[:, :], t.ident[0:WR, 0:WR]).then_inc(mask_ps, 1)
                eng.wait_ge(mask_step, 1)
                eng.matmul(p_sc[0][1][0:WR, 0:WR], member_t[:, :], member_t[:, :], start=True,
                           stop=True).then_inc(mask_ps, 1)
                eng.wait_ge(mask_step, 4)
                eng.wait_ge(wt_done, 10)

                def product(i, par, n, kind, j, first, between=4):
                    o = p_g[j % 2]
                    if kind == "sum" and j < 2:
                        if not first:
                            eng.wait_ge(*((row_done, i * SBW) if j == 0 else (qk_done, i * 12)))
                    else:
                        eng.wait_ge(g_done, n - 1)
                    if kind == "sum":
                        r, half = j // 2, j % 2
                        for k in range(2):
                            mm = eng.matmul(o[:, 0:SN], w[:, r, k, P * half:P * half + P],
                                            agg[par][:, :, k * WR + r:(k + 1) * WR:R6], start=(k == 0), stop=(k == 1))
                    elif kind == "att":
                        for e in range(2):
                            for k in range(2):
                                mm = eng.matmul(o[HD * e:HD * e + HD, 0:SN], wt[:, k, 4 + j, HD * e:HD * e + HD],
                                                ut[:, k, 2 * j + e, :], start=(k == 0), stop=(k == 1))
                    elif kind == "hid":
                        if j == 0:
                            eng.wait_ge(g_done, n - between // 2)
                        for k in range(2):
                            eng.matmul(o[:, 0:SN], wt[:, k, 6 + j, :], att[:, k, :], start=(k == 0), stop=False)
                        for half in range(2):
                            mm = eng.matmul(o[:, HH * half:HH * half + HH], x1[1 - par][:, half, P * j:P * j + P],
                                            t.ident[0:HH, 0:HH], start=False, stop=(half == 1))
                    else:
                        if j == 0:
                            eng.wait_ge(g_done, n - between)
                        for k in range(2):
                            mm = eng.matmul(o[0:HH, 0:D], hid[:, k, HH * j:HH * j + HH],
                                            wt[:, k, 8:10, :].rearrange("p o c -> p (o c)"),
                                            start=(k == 0), stop=(k == 1))
                    mm.then_inc(g_ps, 1)

                def queries_keys(i, j):
                    c, piece = j % 4, j // 4
                    if j in (2, 3) or j >= 6:
                        eng.wait_ge(qk_done, i * 12 + j - 1)
                    for k in range(2):
                        mm = eng.matmul(qk_bank(j)[:, 0:QP], wt[:, k, c, :],
                                        st[:, k, QP * piece:QP * piece + QP], start=(k == 0), stop=(k == 1))
                    mm.then_inc(qk_ps, 1)

                def scores(v, x):
                    if past(v, 2):
                        eng.wait_ge(pr_done, v - 1)
                    for e in range(2):
                        eng.matmul(p_sc[e][x % 2][0:WR, 0:2 * WR], t.ident_b[0:WR, 0:WR], mask[:, :],
                                   start=True, stop=False)
                    for b in range(2):
                        for e in range(2):
                            rows = slice(HD * e, HD * e + HD)
                            eng.matmul(p_sc[e][x % 2][0:WR, WR * b:WR * b + WR], qk[rows, b, WR * x:WR * x + WR],
                                       qk[rows, 2 + b, WR * x:WR * x + WR], start=False, stop=(b == 1)
                                       ).then_inc(sc_ps, 1)
                    if past(v, 1):
                        eng.wait_ge(row_done, v)
                    for k in range(2):
                        mm = eng.transpose(p_g[0][0:WR, P * k:P * k + P], st[:, k, WR * x:WR * x + WR],
                                           t.ident[:, :])
                    mm.then_inc(row_ps, 1)

                def weigh(v, x, h):
                    if h == 0:
                        eng.wait_ge(gd_done, v + 1)
                        if past(v, 1):
                            eng.wait_ge(gt_done, v)
                    mm = eng.matmul(p_gt[0:WR, WN * h:WN * h + WN], pr[x % 4][:, h, :], gd[x % 4][:, h, :],
                                    start=True, stop=True)
                    if h == H - 1:
                        mm.then_inc(gt_ps, 1)

                def gather(v, x):
                    eng.wait_ge(gt_done, v + 1)
                    eng.wait_ge(row_done, v + 1)
                    if past(v, 1):
                        eng.wait_ge(u_done, v)
                    for k in range(2):
                        mm = eng.matmul(p_u[:, H * WN * k:H * WN * k + H * WN], srow[x % 6][:, P * k:P * k + P], gt[x % 2][:, :],
                                        start=True, stop=True)
                    mm.then_inc(u_ps, 1)

                def superblock(i, par, first):
                    eng.wait_ge(agg_in[par], (i - par) * 16 + 32)
                    for n, kind, j in products(i, first):
                        product(i, par, n, kind, j, first)
                        if not first and kind == "sum" and j < 4:
                            for h in range(H if j < 3 else 0):
                                weigh(i * SBW - 3 + j, SBW - 3 + j, h)
                            gather(i * SBW - 4 + j, SBW - 4 + j)
                        if not first and kind == "sum" and j == 4:
                            eng.wait_ge(u_done, i * SBW)
                    eng.wait_ge(g_done, NG if first else i * NT - 6 + NT - 2)
                    for j in range(4):
                        queries_keys(i, j)
                    eng.wait_ge(qk_done, i * 12 + 4)
                    eng.wait_ge(g_done, NG if first else i * NT - 6 + NT)
                    for x in range(SBW):
                        if x == 4:
                            eng.wait_ge(qk_done, i * 12 + 8)
                        if x < 4:
                            queries_keys(i, 4 + 2 * x)
                        scores(i * SBW + x, x)
                        if x < 4:
                            queries_keys(i, 5 + 2 * x)
                        for h in range(H if x >= 3 else 0):
                            weigh(i * SBW + x - 3, x - 3, h)
                        if x == 4:
                            eng.wait_ge(qk_done, i * 12 + 12)
                        if x >= 4:
                            gather(i * SBW + x - 4, x - 4)

                each(eng, superblock)
                for j in range(4):
                    for h in range(H if j < 3 else 0):
                        weigh(NSB * SBW - 3 + j, SBW - 3 + j, h)
                    gather(NSB * SBW - 4 + j, SBW - 4 + j)
                eng.wait_ge(u_done, NSB * SBW)
                for n, kind, j in nodes_last():
                    product(NSB, 1, n, kind, j, False, between=0)

            @block.scalar
            def _(eng):
                act = nc.scalar.activation

                def copy_gt(v, x):
                    eng.wait_ge(gt_ps, v + 1)
                    if past(v, 2):
                        eng.wait_ge(u_ps, v - 1)
                    act(gt[x % 2][:, :], p_gt[0:WR, 0:H * WN], ACT.Copy).then_inc(gt_done, 1)

                def copy_u(v, x):
                    eng.wait_ge(u_ps, v + 1)
                    act(ut[:, :, :, WN * x:WN * x + WN],
                        p_u[:, 0:2 * H * WN].rearrange("p (k h n) -> p k h n", k=2, h=H),
                        ACT.Copy).then_inc(u_done, 1)

                def copy_qk(i, j):
                    c, piece = j % 4, j // 4
                    eng.wait_ge(qk_ps, i * 12 + j + 1)
                    act(qk[:, c, QP * piece:QP * piece + QP], qk_bank(j)[:, 0:QP], ACT.Identity,
                        bias=qkv_b[:, c:c + 1]).then_inc(qk_done, 1)

                def last_windows(i):
                    for j in range(4):
                        if j < 3:
                            copy_gt(i * SBW - 3 + j, SBW - 3 + j)
                        copy_u(i * SBW - 4 + j, SBW - 4 + j)

                def deviations(i):
                    eng.wait_ge(aggr, i * 2)
                    act(dev[:, :], mv[:, :, 1], ACT.Sqrt, bias=eps[0:HH, 0:1]).then_inc(dev_done, 1)

                def superblock(i, par, first):
                    if not first:
                        last_windows(i)
                    for j in range(4):
                        copy_qk(i, j)
                    if not first:
                        deviations(i)
                    for x in range(SBW):
                        v = i * SBW + x
                        if x < 4:
                            copy_qk(i, 4 + 2 * x)
                        eng.wait_ge(ntop_done, v + 1)
                        if past(v, 4):
                            eng.wait_ge(gt_ps, v - 3)
                            eng.wait_ge(rden_done, v - 3)
                        for h in range(H):
                            ins = act(pr[x % 4][:, h, :], p_sc[h % 2][x % 2][0:WR, WR * (h // 2):WR * (h // 2) + WR], ACT.Exp,
                                      bias=ntop[x % 2][:, h:h + 1], scale=HD ** -0.5,
                                      accum_out=den[x % 4][:, h:h + 1])
                        ins.then_inc(pr_done, 1)
                        if x < 4:
                            copy_qk(i, 5 + 2 * x)
                        if x >= 3:
                            copy_gt(v - 3, x - 3)
                        if x >= 4:
                            copy_u(v - 4, x - 4)

                eng.wait_ge(mask_step, 4)
                each(eng, superblock)
                last_windows(NSB)
                deviations(NSB)

            @block.vector
            def _(eng):
                v_ = nc.vector
                for o in range(10):
                    eng.wait_ge(wt_ps, o + 1)
                    v_.tensor_copy(wt[:, :, o, :], p_g[o % 2][:, 0:D].rearrange("p (k c) -> p k c", k=2)
                                   ).then_inc(wt_done, 1)
                eng.wait_ge(mask_ps, 1)
                v_.memset(eps[:, :], EPS)
                v_.tensor_scalar(member6[:, :], member[:, :], 1.0 / R6, None, ALU.mult)
                v_.tensor_copy(member_t[:, :], p_sc[0][0][0:WN, 0:WR]).then_inc(mask_step, 1)
                eng.wait_ge(mask_ps, 2)
                v_.tensor_scalar(same[:, :], p_sc[0][1][0:WR, 0:WR], -1.0, BIG, ALU.add, ALU.mult).then_inc(mask_step, 1)
                eng.wait_ge(mask_step, 2)
                for h in range(2):
                    v_.tensor_copy(mask[:, WR * h:WR * h + WR], same[:, :]).then_inc(mask_step, 1)

                def take(i, par, n, kind, j):
                    o = p_g[j % 2]
                    eng.wait_ge(g_ps, n + 1)
                    if kind == "sum":
                        r, half = j // 2, j % 2
                        ins = v_.scalar_tensor_tensor(
                            st[:, half, r:SR:R6].rearrange("p (w n) -> p w n", w=SBW), agg[par][:, :, 2 * WR + r:3 * WR:R6],
                            b_in[:, r, half:half + 1], o[:, 0:SN].rearrange("p (w n) -> p w n", w=SBW),
                            ALU.mult, ALU.add)
                    elif kind == "att":
                        ins = v_.tensor_scalar(att[:, j, :], o[:, 0:SN], qkv_b[:, 4 + j:5 + j], None, ALU.add)
                    elif kind == "hid":
                        ins = v_.tensor_scalar(hid[:, j, :], o[:, 0:SN], out_b[:, j:j + 1], None, ALU.add)
                    else:
                        if j == 0:
                            eng.wait_ge(xb_done, i * 2)
                            if past(i, 2):
                                eng.wait_ge(y_done, i * 2 - 2)
                        ins = v_.tensor_tensor(z[:, j, :], o[0:HH, 0:D], xb[1 - par][:, j, :], ALU.add)
                    ins.then_inc(g_done, 1)

                def moments(i, n):
                    for half in range(2):
                        eng.wait_ge(g_done, n + half)
                        if half == 0 and past(i, 2):
                            eng.wait_ge(aggr, i * 2 - 2)
                        v_.bn_stats(stats[:, half, :], z[:, half, :]).then_inc(stat, 1)
                    for half in range(2):
                        eng.wait_ge(stat, i * 2 - 1 + half)
                        if half == 0 and past(i, 2):
                            eng.wait_ge(y_done, i * 2 - 2)
                        eng.sem_inc(t.dve_on, 1)
                        v_.bn_aggr(mv[:, half, :], stats[:, half, :]).then_inc(aggr, 1)

                def norm(i, par):
                    eng.wait_ge(dev_done, i)
                    v_.reciprocal(rdev[:, :], dev[:, :]).then_inc(rdev_done, 1)
                    eng.wait_ge(rdev_done, i)
                    if past(i, 3):
                        eng.wait_ge(y_out[par], (i - 1 - par) * 16)
                    for half in range(2):
                        v_.tensor_scalar(y[par][:, half, :], z[:, half, :], mv[:, half, 0:1], rdev[:, half:half + 1],
                                         ALU.subtract, ALU.mult).then_inc(y_done, 1)

                def maxima(v, x):
                    eng.wait_ge(sc_ps, v * 4 + 4)
                    if past(v, 2):
                        eng.wait_ge(ntop_done, v - 1)
                    for e in range(2):
                        v_.tensor_reduce(top[x % 2][:, e:H:2],
                                         p_sc[e][x % 2][0:WR, 0:2 * WR].rearrange("p (b m) -> p b m", b=2),
                                         AXX, ALU.max).then_inc(top_done, 1)

                def over(v, x):
                    eng.wait_ge(top_done, v * 2 + 2)
                    if past(v, 2):
                        eng.wait_ge(pr_done, v - 1)
                    v_.tensor_scalar(ntop[x % 2][:, :], top[x % 2][:, :], -HD ** -0.5, None,
                                     ALU.mult).then_inc(ntop_done, 1)

                def rows(v, x):
                    eng.wait_ge(row_ps, v + 1)
                    if past(v, 6):
                        eng.wait_ge(u_ps, v - 5)
                    v_.tensor_copy(srow[x % 6][:, :], p_g[0][0:WR, 0:D]).then_inc(row_done, 1)

                def shares(v, x):
                    eng.wait_ge(pr_done, v + 1)
                    v_.reciprocal(rden[x % 4][:, :], den[x % 4][:, :]).then_inc(rden_done, 1)
                    eng.wait_ge(rden_done, v + 1)
                    if past(v, 4):
                        eng.wait_ge(gt_ps, v - 3)
                    v_.tensor_tensor(gd[x % 4][:, :, :], member6[:, :].unsqueeze(1).to_broadcast([WR, H, WN]),
                                     rden[x % 4][:, :].unsqueeze(2).to_broadcast([WR, H, WN]),
                                     ALU.mult).then_inc(gd_done, 1)

                def superblock(i, par, first):
                    eng.wait_ge(agg_in[par], (i - par) * 16 + 32)
                    for n, kind, j in products(i, first):
                        take(i, par, n, kind, j)
                    if not first:
                        moments(i, i * NT - 6 + NT - 1)
                    for x in range(SBW):
                        v = i * SBW + x
                        maxima(v, x)
                        over(v, x)
                        if x >= 1:
                            shares(v - 1, x - 1)
                        rows(v, x)
                        if x == 2 and not first:
                            norm(i, 1 - par)
                    shares(i * SBW + SBW - 1, SBW - 1)

                each(eng, superblock)
                for n, kind, j in nodes_last():
                    take(NSB, 1, n, kind, j)
                moments(NSB, NSB * NT - 6 + 5)
                norm(NSB, 0)


class Tensors:
    pass


def resnorm_gnn(nc, a, out):
    with ExitStack() as ctx:
        s = Scope(nc, ctx, "g")
        t = Tensors()
        t.pads = {n: nc.dram_tensor(f"pad_{n}", [EPAD], I32, kind="Internal").ap()
                  for n in ("src", "dst", "edge_type_6", "edge_type_64")}
        t.lastb = nc.dram_tensor("lastb", [G0 * P, H, 514], F32, kind="Internal").ap()
        t.kv = nc.dram_tensor("kv_rows", [NB * P, 2 * D], F32, kind="Internal").ap()
        t.rows0 = nc.dram_tensor("rows0", [G0 * P, 2 * C0], BF16, kind="Internal").ap()
        t.sums0 = nc.dram_tensor("sums0", [NB * P, H * (HD + 1)], F32, kind="Internal").ap()
        t.q3 = nc.dram_tensor("q3_rows", [NB * P, 3 * D], BF16, kind="Internal").ap()
        t.tables1 = [nc.dram_tensor(f"tables1_{k}", [P if k < 3 else 1, G1 * P], dt, kind="Internal").ap()
                     for k, dt in enumerate((I32, F32, F32, I32, I32))]
        t.x1 = nc.dram_tensor("x1_rows", [NW * WN, D], F32, kind="Internal").ap()
        t.agg = nc.dram_tensor("agg_t", [NW * P, 3 * WR], F32, kind="Internal").ap()
        t.iota_i = s.sb("iota_i", [P, P], I32)
        t.iota = s.sb("iota", [P, P])
        t.col = s.sb("col", [P, 1])
        t.ident = s.sb("ident", [P, P])
        t.ident_b = s.sb("ident_b", [P, P], BF16)
        t.ones = s.sb("ones", [P, P])
        t.pool_on, t.pe_on, t.dve_on, t.sp_on = (s.sem(n) for n in ("pool_on", "pe_on", "dve_on", "sp_on"))
        with ExitStack() as layer0:
            s0 = Scope(nc, layer0, "g0")
            t.src0 = s0.sb("src0", [P, G0 * P * 4], I32)
            t.node0 = s0.sb("node0", [P, G0 * P * 4])
            t.blk = s0.sb("blk", [1, G0 * P], I32)
            t.last0 = s0.sb("last0", [1, G0 * P], I32)
            t.fresh0 = s0.sb("fresh0", [P, G0 * P])
            t.rel3 = s0.sb("rel3", [R64, 3, D], BF16)
            tables_phase(nc, a, t)
            project_phase(nc, a, t)
            attend_phase(nc, a, t)
            update_phase(nc, a, t)
        relate_phase(nc, a, t)
        mix_phase(nc, a, out, t)


_L0 = ["query_emb", "Wq", "bq", "Wk", "bk", "Wv", "bv", "rel_w", "Wo", "bo", "gamma", "beta"]
_L1 = ["W", "b", "in_proj_w", "in_proj_b", "attn_out_w", "attn_out_b", "proj_w", "proj_b"]
_INS = (["x", "src", "dst", "edge_type_6", "edge_type_64"] + [f"L0_gnn_{n}" for n in _L0] +
        [f"L1_gnn_{n}" for n in _L1])


def kernel(**inputs):
    import numpy as _np
    import concourse.bacc as _bacc
    from concourse import mybir as _mybir
    from concourse.bass_utils import run_bass_kernel_spmd as _run

    nc = _bacc.Bacc("TRN2", target_bir_lowering=False, num_devices=1)
    arrays, aps = {}, {}
    for name in _INS:
        arr = _np.ascontiguousarray(inputs[name])
        arrays[f"in_{name}_dram"] = arr
        aps[name] = nc.dram_tensor(f"in_{name}_dram", arr.shape, _mybir.dt.from_np(arr.dtype),
                                   kind="ExternalInput").ap()
    out = nc.dram_tensor("out_0_dram", (N, D), _mybir.dt.float32, kind="ExternalOutput").ap()
    resnorm_gnn(nc, aps, out)
    r = _run(nc, [arrays], core_ids=[0])
    return r.results[0]["out_0_dram"]
```
